# Optimizing a Trainium2 kernel written in Bass

```python
import numpy as np
import jax
import jax.numpy as jnp

def _softmax(x, axis=-1):
    return jax.nn.softmax(x, axis=axis)

def _gelu(x):
    return jax.nn.gelu(x, approximate=True)

def _silu(x):
    return jax.nn.silu(x)

def _sigmoid(x):
    return jax.nn.sigmoid(x)

def _layernorm(x, axis=-1, eps=1e-05):
    m = jnp.mean(x, axis=axis, keepdims=True)
    v = jnp.var(x, axis=axis, keepdims=True)
    return (x - m) / jnp.sqrt(v + eps)

def _scatter_add(tgt, idx, src, axis=0):
    return tgt.at[idx].add(src)

def _segment_sum(src, seg, n):
    return jax.ops.segment_sum(src, seg, n)
kernel_name = 'mk_decoder_preln_d2_seqx_r8_7ea5e7'

def setup_inputs(seed: int=0):
    np.random.seed(seed)
    _w = jnp.asarray

    def _rec_inputs():
        import jax
        import jax.numpy as jnp
        _rk = jax.random.key(seed)
        x = -0.0002928 + 1 * jax.random.normal(jax.random.fold_in(_rk, 1), (32, 128, 128), jnp.float32)
        _lenS = 128 - jax.random.randint(jax.random.fold_in(_rk, 7), (32,), 0, max(1, 128 // 4) + 1, jnp.int32)
        _lenS2 = 128 - jax.random.randint(jax.random.fold_in(_rk, 8), (32,), 0, max(1, 128 // 4) + 1, jnp.int32)
        _ctx_1024P = jax.random.normal(jax.random.fold_in(_rk, 11), (32, 16, 128), jnp.float32)
        _ctx_1024c = jax.random.dirichlet(jax.random.fold_in(_rk, 511), 0.3 * jnp.ones((16,), jnp.float32), (32, 128))
        _ctx_1024t = jnp.einsum('bsk,bkd->bsd', _ctx_1024c, _ctx_1024P)
        _ctx_1024t = _ctx_1024t * jax.lax.rsqrt(jnp.mean(jnp.square(_ctx_1024t)) + 1e-12) * 0.953939
        ctx_1024 = -1.39393e-06 + 0.999914 * (_ctx_1024t + 0.3 * jax.random.normal(jax.random.fold_in(_rk, 611), (32, 128, 128), jnp.float32))
        _validS = jnp.arange(128)[None, :] < _lenS[:, None]
        _validS2 = jnp.arange(128)[None, :] < _lenS2[:, None]
        _causal = jnp.tril(jnp.ones((128, 128), dtype=bool))
        mask_1x1xSxS2_fk0 = jnp.where(jnp.broadcast_to(_validS2[0:1, None, None, :], (1, 1, 128, 128)), 0.0, 1.0).astype(jnp.float32)
        return (x, ctx_1024, mask_1x1xSxS2_fk0)
    x, ctx_1024, mask_1x1xSxS2_fk0 = _rec_inputs()

    def _L0_attn_setup():
        import jax, jax.numpy as jnp
        import numpy as np
        import math
        B, S, D = (2, 512, 128)
        H = 16
        HEAD_DIM = D // H
        BLOCK = 128

        def _attention(x, w_qkv):
            b, s, d = x.shape
            hd = d // H
            nblk = s // BLOCK
            qkv = (x @ w_qkv.T).reshape(b, s, 3, H, hd)
            qkv = jnp.moveaxis(qkv, (2, 3), (0, 2))
            q, k, v = (qkv[0], qkv[1], qkv[2])
            kb = jnp.moveaxis(k.reshape(b, H, nblk, BLOCK, hd), 2, 0)
            vb = jnp.moveaxis(v.reshape(b, H, nblk, BLOCK, hd), 2, 0)
            scale = 1.0 / math.sqrt(hd)

            def step(carry, kv):
                out, lse = carry
                k_blk, v_blk = kv
                scores = jnp.einsum('bhid,bhjd->bhij', q, k_blk) * scale
                block_max = scores.max(axis=-1)
                exp_s = jnp.exp(scores - block_max[..., None])
                block_lse = block_max + jnp.log(exp_s.sum(axis=-1))
                new_lse = jnp.logaddexp(lse, block_lse)
                out = jnp.exp(lse - new_lse)[..., None] * out + jnp.exp(block_max - new_lse)[..., None] * jnp.einsum('bhij,bhjd->bhid', exp_s, v_blk)
                return ((out, new_lse), None)
            out0 = jnp.zeros_like(q)
            lse0 = jnp.full((b, H, s), -1e+30, dtype=x.dtype)
            (out, _), _ = jax.lax.scan(step, (out0, lse0), (kb, vb))
            return jnp.moveaxis(out, 1, 2).reshape(b, s, d)
        key = jax.random.key(seed)
        k1, k2, k3 = jax.random.split(key, 3)
        x = jax.random.normal(k1, (B, S, D), dtype=jnp.float32)
        w_qkv = jax.random.normal(k2, (3 * D, D), dtype=jnp.float32) * 0.02
        w_out = jax.random.normal(k3, (D, D), dtype=jnp.float32) * 0.02
        return {'x': x, 'w_qkv': w_qkv, 'w_out': w_out}
    _L0_attn_all = _L0_attn_setup()
    _L0_attn_in = {k: v for k, v in _L0_attn_all.items() if k in ('w_qkv', 'w_out')}
    del _L0_attn_all

    def _L0_xattn_setup():
        import jax, jax.numpy as jnp
        import numpy as np
        B, S, D, H = (2, 256, 128, 16)
        key = jax.random.key(seed)
        kq, kk, kv, kw = jax.random.split(key, 4)
        Q = jax.random.normal(kq, (B, S, D), dtype=jnp.float32)
        K = jax.random.normal(kk, (B, S, D), dtype=jnp.float32)
        V = jax.random.normal(kv, (B, S, D), dtype=jnp.float32)
        Wo = jax.random.normal(kw, (D, D), dtype=jnp.float32) * (1.0 / np.sqrt(D))
        return {'Q': Q, 'K': K, 'V': V, 'Wo': Wo, 'num_heads': H}
    _L0_xattn_all = _L0_xattn_setup()
    _L0_xattn_in = {k: v for k, v in _L0_xattn_all.items() if k in ('Wo',)}
    del _L0_xattn_all

    def _L0_ffn_setup():
        import jax, jax.numpy as jnp
        import numpy as np
        H = 128
        M = 64
        E = 16
        TOP_K = 4
        N_GROUP = 4
        TOPK_GROUP = 2
        SCALE = 2.5
        B, S = (2, 128)

        def _gate(x2d, gate_kernel, gate_bias):
            n = x2d.shape[0]
            logits = jnp.dot(x2d.astype(jnp.float32), gate_kernel.astype(jnp.float32))
            scores = jax.nn.sigmoid(logits)
            scores_for_choice = scores + gate_bias
            group_scores = scores_for_choice.reshape(n, N_GROUP, E // N_GROUP)
            top2 = jax.lax.top_k(group_scores, k=2)[0]
            group_sum = jnp.sum(top2, axis=-1)
            group_idx = jax.lax.top_k(group_sum, k=TOPK_GROUP)[1]
            group_mask = jnp.zeros_like(group_sum).at[jnp.arange(n)[:, None], group_idx].set(1.0)
            score_mask = jnp.repeat(group_mask[:, :, None], E // N_GROUP, axis=2).reshape(n, E)
            masked_scores = jnp.where(score_mask > 0, scores_for_choice, 0.0)
            topk_weight, topk_idx = jax.lax.top_k(masked_scores, k=TOP_K)
            topk_weight = topk_weight / (jnp.sum(topk_weight, axis=-1, keepdims=True) + 1e-20)
            topk_weight = topk_weight * SCALE
            return (topk_idx, topk_weight)
        key = jax.random.key(seed)
        ks = jax.random.split(key, 9)
        sc_h = 1.0 / np.sqrt(H)
        sc_m = 1.0 / np.sqrt(M)
        return {'hidden_states': jax.random.normal(ks[0], (B, S, H), jnp.float32), 'gate_kernel': jax.random.normal(ks[1], (H, E), jnp.float32) * sc_h, 'gate_bias': jax.random.normal(ks[2], (E,), jnp.float32) * 0.01, 'w_gate': jax.random.normal(ks[3], (E, H, M), jnp.float32) * sc_h, 'w_up': jax.random.normal(ks[4], (E, H, M), jnp.float32) * sc_h, 'w_down': jax.random.normal(ks[5], (E, M, H), jnp.float32) * sc_m, 'sw_gate': jax.random.normal(ks[6], (H, 2 * M), jnp.float32) * sc_h, 'sw_up': jax.random.normal(ks[7], (H, 2 * M), jnp.float32) * sc_h, 'sw_down': jax.random.normal(ks[8], (2 * M, H), jnp.float32) * (1.0 / np.sqrt(2 * M))}
    _L0_ffn_all = _L0_ffn_setup()
    _L0_ffn_in = {k: v for k, v in _L0_ffn_all.items() if k in ('gate_kernel', 'gate_bias', 'w_gate', 'w_up', 'w_down', 'sw_gate', 'sw_up', 'sw_down')}
    del _L0_ffn_all

    def _L1_attn_setup():
        import jax, jax.numpy as jnp
        import numpy as np
        EPS = 1e-08

        def elu_feature_map(x):
            return jax.nn.elu(x) + 1.0
        key = jax.random.key(seed)
        ks = jax.random.split(key, 5)
        B, S, D = (2, 512, 128)
        scale = 1.0 / np.sqrt(D).astype(np.float32)
        x = jax.random.normal(ks[0], (B, S, D), dtype=jnp.float32)
        Wq = jax.random.normal(ks[1], (D, D), dtype=jnp.float32) * scale
        Wk = jax.random.normal(ks[2], (D, D), dtype=jnp.float32) * scale
        Wv = jax.random.normal(ks[3], (D, D), dtype=jnp.float32) * scale
        Wo = jax.random.normal(ks[4], (D, D), dtype=jnp.float32) * scale
        return {'x': x, 'Wq': Wq, 'Wk': Wk, 'Wv': Wv, 'Wo': Wo}
    _L1_attn_all = _L1_attn_setup()
    _L1_attn_in = {k: v for k, v in _L1_attn_all.items() if k in ('Wq', 'Wk', 'Wv', 'Wo')}
    del _L1_attn_all

    def _L1_xattn_setup():
        import jax, jax.numpy as jnp
        import numpy as np
        B, S, D = (4, 256, 128)
        H = 16
        KD = 128
        VD = 128
        key = jax.random.key(seed)
        ks = jax.random.split(key, 8)
        queries = jax.random.normal(ks[0], (B, S, D), dtype=jnp.float32)
        keys_ = jax.random.normal(ks[1], (B, S, D), dtype=jnp.float32)
        values = jax.random.normal(ks[2], (B, S, D), dtype=jnp.float32)
        mask = jnp.tril(jnp.ones((S, S), dtype=jnp.float32))[None, None]
        Wq = jax.random.normal(ks[3], (D, KD), dtype=jnp.float32) / np.sqrt(D)
        Wk = jax.random.normal(ks[4], (D, KD), dtype=jnp.float32) / np.sqrt(D)
        Wv = jax.random.normal(ks[5], (D, VD), dtype=jnp.float32) / np.sqrt(D)
        Wo = jax.random.normal(ks[6], (H * VD // H * H // H * 1 if False else VD, D), dtype=jnp.float32) / np.sqrt(VD)
        bo = jnp.zeros((D,), dtype=jnp.float32)
        return {'queries': queries, 'keys': keys_, 'values': values, 'mask': mask, 'Wq': Wq, 'Wk': Wk, 'Wv': Wv, 'Wo': Wo, 'bo': bo}
    _L1_xattn_all = _L1_xattn_setup()
    _L1_xattn_in = {k: v for k, v in _L1_xattn_all.items() if k in ('Wq', 'Wk', 'Wv', 'Wo', 'bo')}
    del _L1_xattn_all

    def _L1_ffn_setup():
        import jax, jax.numpy as jnp
        import numpy as np
        W_SCALE = 0.02
        TOP_K = 2
        key = jax.random.key(seed)
        ks = jax.random.split(key, 5)
        B, S, H, I, E = (2, 128, 128, 512, 8)
        return {'x': jax.random.normal(ks[0], (B, S, H), dtype=jnp.float32), 'gate': jax.random.normal(ks[1], (H, E), dtype=jnp.float32) * W_SCALE, 'experts_w1': jax.random.normal(ks[2], (E, H, I), dtype=jnp.float32) * W_SCALE, 'experts_w2': jax.random.normal(ks[3], (E, I, H), dtype=jnp.float32) * W_SCALE, 'experts_w3': jax.random.normal(ks[4], (E, H, I), dtype=jnp.float32) * W_SCALE}
    _L1_ffn_all = _L1_ffn_setup()
    _L1_ffn_in = {k: v for k, v in _L1_ffn_all.items() if k in ('gate', 'experts_w1', 'experts_w2', 'experts_w3')}
    del _L1_ffn_all
    return {'x': x, 'ctx_1024': ctx_1024, 'mask_1x1xSxS2_fk0': mask_1x1xSxS2_fk0, 'L0_attn_w_qkv': _L0_attn_in['w_qkv'], 'L0_attn_w_out': _L0_attn_in['w_out'], 'L0_xattn_Wo': _L0_xattn_in['Wo'], 'L0_ffn_gate_kernel': _L0_ffn_in['gate_kernel'], 'L0_ffn_gate_bias': _L0_ffn_in['gate_bias'], 'L0_ffn_w_gate': _L0_ffn_in['w_gate'], 'L0_ffn_w_up': _L0_ffn_in['w_up'], 'L0_ffn_w_down': _L0_ffn_in['w_down'], 'L0_ffn_sw_gate': _L0_ffn_in['sw_gate'], 'L0_ffn_sw_up': _L0_ffn_in['sw_up'], 'L0_ffn_sw_down': _L0_ffn_in['sw_down'], 'L1_attn_Wq': _L1_attn_in['Wq'], 'L1_attn_Wk': _L1_attn_in['Wk'], 'L1_attn_Wv': _L1_attn_in['Wv'], 'L1_attn_Wo': _L1_attn_in['Wo'], 'L1_xattn_Wq': _L1_xattn_in['Wq'], 'L1_xattn_Wk': _L1_xattn_in['Wk'], 'L1_xattn_Wv': _L1_xattn_in['Wv'], 'L1_xattn_Wo': _L1_xattn_in['Wo'], 'L1_xattn_bo': _L1_xattn_in['bo'], 'L1_ffn_gate': _L1_ffn_in['gate'], 'L1_ffn_experts_w1': _L1_ffn_in['experts_w1'], 'L1_ffn_experts_w2': _L1_ffn_in['experts_w2'], 'L1_ffn_experts_w3': _L1_ffn_in['experts_w3']}

def reference(x, ctx_1024, mask_1x1xSxS2_fk0, L0_attn_w_qkv, L0_attn_w_out, L0_xattn_Wo, L0_ffn_gate_kernel, L0_ffn_gate_bias, L0_ffn_w_gate, L0_ffn_w_up, L0_ffn_w_down, L0_ffn_sw_gate, L0_ffn_sw_up, L0_ffn_sw_down, L1_attn_Wq, L1_attn_Wk, L1_attn_Wv, L1_attn_Wo, L1_xattn_Wq, L1_xattn_Wk, L1_xattn_Wv, L1_xattn_Wo, L1_xattn_bo, L1_ffn_gate, L1_ffn_experts_w1, L1_ffn_experts_w2, L1_ffn_experts_w3):
    import jax
    import jax.numpy as jnp

    def _L0_attn_ref(x, w_qkv, w_out):
        import jax, jax.numpy as jnp
        import numpy as np
        import math
        B, S, D = (2, 512, 128)
        H = 16
        HEAD_DIM = D // H
        BLOCK = 128

        def _attention(x, w_qkv):
            b, s, d = x.shape
            hd = d // H
            nblk = s // BLOCK
            qkv = (x @ w_qkv.T).reshape(b, s, 3, H, hd)
            qkv = jnp.moveaxis(qkv, (2, 3), (0, 2))
            q, k, v = (qkv[0], qkv[1], qkv[2])
            kb = jnp.moveaxis(k.reshape(b, H, nblk, BLOCK, hd), 2, 0)
            vb = jnp.moveaxis(v.reshape(b, H, nblk, BLOCK, hd), 2, 0)
            scale = 1.0 / math.sqrt(hd)

            def step(carry, kv):
                out, lse = carry
                k_blk, v_blk = kv
                scores = jnp.einsum('bhid,bhjd->bhij', q, k_blk) * scale
                block_max = scores.max(axis=-1)
                exp_s = jnp.exp(scores - block_max[..., None])
                block_lse = block_max + jnp.log(exp_s.sum(axis=-1))
                new_lse = jnp.logaddexp(lse, block_lse)
                out = jnp.exp(lse - new_lse)[..., None] * out + jnp.exp(block_max - new_lse)[..., None] * jnp.einsum('bhij,bhjd->bhid', exp_s, v_blk)
                return ((out, new_lse), None)
            out0 = jnp.zeros_like(q)
            lse0 = jnp.full((b, H, s), -1e+30, dtype=x.dtype)
            (out, _), _ = jax.lax.scan(step, (out0, lse0), (kb, vb))
            return jnp.moveaxis(out, 1, 2).reshape(b, s, d)
        attn = _attention(x, w_qkv)
        return attn @ w_out.T

    def _L0_xattn_ref(Q, K, V, Wo, num_heads):
        import jax, jax.numpy as jnp
        import numpy as np
        B, S, D, H = (2, 256, 128, 16)
        b, s, d = Q.shape
        dk = d // num_heads
        q = Q.reshape(b, s, num_heads, dk).transpose(0, 2, 1, 3)
        k = K.reshape(b, s, num_heads, dk).transpose(0, 2, 1, 3)
        v = V.reshape(b, s, num_heads, dk).transpose(0, 2, 1, 3)
        scale = 1.0 / jnp.sqrt(jnp.asarray(dk, dtype=q.dtype))
        logits = jnp.einsum('bhqd,bhkd->bhqk', q, k) * scale
        probs = jax.nn.softmax(logits, axis=-1).astype(q.dtype)
        o = jnp.einsum('bhqk,bhkd->bhqd', probs, v)
        o = o.transpose(0, 2, 1, 3).reshape(b, s, d)
        return jnp.einsum('dk,bsk->bsd', Wo, o)

    def _L0_ffn_ref(hidden_states, gate_kernel, gate_bias, w_gate, w_up, w_down, sw_gate, sw_up, sw_down):
        import jax, jax.numpy as jnp
        import numpy as np
        H = 128
        M = 64
        E = 16
        TOP_K = 4
        N_GROUP = 4
        TOPK_GROUP = 2
        SCALE = 2.5
        B, S = (2, 128)

        def _gate(x2d, gate_kernel, gate_bias):
            n = x2d.shape[0]
            logits = jnp.dot(x2d.astype(jnp.float32), gate_kernel.astype(jnp.float32))
            scores = jax.nn.sigmoid(logits)
            scores_for_choice = scores + gate_bias
            group_scores = scores_for_choice.reshape(n, N_GROUP, E // N_GROUP)
            top2 = jax.lax.top_k(group_scores, k=2)[0]
            group_sum = jnp.sum(top2, axis=-1)
            group_idx = jax.lax.top_k(group_sum, k=TOPK_GROUP)[1]
            group_mask = jnp.zeros_like(group_sum).at[jnp.arange(n)[:, None], group_idx].set(1.0)
            score_mask = jnp.repeat(group_mask[:, :, None], E // N_GROUP, axis=2).reshape(n, E)
            masked_scores = jnp.where(score_mask > 0, scores_for_choice, 0.0)
            topk_weight, topk_idx = jax.lax.top_k(masked_scores, k=TOP_K)
            topk_weight = topk_weight / (jnp.sum(topk_weight, axis=-1, keepdims=True) + 1e-20)
            topk_weight = topk_weight * SCALE
            return (topk_idx, topk_weight)
        orig_shape = hidden_states.shape
        x = hidden_states.reshape(-1, orig_shape[-1])
        topk_idx, topk_weight = _gate(x, gate_kernel, gate_bias)
        onehot = (topk_idx[:, :, None] == jnp.arange(E)[None, None, :]).astype(topk_weight.dtype)
        combine = jnp.einsum('nke,nk->ne', onehot, topk_weight)
        g = jnp.einsum('nh,ehm->enm', x, w_gate)
        u = jnp.einsum('nh,ehm->enm', x, w_up)
        inter = jax.nn.silu(g) * u
        y_e = jnp.einsum('enm,emh->enh', inter, w_down)
        y = jnp.einsum('ne,enh->nh', combine, y_e)
        shared = jnp.dot(jax.nn.silu(jnp.dot(x, sw_gate)) * jnp.dot(x, sw_up), sw_down)
        return (y + shared).reshape(orig_shape)

    def _L1_attn_ref(x, Wq, Wk, Wv, Wo):
        import jax, jax.numpy as jnp
        import numpy as np
        EPS = 1e-08

        def elu_feature_map(x):
            return jax.nn.elu(x) + 1.0
        B, S, D = x.shape
        H = 16
        Dh = D // H

        def proj(W):
            return (x @ W.T).reshape(B, S, H, Dh)
        q = elu_feature_map(proj(Wq))
        k = elu_feature_map(proj(Wk))
        v = proj(Wv)
        q_t = jnp.moveaxis(q, 1, 0)
        k_t = jnp.moveaxis(k, 1, 0)
        v_t = jnp.moveaxis(v, 1, 0)

        def step(carry, qkv):
            kv_sum, k_sum = carry
            q_i, k_i, v_i = qkv
            kv_sum = kv_sum + jnp.einsum('bhd,bhe->bhde', k_i, v_i)
            k_sum = k_sum + k_i
            num = jnp.einsum('bhd,bhde->bhe', q_i, kv_sum)
            den = jnp.sum(q_i * k_sum, axis=-1, keepdims=True)
            out_i = num / (den + EPS)
            return ((kv_sum, k_sum), out_i)
        kv0 = jnp.zeros((B, H, Dh, Dh), dtype=x.dtype)
        ks0 = jnp.zeros((B, H, Dh), dtype=x.dtype)
        _, out = jax.lax.scan(step, (kv0, ks0), (q_t, k_t, v_t))
        out = jnp.moveaxis(out, 0, 1).reshape(B, S, D)
        return out @ Wo.T

    def _L1_xattn_ref(queries, keys, values, mask, Wq, Wk, Wv, Wo, bo):
        import jax, jax.numpy as jnp
        import numpy as np
        B, S, D = (4, 256, 128)
        H = 16
        KD = 128
        VD = 128
        b, s, _ = queries.shape
        q = (queries @ Wq).reshape(b, s, H, -1).transpose(0, 2, 1, 3)
        k = (keys @ Wk).reshape(b, s, H, -1).transpose(0, 2, 1, 3)
        v = (values @ Wv).reshape(b, s, H, -1).transpose(0, 2, 1, 3)
        dk = k.shape[-1]
        logits = jnp.einsum('bhqd,bhkd->bhqk', q, k) / jnp.sqrt(jnp.float32(dk))
        logits = logits + (1.0 - mask) * -1000000000.0
        attn = jax.nn.softmax(logits, axis=-1)
        o = jnp.einsum('bhqk,bhkd->bhqd', attn, v)
        o = o.transpose(0, 2, 1, 3).reshape(b, s, H * (VD // H))
        return o @ Wo + bo

    def _L1_ffn_ref(x, gate, experts_w1, experts_w2, experts_w3):
        import jax, jax.numpy as jnp
        import numpy as np
        W_SCALE = 0.02
        TOP_K = 2
        E = experts_w1.shape[0]
        router_logits = jnp.einsum('bsh,he->bse', x, gate)
        routing_weights, selected = jax.lax.top_k(router_logits, TOP_K)
        routing_weights = jax.nn.softmax(routing_weights, axis=-1)
        onehot = jax.nn.one_hot(selected, E, dtype=x.dtype)
        tok_w = jnp.einsum('bsk,bske->bse', routing_weights, onehot)
        g = jnp.einsum('bsh,ehi->ebsi', x, experts_w1)
        u = jnp.einsum('bsh,ehi->ebsi', x, experts_w3)
        hid = jax.nn.silu(g) * u
        eo = jnp.einsum('ebsi,eih->ebsh', hid, experts_w2)
        out = jnp.einsum('ebsh,bse->bsh', eo, tok_w)
        return out
    x = x + _L0_attn_ref(_layernorm(x, axis=-1), L0_attn_w_qkv, L0_attn_w_out)
    x = x + _L0_xattn_ref(_layernorm(x, axis=-1), ctx_1024, ctx_1024, L0_xattn_Wo, 16)
    x = x + _L0_ffn_ref(_layernorm(x, axis=-1), L0_ffn_gate_kernel, L0_ffn_gate_bias, L0_ffn_w_gate, L0_ffn_w_up, L0_ffn_w_down, L0_ffn_sw_gate, L0_ffn_sw_up, L0_ffn_sw_down)
    x = x + _L1_attn_ref(_layernorm(x, axis=-1), L1_attn_Wq, L1_attn_Wk, L1_attn_Wv, L1_attn_Wo)
    x = x + _L1_xattn_ref(_layernorm(x, axis=-1), ctx_1024, ctx_1024, mask_1x1xSxS2_fk0, L1_xattn_Wq, L1_xattn_Wk, L1_xattn_Wv, L1_xattn_Wo, L1_xattn_bo)
    x = x + _L1_ffn_ref(_layernorm(x, axis=-1), L1_ffn_gate, L1_ffn_experts_w1, L1_ffn_experts_w2, L1_ffn_experts_w3)
    return x

_drawn_inputs = setup_inputs


def setup_inputs(seed=0):
    import zlib

    import numpy as np

    out = dict(_drawn_inputs(seed))
    spreads = {'L1_xattn_bo': (0.0, 0.1)}
    factors = {'L1_attn_Wq': 3.469,
     'L1_ffn_gate': 8.0,
     'L1_ffn_experts_w1': 8.0,
     'L1_ffn_experts_w2': 8.0,
     'L1_ffn_experts_w3': 8.0}
    for name, (base, spread) in spreads.items():
        noise = np.random.default_rng([zlib.crc32(name.encode()), seed]).standard_normal(out[name].shape)
        drawn = base * np.exp(spread * noise) if base else spread * noise
        out[name] = jnp.asarray(drawn.astype(out[name].dtype))
    for name, factor in factors.items():
        out[name] = (out[name] * factor).astype(out[name].dtype)
    return out
```

```python
from contextlib import ExitStack

import numpy as np

import concourse.bass as bass
from concourse import mybir

F32 = mybir.dt.float32
BF16 = mybir.dt.bfloat16
ALU = mybir.AluOpType
ACT = mybir.ActivationFunctionType
AX = mybir.AxisListType

B, S, D = 32, 128, 128
H, HD = 16, 8
GB = 4
NG = B // GB
GT = GB * S
UH = 8
UN = GB * H // UH
UW = UH * S
SCALE = float(1.0 / np.sqrt(np.float32(HD)))
MASKED = -1e9
LN_EPS = 1e-5
DEN_EPS = 1e-8
E1, M1 = 16, 64
E2, M2 = 8, 512
C1 = E1 * M1 // 128
C2 = E2 * M2 // 128

W1_LOADS = 17

SELF, CROSS, MOE, LINEAR, MASKX, TOP2 = range(6)
CHUNKS = {MOE: C1 + 1, TOP2: C2}
ATTN = (SELF, CROSS, LINEAR, MASKX)

STARTS = {"xupd": 1}

PER_GROUP = {
    "xupd":   (1, 1, 1, 1, 1, 1),
    "stat":   (4, 4, 4, 4, 4, 4),
    "aggr":   (4, 4, 4, 4, 4, 4),
    "veps":   (1, 1, 1, 1, 1, 1),
    "rstd":   (1, 1, 1, 1, 1, 1),
    "xn":     (4, 4, 4, 4, 4, 4),
    "xT":     (1, 1, 1, 1, 1, 1),
    "xTe":    (1, 1, 1, 1, 1, 1),
    "ctx":    (0, 16, 0, 0, 16, 0),
    "cT":     (0, 1, 0, 0, 1, 0),
    "cTe":    (0, 1, 0, 0, 1, 0),
    "q":      (1, 0, 0, 1, 1, 0),
    "qe":     (1, 0, 0, 1, 1, 0),
    "k":      (1, 0, 0, 1, 1, 0),
    "ke":     (1, 0, 0, 1, 1, 0),
    "phi":    (0, 0, 0, 4, 0, 0),
    "v":      (1, 0, 0, 1, 1, 0),
    "ve":     (1, 1, 0, 1, 1, 0),
    "spread": (256, 256, 0, 256, 256, 0),
    "s":      (UN, UN, 0, UN, UN, 0),
    "sm":     (0, 0, 0, 0, UN, 0),
    "negm":   (UN, UN, 0, 0, UN, 0),
    "t":      (UN, UN, 0, UN, UN, 0),
    "e":      (UN, UN, 0, 0, UN, 0),
    "pt":     (UN, UN, 0, 0, UN, 0),
    "pte":    (UN, UN, 0, 0, UN, 0),
    "pv":     (UN, UN, 0, UN, UN, 0),
    "ot":     (GB, GB, 0, GB, GB, 0),
    "oq":     (GB, GB, 0, GB, GB, 0),
    "den":    (0, 0, 0, GB, 0, 0),
    "rden":   (GB, GB, 0, GB, GB, 0),
    "on":     (GB, GB, 0, GB, GB, 0),
    "oT":     (1, 1, 0, 1, 1, 0),
    "oTe":    (1, 1, 0, 1, 1, 0),
    "y":      (1, 1, 0, 1, 1, 0),
    "bias":   (0, 0, 0, 0, 1, 0),
    "lg":     (0, 0, 1, 0, 0, 1),
    "lge":    (0, 0, 0, 0, 0, 1),
    "route":  (0, 0, 25, 0, 0, 13),
    "rexp":   (0, 0, 1, 0, 0, 1),
    "comb":   (0, 0, 1, 0, 0, 1),
    "combT":  (0, 0, 1, 0, 0, 1),
    "combTe": (0, 0, 1, 0, 0, 1),
    "gate":   (0, 0, C1 + 1, 0, 0, C2),
    "up":     (0, 0, C1 + 1, 0, 0, C2),
    "cw":     (0, 0, C1, 0, 0, C2),
    "silu":   (0, 0, C1 + 1, 0, 0, C2),
    "gu":     (0, 0, C1 + 1, 0, 0, C2),
    "h":      (0, 0, C1, 0, 0, C2),
    "wsum":   (0, 0, 5, 0, 0, 5),
    "down":   (0, 0, C1 + 1, 0, 0, C2),
}


def decoder(nc, x, ctx, mask, w_qkv, w_out, x0_wo, gate1, bias1, w_gate1, w_up1, w_down1, s_gate1,
            s_up1, s_down1, l_wq, l_wk, l_wv, l_wo, m_wq, m_wk, m_wv, m_wo, m_bo, gate2, e_w1, e_w2,
            e_w3, ident, causal, tri, sel1, sel2, out):
    with ExitStack() as stack:
        def sb(name, shape, dt=F32):
            return stack.enter_context(nc.sbuf_tensor(name, shape, dt))

        def ps(name, shape, dt=F32):
            return stack.enter_context(nc.psum_tensor(name, shape, dt))

        def semaphore(name):
            return stack.enter_context(nc.semaphore("s_" + name))

        s_xupd = semaphore("xupd")
        s_stat = semaphore("stat")
        s_aggr = semaphore("aggr")
        s_veps = semaphore("veps")
        s_rstd = semaphore("rstd")
        s_xn = semaphore("xn")
        s_xT = semaphore("xT")
        s_xTe = semaphore("xTe")
        s_ctx = semaphore("ctx")
        s_cT = semaphore("cT")
        s_cTe = semaphore("cTe")
        s_q = semaphore("q")
        s_qe = semaphore("qe")
        s_k = semaphore("k")
        s_ke = semaphore("ke")
        s_phi = semaphore("phi")
        s_v = semaphore("v")
        s_ve = semaphore("ve")
        s_spread = semaphore("spread")
        s_s = semaphore("s")
        s_sm = semaphore("sm")
        s_negm = semaphore("negm")
        s_t = semaphore("t")
        s_e = semaphore("e")
        s_pt = semaphore("pt")
        s_pte = semaphore("pte")
        s_pv = semaphore("pv")
        s_ot = semaphore("ot")
        s_oq = semaphore("oq")
        s_den = semaphore("den")
        s_rden = semaphore("rden")
        s_on = semaphore("on")
        s_oT = semaphore("oT")
        s_oTe = semaphore("oTe")
        s_y = semaphore("y")
        s_bias = semaphore("bias")
        s_lg = semaphore("lg")
        s_lge = semaphore("lge")
        s_route = semaphore("route")
        s_rexp = semaphore("rexp")
        s_comb = semaphore("comb")
        s_combT = semaphore("combT")
        s_combTe = semaphore("combTe")
        s_gate = semaphore("gate")
        s_up = semaphore("up")
        s_cw = semaphore("cw")
        s_silu = semaphore("silu")
        s_gu = semaphore("gu")
        s_h = semaphore("h")
        s_down = semaphore("down")
        s_wsum = semaphore("wsum")

        def at(name, st, g, k):
            rate = PER_GROUP[name]
            value = STARTS.get(name, 0) + NG * sum(rate[:st]) + rate[st] * g + k
            return max(value, 0) if isinstance(value, int) else value

        s_passed = {n: semaphore("passed_" + n) for n in ("sp", "pool", "dve")}

        def settle(eng, name):
            eng.sem_inc(s_passed[name], 1)

        s_x0 = semaphore("x0")
        s_x1 = semaphore("x1")
        s_w0 = semaphore("w0")
        s_tab = semaphore("tab")
        s_w1 = semaphore("w1")
        s_w2 = semaphore("w2")
        s_out = semaphore("out")
        s_wT = semaphore("wT")
        s_wTe = semaphore("wTe")
        s_zero = semaphore("zero")
        s_ones = semaphore("ones")
        s_mneg = semaphore("mneg")

        score = ps("score", [128, 2, UW])
        turned = ps("turned", [128, UW])
        front = ps("front", [128, GT])
        back = ps("back", [128, GT])

        X = sb("X", [128, B, D])
        spread = sb("spread", [128, 2, H, GT])
        crow = sb("crow", [128, 2, GB, D])
        cT = sb("cT", [128, 2, GT])
        dense = sb("dense", [128, 2, GT])
        src = sb("src", [128, 2, GT])
        phi_e = sb("phi_e", [128, GT])
        phi_r = sb("phi_r", [128, GT])
        V = sb("V", [128, 2, GB, H, HD + 1])
        xn = sb("xn", [128, 2, GB, D])
        xT = sb("xT", [128, 2, GT])
        work = sb("work", [128, 9 * UW])
        T = work[:, 0:4 * UW].rearrange("p (r c) -> p r c", r=4)
        PT = work[:, 4 * UW:6 * UW].rearrange("p (r c) -> p r c", r=2)
        OT = work[:, 6 * UW:7 * UW].rearrange("p (r c) -> p r c", r=2)
        O = work[:, 7 * UW:8 * UW].rearrange("p (r b c) -> p r b c", r=2, b=GB)
        OdT = work[:, 8 * UW:9 * UW].rearrange("p (r c) -> p r c", r=2)
        sg = work[:, 0:GT * 2].rearrange("p (r c) -> p r c", r=2)
        gu = work[:, GT * 2:GT * 4].rearrange("p (r c) -> p r c", r=2)
        hid = work[:, GT * 4:GT * 6].rearrange("p (r c) -> p r c", r=2)
        wide = work[:, GT * 6:GT * 10]
        wraw = sb("wraw", [128, 9, D])
        wT = sb("wT", [128, 9, D])
        wm = sb("wm", [128, 4, D])
        bo = sb("bo", [128, D])
        mneg = sb("mneg", [128, D])
        cm = sb("cm", [128, D])
        idf = sb("idf", [128, 128])
        idb = sb("idb", [128, 128], BF16)
        tr = sb("tr", [128, 16, 16])
        stats = sb("stats", [128, GB, 6])
        mv = sb("mv", [128, 2, GB, 2])
        veps = sb("veps", [128, GB])
        half = sb("half", [128, GB])
        rstd = sb("rstd", [128, 2, GB])
        negm = sb("negm", [128, 2, UH])
        den = sb("den", [128, H])
        rden = sb("rden", [128, H])
        sel = {MOE: sb("sel1s", [128, C1, 128], BF16), TOP2: sb("sel2s", [128, E2, 128], BF16)}
        gw = {MOE: sb("gw1", [128, E1]), TOP2: sb("gw2", [128, E2])}
        bias_r = sb("bias_r", [128, E1])
        wg1 = sb("wg1", [128, E1 * M1 + 128])
        wu1 = sb("wu1", [128, E1 * M1 + 128])
        wd1 = sb("wd1", [128, C1 + 1, D])
        heavy = spread[:, :, :, :].rearrange("p r h c -> p (r h c)")
        WE = E2 * M2
        wg = {MOE: wg1[:, :], TOP2: heavy[:, 0:WE]}
        wu = {MOE: wu1[:, :], TOP2: heavy[:, WE:2 * WE]}
        wd = {MOE: wd1[:, :, :], TOP2: heavy[:, 2 * WE:3 * WE].rearrange("p (c n) -> p c n", n=D)}
        NR = 64
        lr = sb("lr", [128, 14, NR])
        combp = sb("combp", [128, GB, 128], BF16)
        combT = sb("combT", [128, 2, GT], BF16)
        WQ, WK, WV, WOUT, XWO, LQ, LK, LV, LO = range(9)
        MQ, MK, MV, MO = range(4)
        NE = {MOE: E1, TOP2: E2}

        block = stack.enter_context(nc.Block())

        def groups(eng, body):
            body(0, 0, True, False)
            with eng.Fori(0, (NG - 2) // 2) as j:
                body(2 * j + 1, 1, False, False)
                body(2 * j + 2, 0, False, False)
            body(NG - 1, (NG - 1) % 2, False, True)

        def before(st, g, c):
            if c >= 2:
                return g, c - 2
            n = CHUNKS[st]
            return g - 1, n - 1 if (n - 1) % 2 == c else n - 2

        @block.sync
        def _(sp):
            xv = x.rearrange("b s d -> s b d")
            sp.dma_start(X[:, 0:GB, :], xv[:, 0:GB, :]).then_inc(s_x0, 16)
            sp.dma_start(idf[:, :], ident).then_inc(s_w0, 16)
            sp.dma_start(wraw[:, 0:3, :], w_qkv.rearrange("(t o) i -> o t i", t=3)).then_inc(s_w0, 16)
            for n, w in ((WOUT, w_out), (XWO, x0_wo), (LQ, l_wq), (LK, l_wk), (LV, l_wv), (LO, l_wo)):
                sp.dma_start(wraw[:, n, :], w).then_inc(s_w0, 16)
            sp.dma_start(X[:, GB:B, :], xv[:, GB:B, :]).then_inc(s_x1, 16)
            for n, w in ((MQ, m_wq), (MK, m_wk), (MV, m_wv), (MO, m_wo)):
                sp.dma_start(wm[:, n, :], w).then_inc(s_w1, 16)
            sp.dma_start(bo[:, :], m_bo.rearrange("(a d) -> a d", a=1).broadcast_to([128, D])).then_inc(s_w1, 16)
            sp.dma_start(mneg[:, :], mask[0, 0]).then_inc(s_w1, 16)
            sp.dma_start(cm[:, :], causal).then_inc(s_w1, 16)
            sp.dma_start(tr[:, :, :], tri.rearrange("(a j) i -> a j i", a=1).broadcast_to([128, 16, 16])).then_inc(s_w1, 16)
            sp.dma_start(gw[MOE][:, :], gate1).then_inc(s_w1, 16)
            sp.dma_start(gw[TOP2][:, :], gate2).then_inc(s_w1, 16)
            sp.dma_start(bias_r[:, :], bias1.rearrange("(a d) -> a d", a=1).broadcast_to([128, E1])).then_inc(s_w1, 16)
            sp.dma_start(wg1[:, 0:E1 * M1].rearrange("p (e m) -> p e m", e=E1), w_gate1.rearrange("e h m -> h e m")).then_inc(s_w1, 16)
            sp.dma_start(wu1[:, 0:E1 * M1].rearrange("p (e m) -> p e m", e=E1), w_up1.rearrange("e h m -> h e m")).then_inc(s_w1, 16)
            sp.dma_start(wg1[:, E1 * M1:], s_gate1).then_inc(s_w1, 16)
            sp.dma_start(wu1[:, E1 * M1:], s_up1).then_inc(s_w1, 16)
            sp.dma_start(wd1[:, 0:C1, :], w_down1.rearrange("(c two) m h -> (two m) c h", two=2)).then_inc(s_w1, 16)
            sp.dma_start(wd1[:, C1, :], s_down1).then_inc(s_w1, 16)

            def context(st, g, p):
                sp.wait_ge(s_cT, at("cT", st, g - 1, 0))
                settle(sp, "sp")
                if st == CROSS:
                    sp.wait_ge(s_ve, at("ve", st, g - 1, 0))
                    settle(sp, "sp")
                sp.wait_ge(s_ctx, at("ctx", st, g, 0))
                settle(sp, "sp")
                b0 = g * GB
                sp.dma_start(crow[:, p, :, :], ctx.rearrange("b s d -> s b d")[:, bass.ds(b0, GB), :]).then_inc(s_ctx, 16)

            def spreading(st, g, p):
                if st == CROSS:
                    sp.wait_ge(s_cTe, at("cTe", st, g, 1))
                    settle(sp, "sp")
                    rows = cT
                else:
                    if st == LINEAR:
                        sp.wait_ge(s_qe, at("qe", st, g, 1))
                    else:
                        sp.wait_ge(s_ke, at("ke", st, g, 1))
                    settle(sp, "sp")
                    rows = src
                sp.wait_ge(s_spread, at("spread", st, g, 0))
                settle(sp, "sp")
                for h in range(H):
                    r = slice(HD * h, HD * h + HD)
                    sp.dma_start(spread[r, p, h, :], rows[r, p, :]).then_inc(s_spread, 16)

            sp.wait_ge(s_zero, 3)
            for st in ATTN:
                if st in (CROSS, MASKX):
                    context(st, 0, 0)
                spreading(st, 0, 0)

                def body(g, p, first, last):
                    if not last:
                        if st in (CROSS, MASKX):
                            context(st, g + 1, 1 - p)
                        spreading(st, g + 1, 1 - p)
                groups(sp, body)
            sp.wait_ge(s_s, at("s", MASKX, NG, 0))
            settle(sp, "sp")
            sp.dma_start(wg[TOP2].rearrange("p (e m) -> p e m", e=E2), e_w1.rearrange("e h m -> h e m")).then_inc(s_w2, 16)
            sp.dma_start(wu[TOP2].rearrange("p (e m) -> p e m", e=E2), e_w3.rearrange("e h m -> h e m")).then_inc(s_w2, 16)
            sp.dma_start(wd[TOP2], e_w2.rearrange("e (c p) h -> p (e c) h", p=128)).then_inc(s_w2, 16)

            def store(g, p, first, last):
                sp.wait_ge(s_xupd, at("xupd", TOP2, g, 1))
                settle(sp, "sp")
                sp.dma_start(out.rearrange("b s d -> s b d")[:, bass.ds(g * GB, GB), :], X[:, bass.ds(g * GB, GB), :]).then_inc(s_out, 16)
            groups(sp, store)
            sp.wait_ge(s_out, 16 * NG)

        @block.gpsimd
        def _(pool):
            pool.dma_start(idb[:, :], ident).then_inc(s_tab, 16)
            pool.dma_start(sel[MOE][:, :, :], sel1).then_inc(s_tab, 16)
            pool.dma_start(sel[TOP2][:, :, :], sel2).then_inc(s_tab, 16)
            pool.memset(spread[:, 1, :, :], 0.0).then_inc(s_zero, 1)
            pool.memset(half[:, :], -0.5).then_inc(s_ones, 1)
            pool.memset(V[:, :, :, :, HD:HD + 1], 1.0).then_inc(s_ones, 1)
            pool.memset(combp[:, :, :], 0.0).then_inc(s_ones, 1)
            pool.wait_ge(s_ones, 3)

            def rsqrt(st, g, p):
                pool.wait_ge(s_veps, at("veps", st, g, 1))
                pool.tensor_tensor(rstd[:, p, :], veps[:, :], half[:, :], ALU.pow).then_inc(s_rstd, 1)

            def values(st, g, p):
                pool.wait_ge(s_ctx, at("ctx", st, g, 16))
                pool.wait_ge(s_pv, at("pv", st, g - 1, 0))
                settle(pool, "pool")
                pool.tensor_copy(V[:, p, :, :, 0:HD], crow[:, p, :, :].rearrange("p b (h d) -> p b h d", d=HD)).then_inc(s_ve, 1)

            def shift(st, g, t):
                pool.wait_ge(s_negm, at("negm", st, g, t + 1))
                tv = T[:, t % 4, :].rearrange("p (h k) -> p h k", h=UH)
                pool.tensor_tensor(tv, tv, negm[:, t % 2, :].unsqueeze(2).broadcast_to([128, UH, S]), ALU.add).then_inc(s_t, 1)

            for st in range(6):
                rsqrt(st, 0, 0)
                if st == CROSS:
                    values(st, 0, 0)

                def body(g, p, first, last):
                    if not last:
                        rsqrt(st, g + 1, 1 - p)
                        if st == CROSS:
                            values(st, g + 1, 1 - p)
                    if st == MASKX:
                        for t in range(UN):
                            shift(st, g, t)
                groups(pool, body)

        @block.scalar
        def _(act):
            for n in range(3):
                act.wait_ge(s_wT, n + 1)
                act.activation(wT[:, 3 * n:3 * n + 3, :], front[:, 0:3 * D].rearrange("p (a b) -> p a b", a=3), ACT.Copy).then_inc(s_wTe, 1)

            def features():
                act.activation(phi_e[:, :], front[:, :], ACT.Exp).then_inc(s_phi, 1)
                act.activation(phi_r[:, :], front[:, :], ACT.Relu).then_inc(s_phi, 1)

            def front_part(st, g, p, k):
                if k == 0 and st in (CROSS, MASKX):
                    if st == CROSS:
                        act.wait_ge(s_spread, at("spread", st, g - 1, 0))
                    act.wait_ge(s_cT, at("cT", st, g, 1))
                    act.activation(cT[:, p, :], front[:, :], ACT.Copy).then_inc(s_cTe, 1)
                if k == 1:
                    act.wait_ge(s_xT, at("xT", st, g, 1))
                    act.activation((dense if st == CROSS else xT)[:, p, :], front[:, :], ACT.Copy).then_inc(s_xTe, 1)
                if k == 2 and st in (SELF, MASKX):
                    act.wait_ge(s_q, at("q", st, g, 1))
                    act.activation(dense[:, p, :], front[:, :], ACT.Copy).then_inc(s_qe, 1)
                if k == 2 and st == LINEAR:
                    act.wait_ge(s_q, at("q", st, g, 1))
                    act.wait_ge(s_ke, at("ke", st, g, 0))
                    features()
                if k == 3 and st in (SELF, MASKX):
                    act.wait_ge(s_spread, at("spread", st, g - 1, 0))
                    act.wait_ge(s_k, at("k", st, g, 1))
                    act.activation(src[:, p, :], front[:, :], ACT.Copy).then_inc(s_ke, 1)
                if k == 3 and st == LINEAR:
                    act.wait_ge(s_k, at("k", st, g, 1))
                    act.wait_ge(s_qe, at("qe", st, g, 1))
                    features()
                if k == 5 and st != CROSS:
                    act.wait_ge(s_v, at("v", st, g, 1))
                    act.activation(V[:, p, :, :, 0:HD], front[:, :].rearrange("p (b h d) -> p b h d", b=GB, d=HD), ACT.Copy).then_inc(s_ve, 1)

            def exponential(st, g, t):
                act.wait_ge(s_t, at("t", st, g, t + 1))
                act.activation(T[:, t % 4, :], T[:, t % 4, :], ACT.Exp, scale=1.0 if st == MASKX else SCALE).then_inc(s_e, 1)

            def copy_turned(st, g, t):
                act.wait_ge(s_pt, at("pt", st, g, t + 1))
                act.activation(PT[:, t % 2, :], turned[:, :], ACT.Copy).then_inc(s_pte, 1)

            def copy_out(st, g, b):
                act.wait_ge(s_pv, at("pv", st, g, 2 * b + 2))
                act.activation(OT[:, b % 2, :], back[:, :], ACT.Copy).then_inc(s_ot, 1)

            def slot(st, g, p, t, first, last, flush):
                if not last and not flush:
                    front_part(st, g + 1, 1 - p, t)
                if t == 4 and not first:
                    act.wait_ge(s_oT, at("oT", st, g - 1, 1))
                    act.activation(OdT[:, 1 - p, :], front[:, :], ACT.Copy).then_inc(s_oTe, 1)
                if st != LINEAR:
                    if t >= 2:
                        if not flush:
                            copy_turned(st, g, t - 2)
                    elif not first:
                        copy_turned(st, g - 1, t + UN - 2)
                if t % 2 == 0:
                    if t >= 4 and not flush:
                        copy_out(st, g, (t - 4) // 2)
                    elif t < 4 and not first:
                        copy_out(st, g - 1, (t + UN - 4) // 2)
                if st != LINEAR and not flush:
                    exponential(st, g, t)

            def attention(st):
                for k in range(6):
                    front_part(st, 0, 0, k)

                def body(g, p, first, last):
                    for t in range(UN):
                        slot(st, g, p, t, first, last, False)
                groups(act, body)
                for t in range(5):
                    slot(st, NG, NG % 2, t, False, True, True)

            def experts(st):
                def routing(g, p, k):
                    if k == 0:
                        act.wait_ge(s_xT, at("xT", st, g, 1))
                        act.activation(xT[:, p, :], front[:, :], ACT.Copy).then_inc(s_xTe, 1)
                    if k == 1:
                        n = GB * NE[st]
                        if st == MOE:
                            act.wait_ge(s_lg, at("lg", st, g, 1))
                            act.activation(lr[:, 0, 0:n], front[:, 0:n], ACT.Exp, scale=-1.0).then_inc(s_rexp, 1)
                        else:
                            act.wait_ge(s_route, at("route", st, g, 2))
                            act.activation(lr[:, 3, 0:n], lr[:, 2, 0:n], ACT.Exp).then_inc(s_rexp, 1)
                    if k == 2:
                        act.wait_ge(s_combT, at("combT", st, g, 1))
                        act.activation(combT[:, p, :], front[:, :].bitcast(BF16)[:, 0:GT], ACT.Copy).then_inc(s_combTe, 1)

                for k in range(3):
                    routing(0, 0, k)
                ROUTE_AT = {1: 0, 3 if st == MOE else 5: 1, CHUNKS[st] - 1: 2}

                def body(g, p, first, last):
                    for c in range(CHUNKS[st]):
                        if c in ROUTE_AT and not last:
                            routing(g + 1, 1 - p, ROUTE_AT[c])
                        act.wait_ge(s_gate, at("gate", st, g, c + 1))
                        pg, pc = before(st, g, c)
                        act.wait_ge(s_gu, at("gu", st, pg, pc + 1))
                        act.activation(sg[:, c % 2, :], score[:, 0, (c % 2) * GT:(c % 2 + 1) * GT], ACT.Silu).then_inc(s_silu, 1)
                groups(act, body)

            attention(SELF)
            attention(CROSS)
            experts(MOE)
            attention(LINEAR)
            attention(MASKX)
            experts(TOP2)

        @block.tensor
        def _(pe):
            pe.wait_ge(s_w0, 16 * 8)
            for n in range(3):
                if n:
                    pe.wait_ge(s_wTe, n)
                for k in range(3):
                    m = pe.transpose(front[:, k * D:(k + 1) * D], wraw[:, 3 * n + k, :], idf[:, :])
                m.then_inc(s_wT, 1)
            pe.wait_ge(s_wTe, 3)
            pe.wait_ge(s_zero, 3)
            pe.wait_ge(s_ones, 3)

            def transposed_x(st, g, p):
                pe.wait_ge(s_xn, at("xn", st, g, GB))
                for b in range(GB):
                    m = pe.transpose(front[:, b * S:(b + 1) * S], xn[:, p, b, :], idf[:, :])
                m.then_inc(s_xT, 1)

            def front_free(st, g):
                if st != CROSS:
                    pe.wait_ge(s_ve, at("ve", st, g, 0))
                else:
                    pe.wait_ge(s_xTe, at("xTe", st, g, 0))
                pe.wait_ge(s_xupd, at("xupd", st, g - 2, 0))

            def front_part(st, g, p, k, tail):
                own = st in (SELF, LINEAR)
                if k == 0:
                    front_free(st, g)
                    if st in (CROSS, MASKX):
                        pe.wait_ge(s_ctx, at("ctx", st, g, 16))
                        for b in range(GB):
                            m = pe.transpose(front[:, b * S:(b + 1) * S], crow[:, p, b, :], idf[:, :])
                        m.then_inc(s_cT, 1)
                if k == 1:
                    if st in (CROSS, MASKX):
                        pe.wait_ge(s_cTe, at("cTe", st, g, 1))
                    transposed_x(st, g, p)
                if k == 2 and st != CROSS:
                    pe.wait_ge(s_xTe, at("xTe", st, g, 1))
                    w = {SELF: wT[:, WQ, :], LINEAR: wT[:, LQ, :], MASKX: wm[:, MQ, :]}[st]
                    pe.matmul(front[:, :], w, xT[:, p, :], start=True, stop=True).then_inc(s_q, 1)
                if k == 3 and st != CROSS:
                    pe.wait_ge(s_qe, at("qe", st, g, 1))
                    w = {SELF: wT[:, WK, :], LINEAR: wT[:, LK, :], MASKX: wm[:, MK, :]}[st]
                    pe.matmul(front[:, :], w, (xT if own else cT)[:, p, :], start=True, stop=True).then_inc(s_k, 1)
                if k == 5 and st != CROSS:
                    pe.wait_ge(s_ke, at("ke", st, g, 1))
                    if tail:
                        pe.wait_ge(s_oTe, at("oTe", st, g - 2, 1))
                    w = {SELF: wT[:, WV, :], LINEAR: wT[:, LV, :], MASKX: wm[:, MV, :]}[st]
                    for b in range(GB):
                        m = pe.matmul(front[:, b * D:(b + 1) * D], (xT if own else cT)[:, p, b * S:(b + 1) * S], w, start=True, stop=True)
                    m.then_inc(s_v, 1)

            def scores(st, g, p, t):
                if t == 0:
                    pe.wait_ge(s_spread, at("spread", st, g, 256))
                    if st == CROSS:
                        pe.wait_ge(s_xTe, at("xTe", st, g, 1))
                    elif st == LINEAR:
                        pe.wait_ge(s_ke, at("ke", st, g, 1))
                    else:
                        pe.wait_ge(s_qe, at("qe", st, g, 1))
                if st == MASKX:
                    pe.wait_ge(s_sm, at("sm", st, g, t - 1))
                else:
                    pe.wait_ge(s_t, at("t", st, g, t - 1))
                b, u = t // 2, t % 2
                cols = slice(b * S, (b + 1) * S)
                for q in range(2):
                    h = UH * u + 4 * q
                    m = pe.matmul(score[:, t % 2, q * 512:(q + 1) * 512], dense[:, p, cols], spread[:, p, h:h + 4, cols], start=True, stop=True)
                m.then_inc(s_s, 1)

            def turn(st, g, t):
                pe.wait_ge(s_e, at("e", st, g, t + 1))
                pe.wait_ge(s_pte, at("pte", st, g, t))
                for h in range(UH):
                    m = pe.transpose(turned[:, h * S:(h + 1) * S], T[:, t % 4, h * S:(h + 1) * S], idf[:, :])
                m.then_inc(s_pt, 1)

            def weigh(st, g, p, t):
                b, u = t // 2, t % 2
                if st == LINEAR:
                    pe.wait_ge(s_t, at("t", st, g, t + 1))
                else:
                    pe.wait_ge(s_pte, at("pte", st, g, t + 1))
                if t == 0:
                    pe.wait_ge(s_ve, at("ve", st, g, 1))
                if u == 0:
                    pe.wait_ge(s_on, at("on", st, g, b))
                for i in range(UH):
                    h = UH * u + i
                    j, s = h % 4, h // 4
                    mov = T[:, t % 4, i * S:(i + 1) * S] if st == LINEAR else PT[:, t % 2, i * S:(i + 1) * S]
                    m = pe.matmul(back[32 * j:32 * j + HD + 1, s * S:(s + 1) * S], V[:, p, b, h, :], mov, start=True, stop=True)
                m.then_inc(s_pv, 1)

            def token_rows(st, g, b):
                pe.wait_ge(s_ot, at("ot", st, g, b + 1))
                for s in range(4):
                    m = pe.transpose(back[:, s * 128:(s + 1) * 128], OT[:, b % 2, s * S:(s + 1) * S], idf[:, :])
                m.then_inc(s_oq, 1)

            def out_rows(st, g, p, others):
                pe.wait_ge(s_on, at("on", st, g, GB))
                if others:
                    if st == CROSS:
                        pe.wait_ge(s_xTe, at("xTe", st, g + 2, 1))
                    else:
                        pe.wait_ge(s_ke, at("ke", st, g + 2, 1))
                pe.wait_ge(s_xupd, at("xupd", st, g, 0))
                for b in range(GB):
                    m = pe.transpose(front[:, b * S:(b + 1) * S], O[:, p, b, :], idf[:, :])
                m.then_inc(s_oT, 1)

            def project(st, g, p, others):
                pe.wait_ge(s_oTe, at("oTe", st, g, 1))
                if others and st != CROSS:
                    pe.wait_ge(s_ve, at("ve", st, g + 2, 1))
                w = {SELF: wT[:, WOUT, :], CROSS: wT[:, XWO, :], LINEAR: wT[:, LO, :], MASKX: wm[:, MO, :]}[st]
                for b in range(GB):
                    m = pe.matmul(front[:, b * D:(b + 1) * D], OdT[:, p, b * S:(b + 1) * S], w, start=True, stop=True)
                m.then_inc(s_y, 1)

            def slot(st, g, p, t, first, last, flush):
                if not flush:
                    scores(st, g, p, t)
                    if not last:
                        front_part(st, g + 1, 1 - p, t, not first)
                if t == 4 and not first:
                    out_rows(st, g - 1, 1 - p, not last)
                if t == 6 and not first:
                    project(st, g - 1, 1 - p, not last)
                if t % 2 == 1:
                    if t >= 5 and not flush:
                        token_rows(st, g, (t - 5) // 2)
                    elif t < 5 and not first:
                        token_rows(st, g - 1, (t + UN - 5) // 2)
                if st != LINEAR:
                    if t >= 2:
                        if not flush:
                            turn(st, g, t - 2)
                    elif not first:
                        turn(st, g - 1, t + UN - 2)
                if t >= 3:
                    if not flush:
                        weigh(st, g, p, t - 3)
                elif not first:
                    weigh(st, g - 1, 1 - p, t + UN - 3)

            def attention(st):
                if st > 0:
                    pe.wait_ge(s_xupd, at("xupd", st, 0, 0))
                if st == MASKX:
                    pe.wait_ge(s_w1, 16 * W1_LOADS)
                for k in range(6):
                    front_part(st, 0, 0, k, False)

                def body(g, p, first, last):
                    for t in range(UN):
                        slot(st, g, p, t, first, last, False)
                groups(pe, body)
                for t in range(7):
                    slot(st, NG, NG % 2, t, False, True, True)

            def experts(st):
                n = CHUNKS[st]

                def routing(g, p, k):
                    if k == 0:
                        pe.wait_ge(s_combTe, at("combTe", st, g, 0))
                        transposed_x(st, g, p)
                    if k == 1:
                        pe.wait_ge(s_xTe, at("xTe", st, g, 1))
                        for b in range(GB):
                            m = pe.matmul(front[:, b * NE[st]:(b + 1) * NE[st]], xT[:, p, b * S:(b + 1) * S], gw[st][:, :], start=True, stop=True)
                        m.then_inc(s_lg, 1)
                    if k == 2:
                        pe.wait_ge(s_comb, at("comb", st, g, 1))
                        for b in range(GB):
                            m = pe.transpose(front[:, :].bitcast(BF16)[:, b * S:(b + 1) * S], combp[:, b, :], idb[:, :])
                        m.then_inc(s_combT, 1)

                def chunk(g, p, c):
                    pg, pc = before(st, g, c)
                    e = c // (C2 // E2) if st == TOP2 else c
                    cols = slice(c * 128, (c + 1) * 128)
                    pe.wait_ge(s_silu, at("silu", st, pg, pc + 1))
                    pe.matmul(score[:, 0, (c % 2) * GT:(c % 2 + 1) * GT], wg[st][:, cols], xT[:, p, :], start=True, stop=True).then_inc(s_gate, 1)
                    pe.wait_ge(s_gu, at("gu", st, pg, pc + 1))
                    pe.matmul(score[:, 1, (c % 2) * GT:(c % 2 + 1) * GT], wu[st][:, cols], xT[:, p, :], start=True, stop=True).then_inc(s_up, 1)
                    if st == TOP2 or c < C1:
                        if c == 0:
                            pe.wait_ge(s_combTe, at("combTe", st, g, 1))
                        pe.wait_ge(s_h, at("h", st, g, c - 1))
                        pe.matmul(turned[:, (c % 2) * GT:(c % 2 + 1) * GT], sel[st][:, e, :], combT[:, p, :], start=True, stop=True).then_inc(s_cw, 1)

                def down(g, c):
                    if st == MOE and c == C1:
                        pe.wait_ge(s_gu, at("gu", st, g, c + 1))
                        rows = gu
                    else:
                        pe.wait_ge(s_h, at("h", st, g, c + 1))
                        rows = hid
                    if c == 0:
                        pe.wait_ge(s_xupd, at("xupd", st, g, 0))
                    for b in range(GB):
                        m = pe.matmul(back[:, b * D:(b + 1) * D], rows[:, c % 2, b * S:(b + 1) * S], wd[st][:, c, :],
                                      start=(c == 0 and b == 0), stop=(c == n - 1), skip_group_check=True)
                    m.then_inc(s_down, 1)

                if st == TOP2:
                    pe.wait_ge(s_w2, 16 * 3)
                else:
                    pe.wait_ge(s_w1, 16 * W1_LOADS)
                    pe.wait_ge(s_tab, 16 * 3)
                pe.wait_ge(s_xupd, at("xupd", st, 0, 0))
                for k in range(3):
                    routing(0, 0, k)
                ROUTE_AT = {1: 0, 3: 1, n - 1: 2}

                def body(g, p, first, last):
                    for c in range(n):
                        if c in ROUTE_AT and not last:
                            routing(g + 1, 1 - p, ROUTE_AT[c])
                        if c == 0 and not first:
                            down(g - 1, n - 1)
                        chunk(g, p, c)
                        if c >= 1:
                            down(g, c - 1)
                groups(pe, body)
                down(NG - 1, n - 1)

            attention(SELF)
            attention(CROSS)
            experts(MOE)
            attention(LINEAR)
            attention(MASKX)
            experts(TOP2)

        @block.vector
        def _(dve):
            dve.memset(spread[:, 0, :, :], 0.0).then_inc(s_zero, 1)
            dve.memset(back[:, :], 0.0).then_inc(s_zero, 1)
            dve.wait_ge(s_x0, 16)
            dve.sem_inc(s_xupd, 1)

            def rows(g):
                return X[:, bass.ds(g * GB, GB), :]

            def statistics(st, g, p):
                if st > SELF:
                    dve.wait_ge(s_xupd, at("xupd", st - 1, g, 1))
                xg = rows(g)
                dve.wait_ge(s_aggr, at("aggr", st, g, 0))
                for b in range(GB):
                    dve.bn_stats(stats[:, b, :], xg[:, b, :]).then_inc(s_stat, 1)
                dve.wait_ge(s_stat, at("stat", st, g, GB))
                settle(dve, "dve")
                for b in range(GB):
                    dve.bn_aggr(mv[:, p, b, :], stats[:, b, :]).then_inc(s_aggr, 1)
                dve.wait_ge(s_aggr, at("aggr", st, g, GB))
                dve.wait_ge(s_rstd, at("rstd", st, g, 0))
                dve.tensor_scalar(veps[:, :], mv[:, p, :, 1], LN_EPS, None, ALU.add).then_inc(s_veps, 1)

            def normalise(st, g, p):
                dve.wait_ge(s_rstd, at("rstd", st, g, 1))
                xg = rows(g)
                for b in range(GB):
                    dve.tensor_scalar(xn[:, p, b, :], xg[:, b, :], mv[:, p, b, 0:1], rstd[:, p, b:b + 1], ALU.subtract, ALU.mult).then_inc(s_xn, 1)

            def front_part(st, g, p, k):
                if k == 0:
                    normalise(st, g, p)
                if k == 2 and st == LINEAR:
                    dve.wait_ge(s_spread, at("spread", st, g - 1, 0))
                    dve.wait_ge(s_phi, at("phi", st, g, 2))
                    dve.scalar_tensor_tensor(src[:, p, :], phi_e[:, :], 1.0, phi_r[:, :], ALU.min, ALU.add).then_inc(s_qe, 1)
                if k == 3 and st == LINEAR:
                    dve.wait_ge(s_phi, at("phi", st, g, 4))
                    dve.scalar_tensor_tensor(dense[:, p, :], phi_e[:, :], 1.0, phi_r[:, :], ALU.min, ALU.add).then_inc(s_ke, 1)

            def scores(st, g, t):
                dve.wait_ge(s_s, at("s", st, g, t + 1))
                sv = score[:, t % 2, :].rearrange("p (h k) -> p h k", h=UH)
                tv = T[:, t % 4, :].rearrange("p (h k) -> p h k", h=UH)
                nm = negm[:, t % 2, :]
                if st == LINEAR:
                    dve.tensor_tensor(tv, sv, cm[:, :].unsqueeze(1).broadcast_to([128, UH, S]), ALU.mult).then_inc(s_t, 1)
                elif st == MASKX:
                    dve.scalar_tensor_tensor(tv, sv, SCALE, mneg[:, :].unsqueeze(1).broadcast_to([128, UH, S]), ALU.mult, ALU.add).then_inc(s_sm, 1)
                    dve.wait_ge(s_sm, at("sm", st, g, t + 1))
                    dve.wait_ge(s_t, at("t", st, g, t - 1))
                    dve.tensor_reduce(nm, tv, AX.X, ALU.max, negate=True).then_inc(s_negm, 1)
                else:
                    dve.tensor_reduce(nm, sv, AX.X, ALU.max, negate=True).then_inc(s_negm, 1)
                    dve.wait_ge(s_negm, at("negm", st, g, t + 1))
                    dve.tensor_tensor(tv, sv, nm.unsqueeze(2).broadcast_to([128, UH, S]), ALU.add).then_inc(s_t, 1)

            def divide(st, g, p, b):
                dve.wait_ge(s_oq, at("oq", st, g, b + 1))
                ov = back[:, :].rearrange("p (h r) -> p h r", h=H)
                d = ov[:, :, HD]
                if st == LINEAR:
                    dve.tensor_scalar(den[:, :], d, DEN_EPS, None, ALU.add).then_inc(s_den, 1)
                    dve.wait_ge(s_den, at("den", st, g, b + 1))
                    d = den[:, :]
                dve.reciprocal(rden[:, :], d).then_inc(s_rden, 1)
                dve.wait_ge(s_rden, at("rden", st, g, b + 1))
                dve.tensor_tensor(O[:, p, b, :].rearrange("p (h d) -> p h d", d=HD), ov[:, :, 0:HD],
                                  rden[:, :].unsqueeze(2).broadcast_to([128, H, HD]), ALU.mult).then_inc(s_on, 1)

            def residual(st, g):
                xg = rows(g)
                if st == MASKX:
                    dve.tensor_tensor(xg, xg, bo[:, :].unsqueeze(1).broadcast_to([128, GB, D]), ALU.add).then_inc(s_bias, 1)
                    dve.wait_ge(s_bias, at("bias", st, g, 1))
                dve.wait_ge(s_y, at("y", st, g, 1))
                dve.tensor_tensor(xg, front[:, :].rearrange("p (b d) -> p b d", b=GB), xg, ALU.add).then_inc(s_xupd, 1)

            def slot(st, g, p, t, first, last, flush):
                if not flush:
                    if t == 0 and not last:
                        statistics(st, g + 1, 1 - p)
                    scores(st, g, t)
                    if not last:
                        front_part(st, g + 1, 1 - p, t)
                if t % 2 == 1:
                    if t >= 5 and not flush:
                        divide(st, g, p, (t - 5) // 2)
                    elif t < 5 and not first:
                        divide(st, g - 1, 1 - p, (t + UN - 5) // 2)
                if t == 6 and not first:
                    residual(st, g - 1)

            def attention(st):
                if st == MASKX:
                    dve.tensor_scalar(mneg[:, :], mneg[:, :], -1.0, 1.0, ALU.mult, ALU.add).then_inc(s_mneg, 1)
                    dve.wait_ge(s_mneg, 1)
                    dve.tensor_scalar(mneg[:, :], mneg[:, :], MASKED, None, ALU.mult).then_inc(s_mneg, 1)
                    dve.wait_ge(s_mneg, 2)
                statistics(st, 0, 0)
                for k in range(4):
                    front_part(st, 0, 0, k)
                if st == SELF:
                    dve.wait_ge(s_x1, 16)

                def body(g, p, first, last):
                    for t in range(UN):
                        slot(st, g, p, t, first, last, False)
                groups(dve, body)
                for t in range(7):
                    slot(st, NG, NG % 2, t, False, True, True)

            def experts(st):
                n, ne = CHUNKS[st], NE[st]
                w = GB * ne

                def step(g, k, ins):
                    ins.then_inc(s_route, 1)
                    dve.wait_ge(s_route, at("route", st, g, k))

                def small(i, width=w):
                    return lr[:, i, 0:width]

                def by_row(a, m=ne):
                    return a.rearrange("p (b e) -> p b e", b=GB)

                def ranks(g, k, val, m, out_i):
                    keep = {4: 2, 16: 4, 8: 2}[m]
                    v3 = val.rearrange("p (b e) -> p b e", b=GB)
                    shape = [128, GB, m, m]
                    a = wide[:, 0:GB * m * m]
                    bq = wide[:, 1024:1024 + GB * m * m]
                    comp = v3.unsqueeze(2).broadcast_to(shape)
                    cand = v3.unsqueeze(3).broadcast_to(shape)
                    av = a.rearrange("p (b j i) -> p b j i", b=GB, j=m)
                    bv = bq.rearrange("p (b j i) -> p b j i", b=GB, j=m)
                    left = tr[:, 0:m, 0:m].unsqueeze(1).broadcast_to(shape)
                    dve.tensor_tensor(av, comp, cand, ALU.is_equal).then_inc(s_route, 1)
                    step(g, k + 2, dve.tensor_tensor(bv, comp, cand, ALU.is_gt))
                    step(g, k + 3, dve.tensor_tensor(av, av, left, ALU.mult))
                    step(g, k + 4, dve.tensor_tensor(a, a, bq, ALU.add))
                    step(g, k + 5, dve.tensor_reduce(lr[:, out_i, 0:GB * m], a.rearrange("p (c i) -> p c i", i=m), AX.X, ALU.add))
                    step(g, k + 6, dve.tensor_scalar(lr[:, out_i, 0:GB * m], lr[:, out_i, 0:GB * m], float(keep), None, ALU.is_lt))

                def parts(g, k, c):
                    c3 = by_row(c)
                    r = by_row(small(12))
                    step(g, k + 1, dve.tensor_copy(combp[:, :, 0:ne], c3))
                    step(g, k + 2, dve.tensor_tensor(r, c3, combp[:, :, 0:ne], ALU.subtract))
                    step(g, k + 3, dve.tensor_copy(combp[:, :, 16:16 + ne], r))
                    step(g, k + 4, dve.tensor_tensor(r, r, combp[:, :, 16:16 + ne], ALU.subtract))
                    dve.tensor_copy(combp[:, :, 32:32 + ne], r).then_inc(s_comb, 1)

                def route_moe(g, k):
                    if k == 0:
                        dve.wait_ge(s_rexp, at("rexp", st, g, 1))
                        step(g, 1, dve.tensor_scalar(small(1), small(0), 1.0, None, ALU.add))
                        step(g, 2, dve.reciprocal(small(2), small(1)))
                        step(g, 3, dve.tensor_tensor(by_row(small(3)), by_row(small(2)), bias_r[:, :].unsqueeze(1).broadcast_to([128, GB, E1]), ALU.add))
                        a = small(3).rearrange("p (c i) -> p c i", i=4)
                        pr = wide[:, 0:6 * 16].rearrange("p (c i) -> p c i", i=6)
                        dve.tensor_tensor(pr[:, :, 0:3], a[:, :, 0:3], a[:, :, 1:4], ALU.add).then_inc(s_route, 1)
                        dve.tensor_tensor(pr[:, :, 3:5], a[:, :, 0:2], a[:, :, 2:4], ALU.add).then_inc(s_route, 1)
                        step(g, 6, dve.tensor_tensor(pr[:, :, 5:6], a[:, :, 0:1], a[:, :, 3:4], ALU.add))
                        step(g, 7, dve.tensor_reduce(lr[:, 4, 0:16], pr, AX.X, ALU.max))
                    if k == 1:
                        ranks(g, 7, lr[:, 4, 0:16], 4, 5)
                        step(g, 14, dve.tensor_tensor(small(6).rearrange("p (c i) -> p c i", i=4), small(3).rearrange("p (c i) -> p c i", i=4),
                                                      lr[:, 5, 0:16].unsqueeze(2).broadcast_to([128, 16, 4]), ALU.mult))
                    if k == 2:
                        ranks(g, 14, small(6), 16, 7)
                    if k == 3:
                        step(g, 21, dve.tensor_tensor(small(8), small(6), small(7), ALU.mult))
                        weights(g, 21, 2.5, 1e-20)

                def weights(g, k, scale, eps):
                    dve.tensor_reduce(lr[:, 9, 0:GB], by_row(small(8)), AX.X, ALU.add).then_inc(s_wsum, 1)
                    dve.wait_ge(s_wsum, at("wsum", st, g, 1))
                    dve.tensor_scalar(lr[:, 10, 0:GB], lr[:, 9, 0:GB], eps, None, ALU.add).then_inc(s_wsum, 1)
                    dve.wait_ge(s_wsum, at("wsum", st, g, 2))
                    dve.reciprocal(lr[:, 11, 0:GB], lr[:, 10, 0:GB]).then_inc(s_wsum, 1)
                    dve.wait_ge(s_wsum, at("wsum", st, g, 3))
                    dve.tensor_tensor(by_row(small(13)), by_row(small(8)), lr[:, 11, 0:GB].unsqueeze(2).broadcast_to([128, GB, ne]), ALU.mult).then_inc(s_wsum, 1)
                    dve.wait_ge(s_wsum, at("wsum", st, g, 4))
                    dve.tensor_scalar(small(8), small(13), scale, None, ALU.mult).then_inc(s_wsum, 1)
                    dve.wait_ge(s_wsum, at("wsum", st, g, 5))
                    parts(g, k, small(8))

                def route_top2(g, k):
                    if k == 0:
                        dve.wait_ge(s_lg, at("lg", st, g, 1))
                        dve.tensor_copy(small(0), front[:, 0:w]).then_inc(s_lge, 1)
                        dve.wait_ge(s_lge, at("lge", st, g, 1))
                        step(g, 1, dve.tensor_reduce(lr[:, 1, 0:GB], by_row(small(0)), AX.X, ALU.max))
                        step(g, 2, dve.tensor_tensor(by_row(small(2)), by_row(small(0)), lr[:, 1, 0:GB].unsqueeze(2).broadcast_to([128, GB, ne]), ALU.subtract))
                    if k == 1:
                        ranks(g, 2, small(0), 8, 7)
                    if k == 3:
                        dve.wait_ge(s_rexp, at("rexp", st, g, 1))
                        step(g, 9, dve.tensor_tensor(small(8), small(3), small(7), ALU.mult))
                        weights(g, 9, 1.0, 0.0)

                def routing(g, p, k):
                    if k == 0:
                        statistics(st, g, p)
                        normalise(st, g, p)
                    elif st == MOE:
                        route_moe(g, k - 1)
                    else:
                        route_top2(g, k - 1)

                if st == MOE:
                    dve.wait_ge(s_w1, 16 * W1_LOADS)
                    dve.wait_ge(s_ones, 3)
                for k in range(5):
                    routing(0, 0, k)
                ROUTE_AT = {0: 0, 3: 1, 4: 2, 5: 3, 6: 4}

                def chunk(g, c):
                    b = c % 2
                    dve.wait_ge(s_up, at("up", st, g, c + 1))
                    dve.wait_ge(s_silu, at("silu", st, g, c + 1))
                    dve.tensor_tensor(gu[:, b, :], score[:, 1, b * GT:(b + 1) * GT], sg[:, b, :], ALU.mult).then_inc(s_gu, 1)
                    if st == TOP2 or c < C1:
                        dve.wait_ge(s_cw, at("cw", st, g, c + 1))
                        dve.wait_ge(s_gu, at("gu", st, g, c + 1))
                        dve.tensor_tensor(hid[:, b, :], turned[:, b * GT:(b + 1) * GT], gu[:, b, :], ALU.mult).then_inc(s_h, 1)

                def body(g, p, first, last):
                    for c in range(n):
                        chunk(g, c)
                        if c in ROUTE_AT and not last:
                            routing(g + 1, 1 - p, ROUTE_AT[c])
                        if c == 0 and not first:
                            added(g - 1)

                def added(g):
                    xg = rows(g)
                    dve.wait_ge(s_down, at("down", st, g, n))
                    dve.tensor_tensor(xg, back[:, :].rearrange("p (b d) -> p b d", b=GB), xg, ALU.add).then_inc(s_xupd, 1)
                groups(dve, body)
                added(NG - 1)

            attention(SELF)
            attention(CROSS)
            experts(MOE)
            attention(LINEAR)
            attention(MASKX)
            experts(TOP2)


_INS = ["x", "ctx_1024", "mask_1x1xSxS2_fk0", "L0_attn_w_qkv", "L0_attn_w_out", "L0_xattn_Wo",
        "L0_ffn_gate_kernel", "L0_ffn_gate_bias", "L0_ffn_w_gate", "L0_ffn_w_up", "L0_ffn_w_down",
        "L0_ffn_sw_gate", "L0_ffn_sw_up", "L0_ffn_sw_down", "L1_attn_Wq", "L1_attn_Wk",
        "L1_attn_Wv", "L1_attn_Wo", "L1_xattn_Wq", "L1_xattn_Wk", "L1_xattn_Wv", "L1_xattn_Wo",
        "L1_xattn_bo", "L1_ffn_gate", "L1_ffn_experts_w1", "L1_ffn_experts_w2", "L1_ffn_experts_w3"]


def constants():
    k = np.arange(128)
    col = np.arange(128)
    sel1 = np.stack([(k[:, None] < 48) & (k[:, None] % 16 == 2 * c + (col[None, :] >= M1)) for c in range(C1)], 1)
    sel2 = np.stack([(k[:, None] < 48) & (k[:, None] % 16 == e) & (col[None, :] >= 0) for e in range(E2)], 1)
    return {
        "ident": np.eye(128, dtype=np.float32),
        "causal": (k[:, None] <= k[None, :]).astype(np.float32),
        "tri": (np.arange(16)[None, :] < np.arange(16)[:, None]).astype(np.float32),
        "sel1": sel1.astype(np.float32),
        "sel2": sel2.astype(np.float32),
    }


def kernel(**inputs):
    import concourse.bacc as _bacc
    from concourse.bass_utils import run_bass_kernel_spmd as _run

    nc = _bacc.Bacc("TRN2", target_bir_lowering=False, num_devices=1)
    arrays, args = {}, []
    for name, a in [(n, inputs[n]) for n in _INS] + list(constants().items()):
        a = np.ascontiguousarray(a)
        arrays[f"in_{name}"] = a
        args.append(nc.dram_tensor(f"in_{name}", a.shape, mybir.dt.from_np(a.dtype), kind="ExternalInput").ap())
    args.append(nc.dram_tensor("out_0", (B, S, D), F32, kind="ExternalOutput").ap())
    decoder(nc, *args)
    r = _run(nc, [arrays], core_ids=[0])
    return r.results[0]["out_0"]
```

```python
from contextlib import ExitStack

import numpy as np

import concourse.bass as bass
from concourse import mybir

F32 = mybir.dt.float32
BF16 = mybir.dt.bfloat16
I32 = mybir.dt.int32
ALU = mybir.AluOpType
ACT = mybir.ActivationFunctionType
AX = mybir.AxisListType

B, S, D = 32, 128, 128
H, HD = 16, 8
GB = 4
NG = B // GB
GT = GB * S
UH = 8
UN = GB * H // UH
UW = UH * S
SCALE = float(1.0 / np.sqrt(np.float32(HD)))
MASKED = -1e9
LN_EPS = 1e-5
DEN_EPS = 1e-8
E1, M1 = 16, 64
E2, M2 = 8, 512
C1 = E1 * M1 // 128
KEEP2 = 2
TOKENS = B * S
ROW = D + 2
DEST, WEIGHT = D, D + 1
REGION = TOKENS + S
TILES = TOKENS * KEEP2 // S + E2
GROUP_SENT = 16 * GB * KEEP2
QT = 4
TABLE_STEPS = 17
FAR = 65536.0

W1_LOADS = 21

SELF, CROSS, MOE, LINEAR, MASKX, ROUTE, ADD = range(7)
CHUNKS = {MOE: C1 + 1}
ATTN = (SELF, CROSS, LINEAR, MASKX)

STARTS = {"xupd": 1}

PER_GROUP = {
    "xupd":   (1, 1, 1, 1, 1, 0, 1),
    "stat":   (4, 4, 4, 4, 4, 4, 0),
    "aggr":   (4, 4, 4, 4, 4, 4, 0),
    "veps":   (1, 1, 1, 1, 1, 1, 0),
    "rstd":   (1, 1, 1, 1, 1, 1, 0),
    "xn":     (4, 4, 4, 4, 4, 4, 0),
    "xT":     (1, 1, 1, 1, 1, 1, 0),
    "xTe":    (1, 1, 1, 1, 1, 1, 0),
    "ctx":    (0, 16, 0, 0, 16, 0, 0),
    "cT":     (0, 1, 0, 0, 1, 0, 0),
    "cTe":    (0, 1, 0, 0, 1, 0, 0),
    "q":      (1, 0, 0, 1, 1, 0, 0),
    "qe":     (1, 0, 0, 1, 1, 0, 0),
    "k":      (1, 0, 0, 1, 1, 0, 0),
    "ke":     (1, 0, 0, 1, 1, 0, 0),
    "phi":    (0, 0, 0, 4, 0, 0, 0),
    "v":      (1, 0, 0, 1, 1, 0, 0),
    "ve":     (1, 1, 0, 1, 1, 0, 0),
    "spread": (256, 256, 0, 256, 256, 0, 0),
    "s":      (UN, UN, 0, UN, UN, 0, 0),
    "sm":     (0, 0, 0, 0, UN, 0, 0),
    "negm":   (UN, UN, 0, 0, UN, 0, 0),
    "t":      (UN, UN, 0, UN, UN, 0, 0),
    "e":      (UN, UN, 0, 0, UN, 0, 0),
    "pt":     (UN, UN, 0, 0, UN, 0, 0),
    "pte":    (UN, UN, 0, 0, UN, 0, 0),
    "pv":     (UN, UN, 0, UN, UN, 0, 0),
    "ot":     (GB, GB, 0, GB, GB, 0, 0),
    "oq":     (GB, GB, 0, GB, GB, 0, 0),
    "den":    (0, 0, 0, GB, 0, 0, 0),
    "rden":   (GB, GB, 0, GB, GB, 0, 0),
    "on":     (GB, GB, 0, GB, GB, 0, 0),
    "oT":     (1, 1, 0, 1, 1, 0, 0),
    "oTe":    (1, 1, 0, 1, 1, 0, 0),
    "y":      (1, 1, 0, 1, 1, 0, 0),
    "bias":   (0, 0, 0, 0, 1, 0, 0),
    "lg":     (0, 0, 1, 0, 0, 1, 0),
    "lge":    (0, 0, 0, 0, 0, 1, 0),
    "route":  (0, 0, 25, 0, 0, 18, 0),
    "rexp":   (0, 0, 1, 0, 0, 1, 0),
    "comb":   (0, 0, 1, 0, 0, 0, 0),
    "combT":  (0, 0, 1, 0, 0, 0, 0),
    "combTe": (0, 0, 1, 0, 0, 0, 0),
    "pay":    (0, 0, 0, 0, 0, 2, 0),
    "payw":   (0, 0, 0, 0, 0, 1, 0),
    "chosen": (0, 0, 0, 0, 0, 1, 0),
    "place":  (0, 0, 0, 0, 0, 1, 0),
    "index":  (0, 0, 0, 0, 0, 1, 0),
    "back":   (0, 0, 0, 0, 0, 0, 32),
    "half":   (0, 0, 0, 0, 0, 0, 1),
    "gate":   (0, 0, C1 + 1, 0, 0, 0, 0),
    "up":     (0, 0, C1 + 1, 0, 0, 0, 0),
    "cw":     (0, 0, C1, 0, 0, 0, 0),
    "silu":   (0, 0, C1 + 1, 0, 0, 0, 0),
    "gu":     (0, 0, C1 + 1, 0, 0, 0, 0),
    "h":      (0, 0, C1, 0, 0, 0, 0),
    "wsum":   (0, 0, 5, 0, 0, 3, 0),
    "down":   (0, 0, C1 + 1, 0, 0, 0, 0),
}


def decoder(nc, x, ctx, mask, w_qkv, w_out, x0_wo, gate1, bias1, w_gate1, w_up1, w_down1, s_gate1,
            s_up1, s_down1, l_wq, l_wk, l_wv, l_wo, m_wq, m_wk, m_wv, m_wo, m_bo, gate2, e_w1, e_w2,
            e_w3, ident, causal, tri, sel1, before_t, starts, steps, dests, padding, out):
    with ExitStack() as stack:
        def sb(name, shape, dt=F32):
            return stack.enter_context(nc.sbuf_tensor(name, shape, dt))

        def ps(name, shape, dt=F32):
            return stack.enter_context(nc.psum_tensor(name, shape, dt))

        def semaphore(name):
            return stack.enter_context(nc.semaphore("s_" + name))

        s_xupd = semaphore("xupd")
        s_stat = semaphore("stat")
        s_aggr = semaphore("aggr")
        s_veps = semaphore("veps")
        s_rstd = semaphore("rstd")
        s_xn = semaphore("xn")
        s_xT = semaphore("xT")
        s_xTe = semaphore("xTe")
        s_ctx = semaphore("ctx")
        s_cT = semaphore("cT")
        s_cTe = semaphore("cTe")
        s_q = semaphore("q")
        s_qe = semaphore("qe")
        s_k = semaphore("k")
        s_ke = semaphore("ke")
        s_phi = semaphore("phi")
        s_v = semaphore("v")
        s_ve = semaphore("ve")
        s_spread = semaphore("spread")
        s_s = semaphore("s")
        s_sm = semaphore("sm")
        s_negm = semaphore("negm")
        s_t = semaphore("t")
        s_e = semaphore("e")
        s_pt = semaphore("pt")
        s_pte = semaphore("pte")
        s_pv = semaphore("pv")
        s_ot = semaphore("ot")
        s_oq = semaphore("oq")
        s_den = semaphore("den")
        s_rden = semaphore("rden")
        s_on = semaphore("on")
        s_oT = semaphore("oT")
        s_oTe = semaphore("oTe")
        s_y = semaphore("y")
        s_bias = semaphore("bias")
        s_lg = semaphore("lg")
        s_lge = semaphore("lge")
        s_route = semaphore("route")
        s_rexp = semaphore("rexp")
        s_comb = semaphore("comb")
        s_combT = semaphore("combT")
        s_combTe = semaphore("combTe")
        s_gate = semaphore("gate")
        s_up = semaphore("up")
        s_cw = semaphore("cw")
        s_silu = semaphore("silu")
        s_gu = semaphore("gu")
        s_h = semaphore("h")
        s_down = semaphore("down")
        s_wsum = semaphore("wsum")

        s_pay = semaphore("pay")
        s_payw = semaphore("payw")
        s_chosen = semaphore("chosen")
        s_place = semaphore("place")
        s_index = semaphore("index")
        s_sent = [semaphore("sent_even"), semaphore("sent_odd")]
        s_back = semaphore("back")
        s_half = semaphore("half")

        s_table = semaphore("table")
        s_pad = semaphore("pad")
        s_rows = [semaphore("rows%d" % q) for q in range(QT)]
        s_rT = semaphore("rT")
        s_rTe = semaphore("rTe")
        s_tg = semaphore("tg")
        s_tu = semaphore("tu")
        s_tsilu = semaphore("tsilu")
        s_thid = semaphore("thid")
        s_hT = semaphore("hT")
        s_hTe = semaphore("hTe")
        s_ty = semaphore("ty")
        s_yw = semaphore("yw")
        s_ysent = [semaphore("ysent%d" % q) for q in range(QT)]

        def at(name, st, g, k):
            rate = PER_GROUP[name]
            value = STARTS.get(name, 0) + NG * sum(rate[:st]) + rate[st] * g + k
            return max(value, 0) if isinstance(value, int) else value

        s_passed = {n: semaphore("passed_" + n) for n in ("sp", "pool", "dve")}

        def settle(eng, name):
            eng.sem_inc(s_passed[name], 1)

        s_x0 = semaphore("x0")
        s_x1 = semaphore("x1")
        s_w0 = semaphore("w0")
        s_tab = semaphore("tab")
        s_w1 = semaphore("w1")
        s_w2 = semaphore("w2")
        s_out = semaphore("out")
        s_wT = semaphore("wT")
        s_wTe = semaphore("wTe")
        s_zero = semaphore("zero")
        s_ones = semaphore("ones")
        s_mneg = semaphore("mneg")

        score = ps("score", [128, 2, UW])
        turned = ps("turned", [128, UW])
        front = ps("front", [128, GT])
        back = ps("back", [128, GT])

        X = sb("X", [128, B, D])
        spread = sb("spread", [128, 2, H, GT])
        crow = sb("crow", [128, 2, GB, D])
        cT = sb("cT", [128, 2, GT])
        dense = sb("dense", [128, 2, GT])
        src = sb("src", [128, 2, GT])
        phi_e = sb("phi_e", [128, GT])
        phi_r = sb("phi_r", [128, GT])
        V = sb("V", [128, 2, GB, H, HD + 1])
        xn = sb("xn", [128, 2, GB, D])
        xT = sb("xT", [128, 2, GT])
        work = sb("work", [128, 9 * UW])
        T = work[:, 0:4 * UW].rearrange("p (r c) -> p r c", r=4)
        PT = work[:, 4 * UW:6 * UW].rearrange("p (r c) -> p r c", r=2)
        OT = work[:, 6 * UW:7 * UW].rearrange("p (r c) -> p r c", r=2)
        O = work[:, 7 * UW:8 * UW].rearrange("p (r b c) -> p r b c", r=2, b=GB)
        OdT = work[:, 8 * UW:9 * UW].rearrange("p (r c) -> p r c", r=2)
        sg = work[:, 0:GT * 2].rearrange("p (r c) -> p r c", r=2)
        gu = work[:, GT * 2:GT * 4].rearrange("p (r c) -> p r c", r=2)
        hid = work[:, GT * 4:GT * 6].rearrange("p (r c) -> p r c", r=2)
        wide = work[:, GT * 6:GT * 10]
        wraw = sb("wraw", [128, 9, D])
        wT = sb("wT", [128, 9, D])
        wm = sb("wm", [128, 4, D])
        bo = sb("bo", [128, D])
        mneg = sb("mneg", [128, D])
        cm = sb("cm", [128, D])
        idf = sb("idf", [128, 128])
        idb = sb("idb", [128, 128], BF16)
        tr = sb("tr", [128, 16, 16])
        stats = sb("stats", [128, GB, 6])
        mv = sb("mv", [128, 2, GB, 2])
        veps = sb("veps", [128, GB])
        half = sb("half", [128, GB])
        rstd = sb("rstd", [128, 2, GB])
        negm = sb("negm", [128, 2, UH])
        den = sb("den", [128, H])
        rden = sb("rden", [128, H])
        sel = sb("sel1s", [128, C1, 128], BF16)
        gw = {MOE: sb("gw1", [128, E1]), ROUTE: sb("gw2", [128, E2])}
        earlier = sb("earlier", [128, 2, 128], BF16)
        start_r = sb("start_r", [128, E2])
        base = sb("base", [128, E2])
        step_r = sb("step_r", [128, 32 + TILES])
        dest = sb("dest", [128, B, KEEP2])
        chosen = sb("chosen", [128, 2, GB * E2], BF16)
        indexf = sb("indexf", [128, GB, KEEP2])
        index = sb("index", [128, 2, GB, KEEP2], I32)
        yindex = sb("yindex", [128, QT], I32)
        tl = sb("tl", [1, 8, TILES])
        table = sb("table", [1, 2 * TILES + E2], I32)
        bias_r = sb("bias_r", [128, E1])
        wg1 = sb("wg1", [128, E1 * M1 + 128])
        wu1 = sb("wu1", [128, E1 * M1 + 128])
        wd1 = sb("wd1", [128, C1 + 1, D])
        heavy = spread[:, :, :, :].rearrange("p r h c -> p (r h c)")
        WE = E2 * M2
        wg2 = heavy[:, 0:WE]
        wu2 = heavy[:, WE:2 * WE]
        wd2 = heavy[:, 2 * WE:3 * WE]
        t_sg = work[:, 0:2 * M2].rearrange("p (r c) -> p r c", r=2)
        t_hid = work[:, 2 * M2:4 * M2].rearrange("p (r c) -> p r c", r=2)
        t_hT = work[:, 4 * M2:6 * M2].rearrange("p (r c) -> p r c", r=2)
        free = GT * 10
        pay = work[:, free:free + 2 * GB * KEEP2 * ROW].rearrange("p (r b c w) -> p r b c w", r=2, b=GB, c=KEEP2)
        free += 2 * GB * KEEP2 * ROW
        t_rows = work[:, free:free + QT * ROW].rearrange("p (q w) -> p q w", q=QT)
        free += QT * ROW
        t_y = work[:, free:free + QT * D].rearrange("p (q w) -> p q w", q=QT)
        y_first, y_second = crow, dense[:, :, :].rearrange("p r (b d) -> p r b d", b=GB)
        routed = nc.dram_tensor("routed", (E2 * REGION + E2 * S, ROW), F32, kind="Internal").ap()
        outputs = nc.dram_tensor("outputs", (KEEP2 * TOKENS + 2 * E2 * S, D), F32, kind="Internal").ap()
        NR = 64
        lr = sb("lr", [128, 14, NR])
        combp = sb("combp", [128, GB, 128], BF16)
        combT = sb("combT", [128, 2, GT], BF16)
        WQ, WK, WV, WOUT, XWO, LQ, LK, LV, LO = range(9)
        MQ, MK, MV, MO = range(4)
        NE = {MOE: E1, ROUTE: E2}

        block = stack.enter_context(nc.Block())

        def groups(eng, body):
            body(0, 0, True, False)
            with eng.Fori(0, (NG - 2) // 2) as j:
                body(2 * j + 1, 1, False, False)
                body(2 * j + 2, 0, False, False)
            body(NG - 1, (NG - 1) % 2, False, True)

        def sent_before(g, p):
            return GROUP_SENT // 2 * (g - p)

        def landed(t, q):
            return 16 // QT * (t - q)

        def tiles(eng, body):
            for q in range(QT):
                body(q, q, q == 0, False)
            with eng.Fori(1, TILES // QT - 1) as j:
                for q in range(QT):
                    body(QT * j + q, q, False, False)
            for q in range(QT):
                body(TILES - QT + q, q, False, q == QT - 1)

        def before(st, g, c):
            if c >= 2:
                return g, c - 2
            n = CHUNKS[st]
            return g - 1, n - 1 if (n - 1) % 2 == c else n - 2

        @block.sync
        def _(sp):
            xv = x.rearrange("b s d -> s b d")
            sp.dma_start(X[:, 0:GB, :], xv[:, 0:GB, :]).then_inc(s_x0, 16)
            sp.dma_start(idf[:, :], ident).then_inc(s_w0, 16)
            sp.dma_start(wraw[:, 0:3, :], w_qkv.rearrange("(t o) i -> o t i", t=3)).then_inc(s_w0, 16)
            for n, w in ((WOUT, w_out), (XWO, x0_wo), (LQ, l_wq), (LK, l_wk), (LV, l_wv), (LO, l_wo)):
                sp.dma_start(wraw[:, n, :], w).then_inc(s_w0, 16)
            sp.dma_start(X[:, GB:B, :], xv[:, GB:B, :]).then_inc(s_x1, 16)
            for n, w in ((MQ, m_wq), (MK, m_wk), (MV, m_wv), (MO, m_wo)):
                sp.dma_start(wm[:, n, :], w).then_inc(s_w1, 16)
            sp.dma_start(bo[:, :], m_bo.rearrange("(a d) -> a d", a=1).broadcast_to([128, D])).then_inc(s_w1, 16)
            sp.dma_start(mneg[:, :], mask[0, 0]).then_inc(s_w1, 16)
            sp.dma_start(cm[:, :], causal).then_inc(s_w1, 16)
            sp.dma_start(tr[:, :, :], tri.rearrange("(a j) i -> a j i", a=1).broadcast_to([128, 16, 16])).then_inc(s_w1, 16)
            sp.dma_start(gw[MOE][:, :], gate1).then_inc(s_w1, 16)
            sp.dma_start(gw[ROUTE][:, :], gate2).then_inc(s_w1, 16)
            sp.dma_start(start_r[:, :], starts.rearrange("(a e) -> a e", a=1).broadcast_to([128, E2])).then_inc(s_w1, 16)
            sp.dma_start(base[:, :], starts.rearrange("(a e) -> a e", a=1).broadcast_to([128, E2])).then_inc(s_w1, 16)
            sp.dma_start(step_r[:, :], steps.rearrange("(a e) -> a e", a=1).broadcast_to([128, 32 + TILES])).then_inc(s_w1, 16)
            sp.dma_start(dest[:, :, :], dests).then_inc(s_w1, 16)
            sp.dma_start(routed[E2 * REGION:, :], padding[E2 * S:, :]).then_inc(s_pad, 16)
            sp.dma_start(bias_r[:, :], bias1.rearrange("(a d) -> a d", a=1).broadcast_to([128, E1])).then_inc(s_w1, 16)
            sp.dma_start(wg1[:, 0:E1 * M1].rearrange("p (e m) -> p e m", e=E1), w_gate1.rearrange("e h m -> h e m")).then_inc(s_w1, 16)
            sp.dma_start(wu1[:, 0:E1 * M1].rearrange("p (e m) -> p e m", e=E1), w_up1.rearrange("e h m -> h e m")).then_inc(s_w1, 16)
            sp.dma_start(wg1[:, E1 * M1:], s_gate1).then_inc(s_w1, 16)
            sp.dma_start(wu1[:, E1 * M1:], s_up1).then_inc(s_w1, 16)
            sp.dma_start(wd1[:, 0:C1, :], w_down1.rearrange("(c two) m h -> (two m) c h", two=2)).then_inc(s_w1, 16)
            sp.dma_start(wd1[:, C1, :], s_down1).then_inc(s_w1, 16)

            def context(st, g, p):
                sp.wait_ge(s_cT, at("cT", st, g - 1, 0))
                settle(sp, "sp")
                if st == CROSS:
                    sp.wait_ge(s_ve, at("ve", st, g - 1, 0))
                    settle(sp, "sp")
                sp.wait_ge(s_ctx, at("ctx", st, g, 0))
                settle(sp, "sp")
                b0 = g * GB
                sp.dma_start(crow[:, p, :, :], ctx.rearrange("b s d -> s b d")[:, bass.ds(b0, GB), :]).then_inc(s_ctx, 16)

            def spreading(st, g, p):
                if st == CROSS:
                    sp.wait_ge(s_cTe, at("cTe", st, g, 1))
                    settle(sp, "sp")
                    rows = cT
                else:
                    if st == LINEAR:
                        sp.wait_ge(s_qe, at("qe", st, g, 1))
                    else:
                        sp.wait_ge(s_ke, at("ke", st, g, 1))
                    settle(sp, "sp")
                    rows = src
                sp.wait_ge(s_spread, at("spread", st, g, 0))
                settle(sp, "sp")
                for h in range(H):
                    r = slice(HD * h, HD * h + HD)
                    sp.dma_start(spread[r, p, h, :], rows[r, p, :]).then_inc(s_spread, 16)

            sp.wait_ge(s_zero, 3)
            for st in ATTN:
                if st in (CROSS, MASKX):
                    context(st, 0, 0)
                spreading(st, 0, 0)

                def body(g, p, first, last):
                    if not last:
                        if st in (CROSS, MASKX):
                            context(st, g + 1, 1 - p)
                        spreading(st, g + 1, 1 - p)
                groups(sp, body)
            sp.wait_ge(s_s, at("s", MASKX, NG, 0))
            settle(sp, "sp")
            sp.dma_start(wg2.rearrange("p (e m) -> p e m", e=E2), e_w1.rearrange("e h m -> h e m")).then_inc(s_w2, 16)
            sp.dma_start(wu2.rearrange("p (e m) -> p e m", e=E2), e_w3.rearrange("e h m -> h e m")).then_inc(s_w2, 16)
            sp.dma_start(wd2.rearrange("p (e n) -> p e n", n=D), e_w2.rearrange("e (c p) h -> p (e c) h", p=128)).then_inc(s_w2, 16)

            sp.wait_ge(s_table, TABLE_STEPS)
            for e in range(E2):
                row = sp.value_load(table[0:1, 2 * TILES + e:2 * TILES + e + 1], min_val=0, max_val=E2 * REGION - S)
                sp.dma_start(routed[bass.ds(row, S), :], padding[e * S:(e + 1) * S, :]).then_inc(s_pad, 16)
            sp.wait_ge(s_pad, 16 * (1 + E2))
            for p in range(2):
                sp.wait_ge(s_sent[p], NG // 2 * GROUP_SENT)

            def fetch(t, q, first, last):
                row = sp.value_load(table[0:1, bass.ds(t, 1)], min_val=0, max_val=E2 * REGION + (E2 - 1) * S)
                if not isinstance(t, int) or t >= QT:
                    sp.wait_ge(s_rT, t - QT + 1)
                    settle(sp, "sp")
                    sp.wait_ge(s_yw, 2 * (t - QT + 1))
                    settle(sp, "sp")
                sp.dma_start(t_rows[:, q, :], routed[bass.ds(row, S), :]).then_inc(s_rows[q], 16)
            tiles(sp, fetch)

            def bring(g, p):
                sp.wait_ge(s_xupd, at("xupd", ADD, g - 1, 0))
                settle(sp, "sp")
                sp.wait_ge(s_back, at("back", ADD, g, 0))
                settle(sp, "sp")
                t0 = g * GT
                sp.dma_start(y_first[:, p, :, :], outputs[bass.ds(t0, GT), :].rearrange("(b s) d -> s b d", s=S)).then_inc(s_back, 16)
                t1 = g * GT + TOKENS
                sp.dma_start(y_second[:, p, :, :], outputs[bass.ds(t1, GT), :].rearrange("(b s) d -> s b d", s=S)).then_inc(s_back, 16)

            for q in range(QT):
                sp.wait_ge(s_ysent[q], landed(TILES + q, q))
            bring(0, 0)

            def store(g, p, first, last):
                if not last:
                    bring(g + 1, 1 - p)
                sp.wait_ge(s_xupd, at("xupd", ADD, g, 1))
                settle(sp, "sp")
                sp.dma_start(out.rearrange("b s d -> s b d")[:, bass.ds(g * GB, GB), :], X[:, bass.ds(g * GB, GB), :]).then_inc(s_out, 16)
            groups(sp, store)
            sp.wait_ge(s_out, 16 * NG)

        @block.gpsimd
        def _(pool):
            pool.dma_start(idb[:, :], ident).then_inc(s_tab, 16)
            pool.dma_start(sel[:, :, :], sel1).then_inc(s_tab, 16)
            pool.dma_start(earlier[:, :, :], before_t).then_inc(s_tab, 16)
            pool.memset(spread[:, 1, :, :], 0.0).then_inc(s_zero, 1)
            pool.memset(half[:, :], -0.5).then_inc(s_ones, 1)
            pool.memset(V[:, :, :, :, HD:HD + 1], 1.0).then_inc(s_ones, 1)
            pool.memset(combp[:, :, :], 0.0).then_inc(s_ones, 1)
            pool.wait_ge(s_ones, 3)

            def rsqrt(st, g, p):
                pool.wait_ge(s_veps, at("veps", st, g, 1))
                pool.tensor_tensor(rstd[:, p, :], veps[:, :], half[:, :], ALU.pow).then_inc(s_rstd, 1)

            def values(st, g, p):
                pool.wait_ge(s_ctx, at("ctx", st, g, 16))
                pool.wait_ge(s_pv, at("pv", st, g - 1, 0))
                settle(pool, "pool")
                pool.tensor_copy(V[:, p, :, :, 0:HD], crow[:, p, :, :].rearrange("p b (h d) -> p b h d", d=HD)).then_inc(s_ve, 1)

            def shift(st, g, t):
                pool.wait_ge(s_negm, at("negm", st, g, t + 1))
                tv = T[:, t % 4, :].rearrange("p (h k) -> p h k", h=UH)
                pool.tensor_tensor(tv, tv, negm[:, t % 2, :].unsqueeze(2).broadcast_to([128, UH, S]), ALU.add).then_inc(s_t, 1)

            def scatter(g, p):
                pool.wait_ge(s_pay, at("pay", ROUTE, g, 2))
                settle(pool, "pool")
                pool.wait_ge(s_payw, at("payw", ROUTE, g, 1))
                settle(pool, "pool")
                pool.wait_ge(s_index, at("index", ROUTE, g, 1))
                settle(pool, "pool")
                for b in range(GB):
                    for c in range(KEEP2):
                        pool.indirect_dma_start(out=routed, out_offset=bass.IndirectOffsetOnAxis(ap=index[:, p, b, c:c + 1], axis=0),
                                                in_=pay[:, p, b, c, :], in_offset=None).then_inc(s_sent[p], 16)

            for st in range(ADD):
                rsqrt(st, 0, 0)
                if st == CROSS:
                    values(st, 0, 0)

                def body(g, p, first, last):
                    if not last:
                        rsqrt(st, g + 1, 1 - p)
                        if st == CROSS:
                            values(st, g + 1, 1 - p)
                    if st == MASKX:
                        for t in range(UN):
                            shift(st, g, t)
                    if st == ROUTE:
                        scatter(g, p)
                groups(pool, body)

            def send(t, q, first, last):
                pool.wait_ge(s_yw, 2 * (t + 1))
                settle(pool, "pool")
                pool.indirect_dma_start(out=outputs, out_offset=bass.IndirectOffsetOnAxis(ap=yindex[:, q:q + 1], axis=0),
                                        in_=t_y[:, q, :], in_offset=None).then_inc(s_ysent[q], 16)
            tiles(pool, send)

        @block.scalar
        def _(act):
            for n in range(3):
                act.wait_ge(s_wT, n + 1)
                act.activation(wT[:, 3 * n:3 * n + 3, :], front[:, 0:3 * D].rearrange("p (a b) -> p a b", a=3), ACT.Copy).then_inc(s_wTe, 1)

            def features():
                act.activation(phi_e[:, :], front[:, :], ACT.Exp).then_inc(s_phi, 1)
                act.activation(phi_r[:, :], front[:, :], ACT.Relu).then_inc(s_phi, 1)

            def front_part(st, g, p, k):
                if k == 0 and st in (CROSS, MASKX):
                    if st == CROSS:
                        act.wait_ge(s_spread, at("spread", st, g - 1, 0))
                    act.wait_ge(s_cT, at("cT", st, g, 1))
                    act.activation(cT[:, p, :], front[:, :], ACT.Copy).then_inc(s_cTe, 1)
                if k == 1:
                    act.wait_ge(s_xT, at("xT", st, g, 1))
                    act.activation((dense if st == CROSS else xT)[:, p, :], front[:, :], ACT.Copy).then_inc(s_xTe, 1)
                if k == 2 and st in (SELF, MASKX):
                    act.wait_ge(s_q, at("q", st, g, 1))
                    act.activation(dense[:, p, :], front[:, :], ACT.Copy).then_inc(s_qe, 1)
                if k == 2 and st == LINEAR:
                    act.wait_ge(s_q, at("q", st, g, 1))
                    act.wait_ge(s_ke, at("ke", st, g, 0))
                    features()
                if k == 3 and st in (SELF, MASKX):
                    act.wait_ge(s_spread, at("spread", st, g - 1, 0))
                    act.wait_ge(s_k, at("k", st, g, 1))
                    act.activation(src[:, p, :], front[:, :], ACT.Copy).then_inc(s_ke, 1)
                if k == 3 and st == LINEAR:
                    act.wait_ge(s_k, at("k", st, g, 1))
                    act.wait_ge(s_qe, at("qe", st, g, 1))
                    features()
                if k == 5 and st != CROSS:
                    act.wait_ge(s_v, at("v", st, g, 1))
                    act.activation(V[:, p, :, :, 0:HD], front[:, :].rearrange("p (b h d) -> p b h d", b=GB, d=HD), ACT.Copy).then_inc(s_ve, 1)

            def exponential(st, g, t):
                act.wait_ge(s_t, at("t", st, g, t + 1))
                act.activation(T[:, t % 4, :], T[:, t % 4, :], ACT.Exp, scale=1.0 if st == MASKX else SCALE).then_inc(s_e, 1)

            def copy_turned(st, g, t):
                act.wait_ge(s_pt, at("pt", st, g, t + 1))
                act.activation(PT[:, t % 2, :], turned[:, :], ACT.Copy).then_inc(s_pte, 1)

            def copy_out(st, g, b):
                act.wait_ge(s_pv, at("pv", st, g, 2 * b + 2))
                act.activation(OT[:, b % 2, :], back[:, :], ACT.Copy).then_inc(s_ot, 1)

            def slot(st, g, p, t, first, last, flush):
                if not last and not flush:
                    front_part(st, g + 1, 1 - p, t)
                if t == 4 and not first:
                    act.wait_ge(s_oT, at("oT", st, g - 1, 1))
                    act.activation(OdT[:, 1 - p, :], front[:, :], ACT.Copy).then_inc(s_oTe, 1)
                if st != LINEAR:
                    if t >= 2:
                        if not flush:
                            copy_turned(st, g, t - 2)
                    elif not first:
                        copy_turned(st, g - 1, t + UN - 2)
                if t % 2 == 0:
                    if t >= 4 and not flush:
                        copy_out(st, g, (t - 4) // 2)
                    elif t < 4 and not first:
                        copy_out(st, g - 1, (t + UN - 4) // 2)
                if st != LINEAR and not flush:
                    exponential(st, g, t)

            def attention(st):
                for k in range(6):
                    front_part(st, 0, 0, k)

                def body(g, p, first, last):
                    for t in range(UN):
                        slot(st, g, p, t, first, last, False)
                groups(act, body)
                for t in range(5):
                    slot(st, NG, NG % 2, t, False, True, True)

            def experts(st):
                def routing(g, p, k):
                    if k == 0:
                        act.wait_ge(s_xT, at("xT", st, g, 1))
                        act.activation(xT[:, p, :], front[:, :], ACT.Copy).then_inc(s_xTe, 1)
                    if k == 1:
                        n = GB * NE[st]
                        act.wait_ge(s_lg, at("lg", st, g, 1))
                        act.activation(lr[:, 0, 0:n], front[:, 0:n], ACT.Exp, scale=-1.0).then_inc(s_rexp, 1)
                    if k == 2:
                        act.wait_ge(s_combT, at("combT", st, g, 1))
                        act.activation(combT[:, p, :], front[:, :].bitcast(BF16)[:, 0:GT], ACT.Copy).then_inc(s_combTe, 1)

                for k in range(3):
                    routing(0, 0, k)
                ROUTE_AT = {1: 0, 3: 1, CHUNKS[st] - 1: 2}

                def body(g, p, first, last):
                    for c in range(CHUNKS[st]):
                        if c in ROUTE_AT and not last:
                            routing(g + 1, 1 - p, ROUTE_AT[c])
                        act.wait_ge(s_gate, at("gate", st, g, c + 1))
                        pg, pc = before(st, g, c)
                        act.wait_ge(s_gu, at("gu", st, pg, pc + 1))
                        act.activation(sg[:, c % 2, :], score[:, 0, (c % 2) * GT:(c % 2 + 1) * GT], ACT.Silu).then_inc(s_silu, 1)
                groups(act, body)

            def route():
                st = ROUTE

                def fill(g, p):
                    act.wait_ge(s_xn, at("xn", st, g, GB))
                    if not isinstance(g, int) or g >= 2:
                        act.wait_ge(s_sent[p], sent_before(g, p))
                    act.activation(pay[:, p, :, :, 0:D], xn[:, p, :, :].unsqueeze(2).broadcast_to([128, GB, KEEP2, D]), ACT.Copy).then_inc(s_pay, 1)
                    act.activation(pay[:, p, :, :, DEST], dest[:, bass.ds(g * GB, GB), :], ACT.Copy).then_inc(s_pay, 1)

                def copy_x(g, p):
                    act.wait_ge(s_xT, at("xT", st, g, 1))
                    act.activation(xT[:, p, :], front[:, :], ACT.Copy).then_inc(s_xTe, 1)

                copy_x(0, 0)
                fill(0, 0)

                def body(g, p, first, last):
                    n = GB * E2
                    act.wait_ge(s_route, at("route", st, g, 2))
                    act.activation(lr[:, 3, 0:n], lr[:, 2, 0:n], ACT.Exp).then_inc(s_rexp, 1)
                    if not last:
                        copy_x(g + 1, 1 - p)
                        fill(g + 1, 1 - p)
                groups(act, body)

            def routed_experts():
                def copy_hidden(t, p):
                    act.wait_ge(s_hT, t + 1)
                    act.activation(t_hT[:, p, :], turned[:, p * M2:(p + 1) * M2], ACT.Copy).then_inc(s_hTe, 1)

                def body(t, q, first, last):
                    p = q % 2
                    act.wait_ge(s_tg, t + 1)
                    if not isinstance(t, int) or t >= 2:
                        act.wait_ge(s_thid, t - 1)
                    act.activation(t_sg[:, p, :], score[:, 0, p * M2:(p + 1) * M2], ACT.Silu).then_inc(s_tsilu, 1)
                    if not first:
                        copy_hidden(t - 1, 1 - p)
                tiles(act, body)
                copy_hidden(TILES - 1, (TILES - 1) % 2)

            attention(SELF)
            attention(CROSS)
            experts(MOE)
            attention(LINEAR)
            attention(MASKX)
            route()
            routed_experts()

        @block.tensor
        def _(pe):
            pe.wait_ge(s_w0, 16 * 8)
            for n in range(3):
                if n:
                    pe.wait_ge(s_wTe, n)
                for k in range(3):
                    m = pe.transpose(front[:, k * D:(k + 1) * D], wraw[:, 3 * n + k, :], idf[:, :])
                m.then_inc(s_wT, 1)
            pe.wait_ge(s_wTe, 3)
            pe.wait_ge(s_zero, 3)
            pe.wait_ge(s_ones, 3)

            def transposed_x(st, g, p):
                pe.wait_ge(s_xn, at("xn", st, g, GB))
                for b in range(GB):
                    m = pe.transpose(front[:, b * S:(b + 1) * S], xn[:, p, b, :], idf[:, :])
                m.then_inc(s_xT, 1)

            def front_free(st, g):
                if st != CROSS:
                    pe.wait_ge(s_ve, at("ve", st, g, 0))
                else:
                    pe.wait_ge(s_xTe, at("xTe", st, g, 0))
                pe.wait_ge(s_xupd, at("xupd", st, g - 2, 0))

            def front_part(st, g, p, k, tail):
                own = st in (SELF, LINEAR)
                if k == 0:
                    front_free(st, g)
                    if st in (CROSS, MASKX):
                        pe.wait_ge(s_ctx, at("ctx", st, g, 16))
                        for b in range(GB):
                            m = pe.transpose(front[:, b * S:(b + 1) * S], crow[:, p, b, :], idf[:, :])
                        m.then_inc(s_cT, 1)
                if k == 1:
                    if st in (CROSS, MASKX):
                        pe.wait_ge(s_cTe, at("cTe", st, g, 1))
                    transposed_x(st, g, p)
                if k == 2 and st != CROSS:
                    pe.wait_ge(s_xTe, at("xTe", st, g, 1))
                    w = {SELF: wT[:, WQ, :], LINEAR: wT[:, LQ, :], MASKX: wm[:, MQ, :]}[st]
                    pe.matmul(front[:, :], w, xT[:, p, :], start=True, stop=True).then_inc(s_q, 1)
                if k == 3 and st != CROSS:
                    pe.wait_ge(s_qe, at("qe", st, g, 1))
                    w = {SELF: wT[:, WK, :], LINEAR: wT[:, LK, :], MASKX: wm[:, MK, :]}[st]
                    pe.matmul(front[:, :], w, (xT if own else cT)[:, p, :], start=True, stop=True).then_inc(s_k, 1)
                if k == 5 and st != CROSS:
                    pe.wait_ge(s_ke, at("ke", st, g, 1))
                    if tail:
                        pe.wait_ge(s_oTe, at("oTe", st, g - 2, 1))
                    w = {SELF: wT[:, WV, :], LINEAR: wT[:, LV, :], MASKX: wm[:, MV, :]}[st]
                    for b in range(GB):
                        m = pe.matmul(front[:, b * D:(b + 1) * D], (xT if own else cT)[:, p, b * S:(b + 1) * S], w, start=True, stop=True)
                    m.then_inc(s_v, 1)

            def scores(st, g, p, t):
                if t == 0:
                    pe.wait_ge(s_spread, at("spread", st, g, 256))
                    if st == CROSS:
                        pe.wait_ge(s_xTe, at("xTe", st, g, 1))
                    elif st == LINEAR:
                        pe.wait_ge(s_ke, at("ke", st, g, 1))
                    else:
                        pe.wait_ge(s_qe, at("qe", st, g, 1))
                if st == MASKX:
                    pe.wait_ge(s_sm, at("sm", st, g, t - 1))
                else:
                    pe.wait_ge(s_t, at("t", st, g, t - 1))
                b, u = t // 2, t % 2
                cols = slice(b * S, (b + 1) * S)
                for q in range(2):
                    h = UH * u + 4 * q
                    m = pe.matmul(score[:, t % 2, q * 512:(q + 1) * 512], dense[:, p, cols], spread[:, p, h:h + 4, cols], start=True, stop=True)
                m.then_inc(s_s, 1)

            def turn(st, g, t):
                pe.wait_ge(s_e, at("e", st, g, t + 1))
                pe.wait_ge(s_pte, at("pte", st, g, t))
                for h in range(UH):
                    m = pe.transpose(turned[:, h * S:(h + 1) * S], T[:, t % 4, h * S:(h + 1) * S], idf[:, :])
                m.then_inc(s_pt, 1)

            def weigh(st, g, p, t):
                b, u = t // 2, t % 2
                if st == LINEAR:
                    pe.wait_ge(s_t, at("t", st, g, t + 1))
                else:
                    pe.wait_ge(s_pte, at("pte", st, g, t + 1))
                if t == 0:
                    pe.wait_ge(s_ve, at("ve", st, g, 1))
                if u == 0:
                    pe.wait_ge(s_on, at("on", st, g, b))
                for i in range(UH):
                    h = UH * u + i
                    j, s = h % 4, h // 4
                    mov = T[:, t % 4, i * S:(i + 1) * S] if st == LINEAR else PT[:, t % 2, i * S:(i + 1) * S]
                    m = pe.matmul(back[32 * j:32 * j + HD + 1, s * S:(s + 1) * S], V[:, p, b, h, :], mov, start=True, stop=True)
                m.then_inc(s_pv, 1)

            def token_rows(st, g, b):
                pe.wait_ge(s_ot, at("ot", st, g, b + 1))
                for s in range(4):
                    m = pe.transpose(back[:, s * 128:(s + 1) * 128], OT[:, b % 2, s * S:(s + 1) * S], idf[:, :])
                m.then_inc(s_oq, 1)

            def out_rows(st, g, p, others):
                pe.wait_ge(s_on, at("on", st, g, GB))
                if others:
                    if st == CROSS:
                        pe.wait_ge(s_xTe, at("xTe", st, g + 2, 1))
                    else:
                        pe.wait_ge(s_ke, at("ke", st, g + 2, 1))
                pe.wait_ge(s_xupd, at("xupd", st, g, 0))
                for b in range(GB):
                    m = pe.transpose(front[:, b * S:(b + 1) * S], O[:, p, b, :], idf[:, :])
                m.then_inc(s_oT, 1)

            def project(st, g, p, others):
                pe.wait_ge(s_oTe, at("oTe", st, g, 1))
                if others and st != CROSS:
                    pe.wait_ge(s_ve, at("ve", st, g + 2, 1))
                w = {SELF: wT[:, WOUT, :], CROSS: wT[:, XWO, :], LINEAR: wT[:, LO, :], MASKX: wm[:, MO, :]}[st]
                for b in range(GB):
                    m = pe.matmul(front[:, b * D:(b + 1) * D], OdT[:, p, b * S:(b + 1) * S], w, start=True, stop=True)
                m.then_inc(s_y, 1)

            def slot(st, g, p, t, first, last, flush):
                if not flush:
                    scores(st, g, p, t)
                    if not last:
                        front_part(st, g + 1, 1 - p, t, not first)
                if t == 4 and not first:
                    out_rows(st, g - 1, 1 - p, not last)
                if t == 6 and not first:
                    project(st, g - 1, 1 - p, not last)
                if t % 2 == 1:
                    if t >= 5 and not flush:
                        token_rows(st, g, (t - 5) // 2)
                    elif t < 5 and not first:
                        token_rows(st, g - 1, (t + UN - 5) // 2)
                if st != LINEAR:
                    if t >= 2:
                        if not flush:
                            turn(st, g, t - 2)
                    elif not first:
                        turn(st, g - 1, t + UN - 2)
                if t >= 3:
                    if not flush:
                        weigh(st, g, p, t - 3)
                elif not first:
                    weigh(st, g - 1, 1 - p, t + UN - 3)

            def attention(st):
                if st > 0:
                    pe.wait_ge(s_xupd, at("xupd", st, 0, 0))
                if st == MASKX:
                    pe.wait_ge(s_w1, 16 * W1_LOADS)
                for k in range(6):
                    front_part(st, 0, 0, k, False)

                def body(g, p, first, last):
                    for t in range(UN):
                        slot(st, g, p, t, first, last, False)
                groups(pe, body)
                for t in range(7):
                    slot(st, NG, NG % 2, t, False, True, True)

            def experts(st):
                n = CHUNKS[st]

                def routing(g, p, k):
                    if k == 0:
                        pe.wait_ge(s_combTe, at("combTe", st, g, 0))
                        transposed_x(st, g, p)
                    if k == 1:
                        pe.wait_ge(s_xTe, at("xTe", st, g, 1))
                        for b in range(GB):
                            m = pe.matmul(front[:, b * NE[st]:(b + 1) * NE[st]], xT[:, p, b * S:(b + 1) * S], gw[st][:, :], start=True, stop=True)
                        m.then_inc(s_lg, 1)
                    if k == 2:
                        pe.wait_ge(s_comb, at("comb", st, g, 1))
                        for b in range(GB):
                            m = pe.transpose(front[:, :].bitcast(BF16)[:, b * S:(b + 1) * S], combp[:, b, :], idb[:, :])
                        m.then_inc(s_combT, 1)

                def chunk(g, p, c):
                    pg, pc = before(st, g, c)
                    cols = slice(c * 128, (c + 1) * 128)
                    pe.wait_ge(s_silu, at("silu", st, pg, pc + 1))
                    pe.matmul(score[:, 0, (c % 2) * GT:(c % 2 + 1) * GT], wg1[:, cols], xT[:, p, :], start=True, stop=True).then_inc(s_gate, 1)
                    pe.wait_ge(s_gu, at("gu", st, pg, pc + 1))
                    pe.matmul(score[:, 1, (c % 2) * GT:(c % 2 + 1) * GT], wu1[:, cols], xT[:, p, :], start=True, stop=True).then_inc(s_up, 1)
                    if c < C1:
                        if c == 0:
                            pe.wait_ge(s_combTe, at("combTe", st, g, 1))
                        pe.wait_ge(s_h, at("h", st, g, c - 1))
                        pe.matmul(turned[:, (c % 2) * GT:(c % 2 + 1) * GT], sel[:, c, :], combT[:, p, :], start=True, stop=True).then_inc(s_cw, 1)

                def down(g, c):
                    if c == C1:
                        pe.wait_ge(s_gu, at("gu", st, g, c + 1))
                        rows = gu
                    else:
                        pe.wait_ge(s_h, at("h", st, g, c + 1))
                        rows = hid
                    if c == 0:
                        pe.wait_ge(s_xupd, at("xupd", st, g, 0))
                    for b in range(GB):
                        m = pe.matmul(back[:, b * D:(b + 1) * D], rows[:, c % 2, b * S:(b + 1) * S], wd1[:, c, :],
                                      start=(c == 0 and b == 0), stop=(c == n - 1), skip_group_check=True)
                    m.then_inc(s_down, 1)

                pe.wait_ge(s_w1, 16 * W1_LOADS)
                pe.wait_ge(s_tab, 16 * 3)
                pe.wait_ge(s_xupd, at("xupd", st, 0, 0))
                for k in range(3):
                    routing(0, 0, k)
                ROUTE_AT = {1: 0, 3: 1, n - 1: 2}

                def body(g, p, first, last):
                    for c in range(n):
                        if c in ROUTE_AT and not last:
                            routing(g + 1, 1 - p, ROUTE_AT[c])
                        if c == 0 and not first:
                            down(g - 1, n - 1)
                        chunk(g, p, c)
                        if c >= 1:
                            down(g, c - 1)
                groups(pe, body)
                down(NG - 1, n - 1)

            def route():
                st = ROUTE

                def logits(g, p):
                    pe.wait_ge(s_xTe, at("xTe", st, g, 1))
                    for b in range(GB):
                        m = pe.matmul(back[:, b * E2:(b + 1) * E2], xT[:, p, b * S:(b + 1) * S], gw[st][:, :], start=True, stop=True)
                    m.then_inc(s_lg, 1)

                def places(g, p):
                    pe.wait_ge(s_chosen, at("chosen", st, g, 1))
                    ch = chosen[:, p, :].rearrange("p (b e) -> p b e", b=GB)
                    for b in range(GB + 1):
                        if b < GB:
                            m = pe.matmul(score[:, 0, b * E2:(b + 1) * E2], earlier[:, 0, :], ch[:, b, :], start=True, stop=(b == 0))
                        for a in range(b):
                            m = pe.matmul(score[:, 0, b * E2:(b + 1) * E2], earlier[:, 1, :], ch[:, a, :], start=(b == GB and a == 0), stop=(a == b - 1))
                    m.then_inc(s_place, 1)

                pe.wait_ge(s_xupd, at("xupd", st, 0, 0))
                transposed_x(st, 0, 0)

                def body(g, p, first, last):
                    logits(g, p)
                    if not last:
                        transposed_x(st, g + 1, 1 - p)
                    places(g, p)
                groups(pe, body)

            def routed_experts():
                def turn_rows(t, q):
                    pe.wait_ge(s_rows[q], landed(t, q) + 16)
                    if not isinstance(t, int) or t >= 1:
                        pe.wait_ge(s_rTe, t)
                    pe.transpose(front[:, 0:S], t_rows[:, q, 0:D], idf[:, :]).then_inc(s_rT, 1)

                def turn_hidden(t, p):
                    pe.wait_ge(s_thid, t + 1)
                    if not isinstance(t, int) or t >= 2:
                        pe.wait_ge(s_hTe, t - 1)
                    for c in range(M2 // 128):
                        m = pe.transpose(turned[:, p * M2 + c * 128:p * M2 + (c + 1) * 128], t_hid[:, p, c * 128:(c + 1) * 128], idf[:, :])
                    m.then_inc(s_hT, 1)

                def down(t, p, col):
                    pe.wait_ge(s_hTe, t + 1)
                    if not isinstance(t, int) or t >= 1:
                        pe.wait_ge(s_yw, 2 * t)
                    for c in range(M2 // 128):
                        m = pe.matmul(back[:, 0:D], t_hT[:, p, c * 128:(c + 1) * 128], wd2[:, bass.ds(col + c * D, D)],
                                      start=(c == 0), stop=(c == M2 // 128 - 1))
                    m.then_inc(s_ty, 1)

                def column(t):
                    return pe.value_load(table[0:1, bass.ds(TILES + t, 1)], min_val=0, max_val=(E2 - 1) * M2)

                pe.wait_ge(s_table, TABLE_STEPS)
                pe.wait_ge(s_w2, 16 * 3)
                turn_rows(0, 0)

                def body(t, q, first, last):
                    p = q % 2
                    col = column(t)
                    pe.wait_ge(s_rTe, t + 1)
                    if not isinstance(t, int) or t >= 2:
                        pe.wait_ge(s_tsilu, t - 1)
                    pe.matmul(score[:, 0, p * M2:(p + 1) * M2], xT[:, p, 0:S], wg2[:, bass.ds(col, M2)], start=True, stop=True).then_inc(s_tg, 1)
                    if not first:
                        turn_hidden(t - 1, 1 - p)
                    if not last:
                        turn_rows(t + 1, (q + 1) % QT)
                    if not isinstance(t, int) or t >= 2:
                        pe.wait_ge(s_thid, t - 1)
                    pe.matmul(score[:, 1, p * M2:(p + 1) * M2], xT[:, p, 0:S], wu2[:, bass.ds(col, M2)], start=True, stop=True).then_inc(s_tu, 1)
                    if not first:
                        down(t - 1, 1 - p, column(t - 1))
                tiles(pe, body)
                turn_hidden(TILES - 1, (TILES - 1) % 2)
                down(TILES - 1, (TILES - 1) % 2, column(TILES - 1))

            attention(SELF)
            attention(CROSS)
            experts(MOE)
            attention(LINEAR)
            attention(MASKX)
            route()
            routed_experts()

        @block.vector
        def _(dve):
            dve.memset(spread[:, 0, :, :], 0.0).then_inc(s_zero, 1)
            dve.memset(back[:, :], 0.0).then_inc(s_zero, 1)
            dve.wait_ge(s_x0, 16)
            dve.sem_inc(s_xupd, 1)

            def rows(g):
                return X[:, bass.ds(g * GB, GB), :]

            def statistics(st, g, p):
                if st > SELF:
                    dve.wait_ge(s_xupd, at("xupd", st - 1, g, 1))
                xg = rows(g)
                dve.wait_ge(s_aggr, at("aggr", st, g, 0))
                for b in range(GB):
                    dve.bn_stats(stats[:, b, :], xg[:, b, :]).then_inc(s_stat, 1)
                dve.wait_ge(s_stat, at("stat", st, g, GB))
                settle(dve, "dve")
                for b in range(GB):
                    dve.bn_aggr(mv[:, p, b, :], stats[:, b, :]).then_inc(s_aggr, 1)
                dve.wait_ge(s_aggr, at("aggr", st, g, GB))
                dve.wait_ge(s_rstd, at("rstd", st, g, 0))
                dve.tensor_scalar(veps[:, :], mv[:, p, :, 1], LN_EPS, None, ALU.add).then_inc(s_veps, 1)

            def normalise(st, g, p):
                dve.wait_ge(s_rstd, at("rstd", st, g, 1))
                xg = rows(g)
                for b in range(GB):
                    dve.tensor_scalar(xn[:, p, b, :], xg[:, b, :], mv[:, p, b, 0:1], rstd[:, p, b:b + 1], ALU.subtract, ALU.mult).then_inc(s_xn, 1)

            def front_part(st, g, p, k):
                if k == 0:
                    normalise(st, g, p)
                if k == 2 and st == LINEAR:
                    dve.wait_ge(s_spread, at("spread", st, g - 1, 0))
                    dve.wait_ge(s_phi, at("phi", st, g, 2))
                    dve.scalar_tensor_tensor(src[:, p, :], phi_e[:, :], 1.0, phi_r[:, :], ALU.min, ALU.add).then_inc(s_qe, 1)
                if k == 3 and st == LINEAR:
                    dve.wait_ge(s_phi, at("phi", st, g, 4))
                    dve.scalar_tensor_tensor(dense[:, p, :], phi_e[:, :], 1.0, phi_r[:, :], ALU.min, ALU.add).then_inc(s_ke, 1)

            def scores(st, g, t):
                dve.wait_ge(s_s, at("s", st, g, t + 1))
                sv = score[:, t % 2, :].rearrange("p (h k) -> p h k", h=UH)
                tv = T[:, t % 4, :].rearrange("p (h k) -> p h k", h=UH)
                nm = negm[:, t % 2, :]
                if st == LINEAR:
                    dve.tensor_tensor(tv, sv, cm[:, :].unsqueeze(1).broadcast_to([128, UH, S]), ALU.mult).then_inc(s_t, 1)
                elif st == MASKX:
                    dve.scalar_tensor_tensor(tv, sv, SCALE, mneg[:, :].unsqueeze(1).broadcast_to([128, UH, S]), ALU.mult, ALU.add).then_inc(s_sm, 1)
                    dve.wait_ge(s_sm, at("sm", st, g, t + 1))
                    dve.wait_ge(s_t, at("t", st, g, t - 1))
                    dve.tensor_reduce(nm, tv, AX.X, ALU.max, negate=True).then_inc(s_negm, 1)
                else:
                    dve.tensor_reduce(nm, sv, AX.X, ALU.max, negate=True).then_inc(s_negm, 1)
                    dve.wait_ge(s_negm, at("negm", st, g, t + 1))
                    dve.tensor_tensor(tv, sv, nm.unsqueeze(2).broadcast_to([128, UH, S]), ALU.add).then_inc(s_t, 1)

            def divide(st, g, p, b):
                dve.wait_ge(s_oq, at("oq", st, g, b + 1))
                ov = back[:, :].rearrange("p (h r) -> p h r", h=H)
                d = ov[:, :, HD]
                if st == LINEAR:
                    dve.tensor_scalar(den[:, :], d, DEN_EPS, None, ALU.add).then_inc(s_den, 1)
                    dve.wait_ge(s_den, at("den", st, g, b + 1))
                    d = den[:, :]
                dve.reciprocal(rden[:, :], d).then_inc(s_rden, 1)
                dve.wait_ge(s_rden, at("rden", st, g, b + 1))
                dve.tensor_tensor(O[:, p, b, :].rearrange("p (h d) -> p h d", d=HD), ov[:, :, 0:HD],
                                  rden[:, :].unsqueeze(2).broadcast_to([128, H, HD]), ALU.mult).then_inc(s_on, 1)

            def residual(st, g):
                xg = rows(g)
                if st == MASKX:
                    dve.tensor_tensor(xg, xg, bo[:, :].unsqueeze(1).broadcast_to([128, GB, D]), ALU.add).then_inc(s_bias, 1)
                    dve.wait_ge(s_bias, at("bias", st, g, 1))
                dve.wait_ge(s_y, at("y", st, g, 1))
                dve.tensor_tensor(xg, front[:, :].rearrange("p (b d) -> p b d", b=GB), xg, ALU.add).then_inc(s_xupd, 1)

            def slot(st, g, p, t, first, last, flush):
                if not flush:
                    if t == 0 and not last:
                        statistics(st, g + 1, 1 - p)
                    scores(st, g, t)
                    if not last:
                        front_part(st, g + 1, 1 - p, t)
                if t % 2 == 1:
                    if t >= 5 and not flush:
                        divide(st, g, p, (t - 5) // 2)
                    elif t < 5 and not first:
                        divide(st, g - 1, 1 - p, (t + UN - 5) // 2)
                if t == 6 and not first:
                    residual(st, g - 1)

            def attention(st):
                if st == MASKX:
                    dve.tensor_scalar(mneg[:, :], mneg[:, :], -1.0, 1.0, ALU.mult, ALU.add).then_inc(s_mneg, 1)
                    dve.wait_ge(s_mneg, 1)
                    dve.tensor_scalar(mneg[:, :], mneg[:, :], MASKED, None, ALU.mult).then_inc(s_mneg, 1)
                    dve.wait_ge(s_mneg, 2)
                statistics(st, 0, 0)
                for k in range(4):
                    front_part(st, 0, 0, k)
                if st == SELF:
                    dve.wait_ge(s_x1, 16)

                def body(g, p, first, last):
                    for t in range(UN):
                        slot(st, g, p, t, first, last, False)
                groups(dve, body)
                for t in range(7):
                    slot(st, NG, NG % 2, t, False, True, True)

            def ranks(st, g, k, val, m, out_i):
                keep = {4: 2, 16: 4, 8: 2}[m]
                v3 = val.rearrange("p (b e) -> p b e", b=GB)
                def step(g, k, ins):
                    ins.then_inc(s_route, 1)
                    dve.wait_ge(s_route, at("route", st, g, k))

                shape = [128, GB, m, m]
                a = wide[:, 0:GB * m * m]
                bq = wide[:, 1024:1024 + GB * m * m]
                comp = v3.unsqueeze(2).broadcast_to(shape)
                cand = v3.unsqueeze(3).broadcast_to(shape)
                av = a.rearrange("p (b j i) -> p b j i", b=GB, j=m)
                bv = bq.rearrange("p (b j i) -> p b j i", b=GB, j=m)
                left = tr[:, 0:m, 0:m].unsqueeze(1).broadcast_to(shape)
                dve.tensor_tensor(av, comp, cand, ALU.is_equal).then_inc(s_route, 1)
                step(g, k + 2, dve.tensor_tensor(bv, comp, cand, ALU.is_gt))
                step(g, k + 3, dve.tensor_tensor(av, av, left, ALU.mult))
                step(g, k + 4, dve.tensor_tensor(a, a, bq, ALU.add))
                step(g, k + 5, dve.tensor_reduce(lr[:, out_i, 0:GB * m], a.rearrange("p (c i) -> p c i", i=m), AX.X, ALU.add))
                step(g, k + 6, dve.tensor_scalar(lr[:, out_i, 0:GB * m], lr[:, out_i, 0:GB * m], float(keep), None, ALU.is_lt))

            def experts(st):
                n, ne = CHUNKS[st], NE[st]
                w = GB * ne

                def step(g, k, ins):
                    ins.then_inc(s_route, 1)
                    dve.wait_ge(s_route, at("route", st, g, k))

                def small(i, width=w):
                    return lr[:, i, 0:width]

                def by_row(a, m=ne):
                    return a.rearrange("p (b e) -> p b e", b=GB)

                def parts(g, k, c):
                    c3 = by_row(c)
                    r = by_row(small(12))
                    step(g, k + 1, dve.tensor_copy(combp[:, :, 0:ne], c3))
                    step(g, k + 2, dve.tensor_tensor(r, c3, combp[:, :, 0:ne], ALU.subtract))
                    step(g, k + 3, dve.tensor_copy(combp[:, :, 16:16 + ne], r))
                    step(g, k + 4, dve.tensor_tensor(r, r, combp[:, :, 16:16 + ne], ALU.subtract))
                    dve.tensor_copy(combp[:, :, 32:32 + ne], r).then_inc(s_comb, 1)

                def route_moe(g, k):
                    if k == 0:
                        dve.wait_ge(s_rexp, at("rexp", st, g, 1))
                        step(g, 1, dve.tensor_scalar(small(1), small(0), 1.0, None, ALU.add))
                        step(g, 2, dve.reciprocal(small(2), small(1)))
                        step(g, 3, dve.tensor_tensor(by_row(small(3)), by_row(small(2)), bias_r[:, :].unsqueeze(1).broadcast_to([128, GB, E1]), ALU.add))
                        a = small(3).rearrange("p (c i) -> p c i", i=4)
                        pr = wide[:, 0:6 * 16].rearrange("p (c i) -> p c i", i=6)
                        dve.tensor_tensor(pr[:, :, 0:3], a[:, :, 0:3], a[:, :, 1:4], ALU.add).then_inc(s_route, 1)
                        dve.tensor_tensor(pr[:, :, 3:5], a[:, :, 0:2], a[:, :, 2:4], ALU.add).then_inc(s_route, 1)
                        step(g, 6, dve.tensor_tensor(pr[:, :, 5:6], a[:, :, 0:1], a[:, :, 3:4], ALU.add))
                        step(g, 7, dve.tensor_reduce(lr[:, 4, 0:16], pr, AX.X, ALU.max))
                    if k == 1:
                        ranks(st, g, 7, lr[:, 4, 0:16], 4, 5)
                        step(g, 14, dve.tensor_tensor(small(6).rearrange("p (c i) -> p c i", i=4), small(3).rearrange("p (c i) -> p c i", i=4),
                                                      lr[:, 5, 0:16].unsqueeze(2).broadcast_to([128, 16, 4]), ALU.mult))
                    if k == 2:
                        ranks(st, g, 14, small(6), 16, 7)
                    if k == 3:
                        step(g, 21, dve.tensor_tensor(small(8), small(6), small(7), ALU.mult))
                        weights(g, 21, 2.5, 1e-20)

                def weights(g, k, scale, eps):
                    dve.tensor_reduce(lr[:, 9, 0:GB], by_row(small(8)), AX.X, ALU.add).then_inc(s_wsum, 1)
                    dve.wait_ge(s_wsum, at("wsum", st, g, 1))
                    dve.tensor_scalar(lr[:, 10, 0:GB], lr[:, 9, 0:GB], eps, None, ALU.add).then_inc(s_wsum, 1)
                    dve.wait_ge(s_wsum, at("wsum", st, g, 2))
                    dve.reciprocal(lr[:, 11, 0:GB], lr[:, 10, 0:GB]).then_inc(s_wsum, 1)
                    dve.wait_ge(s_wsum, at("wsum", st, g, 3))
                    dve.tensor_tensor(by_row(small(13)), by_row(small(8)), lr[:, 11, 0:GB].unsqueeze(2).broadcast_to([128, GB, ne]), ALU.mult).then_inc(s_wsum, 1)
                    dve.wait_ge(s_wsum, at("wsum", st, g, 4))
                    dve.tensor_scalar(small(8), small(13), scale, None, ALU.mult).then_inc(s_wsum, 1)
                    dve.wait_ge(s_wsum, at("wsum", st, g, 5))
                    parts(g, k, small(8))

                def routing(g, p, k):
                    if k == 0:
                        statistics(st, g, p)
                        normalise(st, g, p)
                    else:
                        route_moe(g, k - 1)

                dve.wait_ge(s_w1, 16 * W1_LOADS)
                dve.wait_ge(s_ones, 3)
                for k in range(5):
                    routing(0, 0, k)
                ROUTE_AT = {0: 0, 3: 1, 4: 2, 5: 3, 6: 4}

                def chunk(g, c):
                    b = c % 2
                    dve.wait_ge(s_up, at("up", st, g, c + 1))
                    dve.wait_ge(s_silu, at("silu", st, g, c + 1))
                    dve.tensor_tensor(gu[:, b, :], score[:, 1, b * GT:(b + 1) * GT], sg[:, b, :], ALU.mult).then_inc(s_gu, 1)
                    if c < C1:
                        dve.wait_ge(s_cw, at("cw", st, g, c + 1))
                        dve.wait_ge(s_gu, at("gu", st, g, c + 1))
                        dve.tensor_tensor(hid[:, b, :], turned[:, b * GT:(b + 1) * GT], gu[:, b, :], ALU.mult).then_inc(s_h, 1)

                def body(g, p, first, last):
                    for c in range(n):
                        chunk(g, c)
                        if c in ROUTE_AT and not last:
                            routing(g + 1, 1 - p, ROUTE_AT[c])
                        if c == 0 and not first:
                            added(g - 1)

                def added(g):
                    xg = rows(g)
                    dve.wait_ge(s_down, at("down", st, g, n))
                    dve.tensor_tensor(xg, back[:, :].rearrange("p (b d) -> p b d", b=GB), xg, ALU.add).then_inc(s_xupd, 1)
                groups(dve, body)
                added(NG - 1)

            def route():
                st = ROUTE
                w = GB * E2
                dve.wait_ge(s_w1, 16 * W1_LOADS)
                statistics(st, 0, 0)
                normalise(st, 0, 0)

                def step(g, k, ins):
                    ins.then_inc(s_route, 1)
                    dve.wait_ge(s_route, at("route", st, g, k))

                def small(i):
                    return lr[:, i, 0:w]

                def by_row(a):
                    return a.rearrange("p (b e) -> p b e", b=GB)

                def body(g, p, first, last):
                    if not last:
                        statistics(st, g + 1, 1 - p)
                    dve.wait_ge(s_lg, at("lg", st, g, 1))
                    dve.tensor_copy(small(0), back[:, 0:w]).then_inc(s_lge, 1)
                    dve.wait_ge(s_lge, at("lge", st, g, 1))
                    step(g, 1, dve.tensor_reduce(lr[:, 1, 0:GB], by_row(small(0)), AX.X, ALU.max))
                    step(g, 2, dve.tensor_tensor(by_row(small(2)), by_row(small(0)), lr[:, 1, 0:GB].unsqueeze(2).broadcast_to([128, GB, E2]), ALU.subtract))
                    ranks(st, g, 2, small(0), E2, 7)
                    dve.tensor_copy(chosen[:, p, :], small(7)).then_inc(s_chosen, 1)
                    if not last:
                        normalise(st, g + 1, 1 - p)
                    dve.wait_ge(s_rexp, at("rexp", st, g, 1))
                    step(g, 9, dve.tensor_tensor(small(8), small(3), small(7), ALU.mult))
                    dve.tensor_reduce(lr[:, 9, 0:GB], by_row(small(8)), AX.X, ALU.add).then_inc(s_wsum, 1)
                    dve.wait_ge(s_wsum, at("wsum", st, g, 1))
                    dve.reciprocal(lr[:, 10, 0:GB], lr[:, 9, 0:GB]).then_inc(s_wsum, 1)
                    dve.wait_ge(s_wsum, at("wsum", st, g, 2))
                    dve.tensor_tensor(by_row(small(13)), by_row(small(8)), lr[:, 10, 0:GB].unsqueeze(2).broadcast_to([128, GB, E2]), ALU.mult).then_inc(s_wsum, 1)
                    dve.wait_ge(s_wsum, at("wsum", st, g, 3))
                    dve.wait_ge(s_place, at("place", st, g, 1))
                    step(g, 10, dve.tensor_tensor(by_row(small(4)), by_row(score[:, 0, 0:w]), base[:, :].unsqueeze(1).broadcast_to([128, GB, E2]), ALU.add))
                    step(g, 11, dve.tensor_tensor(base[:, :], score[:, 0, w:w + E2], base[:, :], ALU.add))
                    step(g, 12, dve.tensor_tensor(small(5), small(4), small(7), ALU.mult))
                    step(g, 13, dve.tensor_reduce(indexf[:, :, 1], by_row(small(5)), AX.X, ALU.max))
                    step(g, 14, dve.scalar_tensor_tensor(small(6), small(7), -FAR, small(4), ALU.mult, ALU.add))
                    step(g, 15, dve.tensor_reduce(lr[:, 11, 0:GB], by_row(small(6)), AX.X, ALU.min))
                    step(g, 16, dve.tensor_scalar(indexf[:, :, 0], lr[:, 11, 0:GB], FAR, None, ALU.add))
                    both = wide[:, 0:KEEP2 * w].rearrange("p (b c e) -> p b c e", b=GB, c=KEEP2)
                    shape = [128, GB, KEEP2, E2]
                    step(g, 17, dve.tensor_tensor(both, by_row(small(5)).unsqueeze(2).broadcast_to(shape), indexf[:, :, :].unsqueeze(3).broadcast_to(shape), ALU.is_equal))
                    step(g, 18, dve.tensor_tensor(both, both, by_row(small(13)).unsqueeze(2).broadcast_to(shape), ALU.mult))
                    if not isinstance(g, int) or g >= 2:
                        dve.wait_ge(s_sent[p], sent_before(g, p))
                    dve.tensor_reduce(pay[:, p, :, :, WEIGHT], both, AX.X, ALU.add).then_inc(s_payw, 1)
                    dve.tensor_copy(index[:, p, :, :], indexf[:, :, :]).then_inc(s_index, 1)
                groups(dve, body)

            def tabulate():
                def step(k, ins):
                    ins.then_inc(s_table, 1)
                    dve.wait_ge(s_table, k)

                ends = base[0:1, :]
                big = wide[0:1, 0:TILES * E2]
                tokens, full, cover, end = (tl[:, i, 0:E2] for i in range(4))
                expert, skipped, row, col = (tl[:, i, :] for i in range(4, 8))
                step(1, dve.tensor_tensor(tokens, ends, start_r[0:1, :], ALU.subtract))
                over = wide[0:1, 0:E2 * 32].rearrange("p (e k) -> p e k", e=E2)
                step(2, dve.tensor_tensor(over, tokens.unsqueeze(2).broadcast_to([1, E2, 32]), step_r[0:1, 0:32].unsqueeze(1).broadcast_to([1, E2, 32]), ALU.is_gt))
                step(3, dve.tensor_reduce(full, over, AX.X, ALU.add))
                square = wide[0:1, 0:E2 * E2].rearrange("p (e k) -> p e k", e=E2)
                step(4, dve.tensor_tensor(square, tr[0:1, 0:E2, 0:E2], full.unsqueeze(1).broadcast_to([1, E2, E2]), ALU.mult))
                step(5, dve.tensor_reduce(cover, square, AX.X, ALU.add))
                step(6, dve.tensor_tensor(end, cover, full, ALU.add))
                step(7, dve.tensor_scalar(end, end, float(S), None, ALU.mult))
                past = big.rearrange("p (t e) -> p t e", e=E2)
                shape = [1, TILES, E2]
                nth = step_r[0:1, 32:32 + TILES]
                step(8, dve.tensor_tensor(past, nth.unsqueeze(2).broadcast_to(shape), end.unsqueeze(1).broadcast_to(shape), ALU.is_ge))
                step(9, dve.tensor_reduce(expert, past, AX.X, ALU.add))
                step(10, dve.tensor_tensor(past, past, full.unsqueeze(1).broadcast_to(shape), ALU.mult))
                step(11, dve.tensor_reduce(skipped, past, AX.X, ALU.add))
                step(12, dve.scalar_tensor_tensor(row, skipped, -float(S), nth, ALU.mult, ALU.add))
                step(13, dve.scalar_tensor_tensor(row, expert, float(REGION), row, ALU.mult, ALU.add))
                step(14, dve.tensor_scalar(col, expert, float(E2 - 1), float(M2), ALU.min, ALU.mult))
                dve.tensor_copy(table[:, 0:TILES], row).then_inc(s_table, 1)
                dve.tensor_copy(table[:, TILES:2 * TILES], col).then_inc(s_table, 1)
                dve.tensor_copy(table[:, 2 * TILES:], ends).then_inc(s_table, 1)

            def routed_experts():
                def copy_rows(t, p):
                    dve.wait_ge(s_rT, t + 1)
                    dve.tensor_copy(xT[:, p, 0:S], front[:, 0:S]).then_inc(s_rTe, 1)

                def weighted(t, q):
                    dve.wait_ge(s_ty, t + 1)
                    if not isinstance(t, int) or t >= QT:
                        dve.wait_ge(s_ysent[q], landed(t, q))
                    dve.tensor_scalar(t_y[:, q, :], back[:, 0:D], t_rows[:, q, WEIGHT:WEIGHT + 1], None, ALU.mult).then_inc(s_yw, 1)
                    dve.tensor_copy(yindex[:, q:q + 1], t_rows[:, q, DEST:DEST + 1]).then_inc(s_yw, 1)

                copy_rows(0, 0)

                def body(t, q, first, last):
                    p = q % 2
                    if not last:
                        if not isinstance(t, int) or t >= 1:
                            dve.wait_ge(s_tu, t)
                        copy_rows(t + 1, 1 - p)
                    dve.wait_ge(s_tsilu, t + 1)
                    dve.wait_ge(s_tu, t + 1)
                    if not isinstance(t, int) or t >= 2:
                        dve.wait_ge(s_hT, t - 1)
                    dve.tensor_tensor(t_hid[:, p, :], score[:, 1, p * M2:(p + 1) * M2], t_sg[:, p, :], ALU.mult).then_inc(s_thid, 1)
                    if not first:
                        weighted(t - 1, (q - 1) % QT)
                tiles(dve, body)
                weighted(TILES - 1, (TILES - 1) % QT)

            def add():
                def body(g, p, first, last):
                    xg = rows(g)
                    dve.wait_ge(s_back, at("back", ADD, g, 32))
                    dve.tensor_tensor(xg, y_first[:, p, :, :], xg, ALU.add).then_inc(s_half, 1)
                    dve.wait_ge(s_half, at("half", ADD, g, 1))
                    dve.tensor_tensor(xg, y_second[:, p, :, :], xg, ALU.add).then_inc(s_xupd, 1)
                groups(dve, body)

            attention(SELF)
            attention(CROSS)
            experts(MOE)
            attention(LINEAR)
            attention(MASKX)
            route()
            tabulate()
            routed_experts()
            add()


_INS = ["x", "ctx_1024", "mask_1x1xSxS2_fk0", "L0_attn_w_qkv", "L0_attn_w_out", "L0_xattn_Wo",
        "L0_ffn_gate_kernel", "L0_ffn_gate_bias", "L0_ffn_w_gate", "L0_ffn_w_up", "L0_ffn_w_down",
        "L0_ffn_sw_gate", "L0_ffn_sw_up", "L0_ffn_sw_down", "L1_attn_Wq", "L1_attn_Wk",
        "L1_attn_Wv", "L1_attn_Wo", "L1_xattn_Wq", "L1_xattn_Wk", "L1_xattn_Wv", "L1_xattn_Wo",
        "L1_xattn_bo", "L1_ffn_gate", "L1_ffn_experts_w1", "L1_ffn_experts_w2", "L1_ffn_experts_w3"]


def constants():
    k = np.arange(128)
    col = np.arange(128)
    sel1 = np.stack([(k[:, None] < 48) & (k[:, None] % 16 == 2 * c + (col[None, :] >= M1)) for c in range(C1)], 1)
    padding = np.zeros((2 * E2 * S, ROW), np.float32)
    padding[:, DEST] = KEEP2 * TOKENS + np.arange(2 * E2 * S)
    dests = k[:, None, None] + S * np.arange(B)[None, :, None] + TOKENS * np.arange(KEEP2)[None, None, :]
    return {
        "ident": np.eye(128, dtype=np.float32),
        "causal": (k[:, None] <= k[None, :]).astype(np.float32),
        "tri": (np.arange(16)[None, :] < np.arange(16)[:, None]).astype(np.float32),
        "sel1": sel1.astype(np.float32),
        "before": np.stack([k[:, None] < col[None, :], np.ones((128, 128), bool)], 1).astype(np.float32),
        "starts": (REGION * np.arange(E2)).astype(np.float32),
        "steps": (S * np.concatenate([np.arange(32), np.arange(TILES)])).astype(np.float32),
        "dests": dests.astype(np.float32),
        "padding": padding,
    }


def kernel(**inputs):
    import concourse.bacc as _bacc
    from concourse.bass_utils import run_bass_kernel_spmd as _run

    nc = _bacc.Bacc("TRN2", target_bir_lowering=False, num_devices=1)
    arrays, args = {}, []
    for name, a in [(n, inputs[n]) for n in _INS] + list(constants().items()):
        a = np.ascontiguousarray(a)
        arrays[f"in_{name}"] = a
        args.append(nc.dram_tensor(f"in_{name}", a.shape, mybir.dt.from_np(a.dtype), kind="ExternalInput").ap())
    args.append(nc.dram_tensor("out_0", (B, S, D), F32, kind="ExternalOutput").ap())
    decoder(nc, *args)
    r = _run(nc, [arrays], core_ids=[0])
    return r.results[0]["out_0"]
```

```python
from contextlib import ExitStack

import numpy as np

import concourse.bass as bass
from concourse import mybir

F32 = mybir.dt.float32
BF16 = mybir.dt.bfloat16
I32 = mybir.dt.int32
ALU = mybir.AluOpType
ACT = mybir.ActivationFunctionType
AX = mybir.AxisListType

B, S, D = 32, 128, 128
H, HD = 16, 8
GB = 4
NG = B // GB
GT = GB * S
UH = 8
UN = GB * H // UH
UW = UH * S
SCALE = float(1.0 / np.sqrt(np.float32(HD)))
MASKED = -1e9
SLOTS = 6
STACK = SLOTS * HD
ONE_SIDE = (0, 0, 1, 1, 2, 0)
OTHER_SIDE = (0, 1, 0, 1, 0, 2)
EARLY = 4
PAIRS = H // 2
LN_EPS = 1e-5
DEN_EPS = 1e-8
E1, M1 = 16, 64
E2, M2 = 8, 512
C1 = E1 * M1 // 128
KEEP2 = 2
TOKENS = B * S
ROW = D + 2
DEST, WEIGHT = D, D + 1
REGION = TOKENS + S
TILES = TOKENS * KEEP2 // S + E2
GROUP_SENT = 16 * GB * KEEP2
QT = 4
TABLE_STEPS = 16
SUMS = 4
SB = B // SUMS
FAR = 65536.0

W1_LOADS = 21

SELF, CROSS, MOE, LINEAR, MASKX, ROUTE, ADD = range(7)
CHUNKS = {MOE: C1 + 1}
ATTN = (SELF, CROSS, LINEAR, MASKX)
UE = {SELF: UH, CROSS: UH, MASKX: 6}

STARTS = {"xupd": 1}

PARTS_AT = {
    SELF:   {7: (2, (0, 1)), 0: (1, (2,)), 1: (1, (3,)), 5: (1, (5,))},
    CROSS:  {0: (1, (0,)), 1: (1, (1,))},
    LINEAR: {7: (2, (0, 1, 2)), 0: (1, (3,)), 1: (1, (4,)), 5: (1, (5,))},
    MASKX:  {7: (2, (0, 1)), 0: (1, (2,)), 1: (1, (3,)), 5: (1, (5,))},
}
TWO_AHEAD = (SELF, LINEAR, MASKX)

PER_GROUP = {
    "xupd":   (1, 1, 1, 1, 1, 0, 0),
    "stat":   (4, 4, 4, 4, 4, 4, 0),
    "aggr":   (4, 4, 4, 4, 4, 4, 0),
    "veps":   (1, 1, 1, 1, 1, 1, 0),
    "rstd":   (1, 1, 1, 1, 1, 1, 0),
    "xn":     (4, 4, 4, 4, 4, 4, 0),
    "xT":     (1, 1, 1, 1, 1, 1, 0),
    "xTe":    (1, 0, 1, 1, 1, 1, 0),
    "ctx":    (0, 16, 0, 0, 16, 0, 0),
    "cT":     (0, 1, 0, 0, 1, 0, 0),
    "cTe":    (0, 0, 0, 0, 1, 0, 0),
    "q":      (1, 0, 0, 1, 1, 0, 0),
    "qe":     (1, 1, 0, 1, 1, 0, 0),
    "qf":     (0, 0, 0, 1, 0, 0, 0),
    "qr":     (1, 1, 0, 1, 1, 0, 0),
    "qp":     (2, 2, 0, 2, 2, 0, 0),
    "qst":    (64, 64, 0, 64, 64, 0, 0),
    "qsl":    (32, 32, 0, 32, 32, 0, 0),
    "k":      (1, 0, 0, 1, 1, 0, 0),
    "ke":     (1, 1, 0, 1, 1, 0, 0),
    "kf":     (0, 0, 0, 1, 0, 0, 0),
    "kr":     (1, 1, 0, 1, 1, 0, 0),
    "kp":     (2, 2, 0, 2, 2, 0, 0),
    "kst":    (64, 64, 0, 64, 64, 0, 0),
    "ksl":    (32, 32, 0, 32, 32, 0, 0),
    "phi":    (0, 0, 0, 4, 0, 0, 0),
    "v":      (1, 0, 0, 1, 1, 0, 0),
    "ve":     (1, 1, 0, 1, 1, 0, 0),
    "spread": (128, 128, 0, 128, 128, 0, 0),
    "s":      (UN, UN, 0, UN, UN, 0, 0),
    "sm":     (0, 0, 0, 0, UN, 0, 0),
    "negm":   (UN, UN, 0, 0, UN, 0, 0),
    "t":      (UN, UN, 0, UN, UN, 0, 0),
    "eb":     (0, 0, 0, 0, UN, 0, 0),
    "e":      (UN, UN, 0, 0, UN, 0, 0),
    "pt":     (UN, UN, 0, 0, UN, 0, 0),
    "pte":    (UN, UN, 0, 0, UN, 0, 0),
    "pv":     (UN, UN, 0, UN, UN, 0, 0),
    "ot":     (GB, GB, 0, GB, GB, 0, 0),
    "oq":     (GB, GB, 0, GB, GB, 0, 0),
    "den":    (0, 0, 0, GB, 0, 0, 0),
    "rden":   (GB, GB, 0, GB, GB, 0, 0),
    "on":     (GB, GB, 0, GB, GB, 0, 0),
    "oT":     (1, 1, 0, 1, 1, 0, 0),
    "oTe":    (1, 1, 0, 1, 1, 0, 0),
    "y":      (1, 1, 0, 1, 1, 0, 0),
    "bias":   (0, 0, 0, 0, 1, 0, 0),
    "lg":     (0, 0, 1, 0, 0, 1, 0),
    "lge":    (0, 0, 0, 0, 0, 1, 0),
    "route":  (0, 0, 23, 0, 0, 18, 0),
    "before": (0, 0, 2, 0, 0, 0, 0),
    "rexp":   (0, 0, 1, 0, 0, 1, 0),
    "comb":   (0, 0, 1, 0, 0, 0, 0),
    "combT":  (0, 0, 1, 0, 0, 0, 0),
    "combTe": (0, 0, 1, 0, 0, 0, 0),
    "pay":    (0, 0, 0, 0, 0, 2, 0),
    "payw":   (0, 0, 0, 0, 0, 1, 0),
    "chosen": (0, 0, 0, 0, 0, 1, 0),
    "place":  (0, 0, 0, 0, 0, 1, 0),
    "index":  (0, 0, 0, 0, 0, 1, 0),
    "gate":   (0, 0, C1 + 1, 0, 0, 0, 0),
    "up":     (0, 0, C1 + 1, 0, 0, 0, 0),
    "cw":     (0, 0, C1, 0, 0, 0, 0),
    "silu":   (0, 0, C1 + 1, 0, 0, 0, 0),
    "gu":     (0, 0, C1 + 1, 0, 0, 0, 0),
    "h":      (0, 0, C1, 0, 0, 0, 0),
    "wsum":   (0, 0, 5, 0, 0, 3, 0),
    "down":   (0, 0, C1 + 1, 0, 0, 0, 0),
}


def decoder(nc, x, ctx, mask, w_qkv, w_out, x0_wo, gate1, bias1, w_gate1, w_up1, w_down1, s_gate1,
            s_up1, s_down1, l_wq, l_wk, l_wv, l_wo, m_wq, m_wk, m_wv, m_wo, m_bo, gate2, e_w1, e_w2,
            e_w3, ident, causal, tri, sel1, before_t, starts, steps, dests, padding, out):
    with ExitStack() as stack:
        def sb(name, shape, dt=F32):
            return stack.enter_context(nc.sbuf_tensor(name, shape, dt))

        def ps(name, shape, dt=F32):
            return stack.enter_context(nc.psum_tensor(name, shape, dt))

        def semaphore(name):
            return stack.enter_context(nc.semaphore("s_" + name))

        s_xupd = semaphore("xupd")
        s_stat = semaphore("stat")
        s_aggr = semaphore("aggr")
        s_veps = semaphore("veps")
        s_rstd = semaphore("rstd")
        s_xn = semaphore("xn")
        s_xT = semaphore("xT")
        s_xTe = semaphore("xTe")
        s_ctx = semaphore("ctx")
        s_cT = semaphore("cT")
        s_cTe = semaphore("cTe")
        s_q = semaphore("q")
        s_qe = semaphore("qe")
        s_qf = semaphore("qf")
        s_qr = semaphore("qr")
        s_qp = semaphore("qp")
        s_qst = semaphore("qst")
        s_qsl = semaphore("qsl")
        s_k = semaphore("k")
        s_ke = semaphore("ke")
        s_kf = semaphore("kf")
        s_kr = semaphore("kr")
        s_kp = semaphore("kp")
        s_kst = semaphore("kst")
        s_ksl = semaphore("ksl")
        s_phi = semaphore("phi")
        s_v = semaphore("v")
        s_ve = semaphore("ve")
        s_spread = semaphore("spread")
        s_s = semaphore("s")
        s_sm = semaphore("sm")
        s_negm = semaphore("negm")
        s_t = semaphore("t")
        s_eb = semaphore("eb")
        s_e = semaphore("e")
        s_pt = semaphore("pt")
        s_pte = semaphore("pte")
        s_pv = semaphore("pv")
        s_ot = semaphore("ot")
        s_oq = semaphore("oq")
        s_den = semaphore("den")
        s_rden = semaphore("rden")
        s_on = semaphore("on")
        s_oT = semaphore("oT")
        s_oTe = semaphore("oTe")
        s_y = semaphore("y")
        s_bias = semaphore("bias")
        s_lg = semaphore("lg")
        s_lge = semaphore("lge")
        s_route = semaphore("route")
        s_before = semaphore("before")
        s_rexp = semaphore("rexp")
        s_comb = semaphore("comb")
        s_combT = semaphore("combT")
        s_combTe = semaphore("combTe")
        s_gate = semaphore("gate")
        s_up = semaphore("up")
        s_cw = semaphore("cw")
        s_silu = semaphore("silu")
        s_gu = semaphore("gu")
        s_h = semaphore("h")
        s_down = semaphore("down")
        s_wsum = semaphore("wsum")

        s_pay = semaphore("pay")
        s_payw = semaphore("payw")
        s_chosen = semaphore("chosen")
        s_place = semaphore("place")
        s_index = semaphore("index")
        s_sent = [semaphore("sent_even"), semaphore("sent_odd")]

        s_back = [semaphore("back%d" % c) for c in range(SUMS)]
        s_half = semaphore("half")
        s_sum = semaphore("sum")

        s_table = semaphore("table")
        s_padodd = semaphore("padodd")
        s_ends = semaphore("ends")
        s_pad = semaphore("pad")
        s_rows = [semaphore("rows%d" % q) for q in range(QT)]
        s_rT = semaphore("rT")
        s_rTe = semaphore("rTe")
        s_tg = semaphore("tg")
        s_tu = semaphore("tu")
        s_tsilu = semaphore("tsilu")
        s_thid = semaphore("thid")
        s_hT = semaphore("hT")
        s_hTe = semaphore("hTe")
        s_ty = semaphore("ty")
        s_yw = semaphore("yw")
        s_ysent = [semaphore("ysent%d" % q) for q in range(QT)]

        def at(name, st, g, k):
            rate = PER_GROUP[name]
            value = STARTS.get(name, 0) + NG * sum(rate[:st]) + rate[st] * g + k
            return max(value, 0) if isinstance(value, int) else value

        s_passed = {n: semaphore("passed_" + n) for n in ("sp", "pool", "dve")}

        def settle(eng, name):
            eng.sem_inc(s_passed[name], 1)

        s_x0 = semaphore("x0")
        s_x1 = semaphore("x1")
        s_w0 = semaphore("w0")
        s_tab = semaphore("tab")
        s_w1 = semaphore("w1")
        s_w2 = semaphore("w2")
        s_out = semaphore("out")
        s_wT = semaphore("wT")
        s_wTe = semaphore("wTe")
        s_zero = semaphore("zero")
        s_ones = semaphore("ones")
        s_mneg = semaphore("mneg")

        score = ps("score", [128, 2, UW])
        turned = ps("turned", [128, UW])
        front = ps("front", [128, GT])
        back = ps("back", [128, GT])

        X = sb("X", [128, B, D])
        WE = E2 * M2
        heavy = sb("heavy", [128, 3 * WE])
        spread = heavy[:, 0:2 * WE].bitcast(BF16).rearrange("p (r a i t) -> p r a i t", r=2, a=PAIRS, i=2)
        stacked = heavy[:, 2 * WE:3 * WE].bitcast(BF16).rearrange("p (r a t) -> p r a t", r=2, a=PAIRS)
        parts = sb("parts", [128, 2, 3, GT], BF16)
        rest = sb("rest", [128, 2, GT])
        crow = sb("crow", [128, 2, GB, D])
        cT = sb("cT", [128, 2, GT])
        dense = sb("dense", [128, 2, GT])
        src = sb("src", [128, 2, GT])
        phi_e = sb("phi_e", [128, GT])
        phi_r = sb("phi_r", [128, GT])
        V = sb("V", [128, 2, GB, H, HD + 1])
        xn = sb("xn", [128, 2, GB, D])
        xT = sb("xT", [128, 2, GT])
        work = sb("work", [128, 9 * UW])
        T = work[:, 0:4 * UW].rearrange("p (r c) -> p r c", r=4)
        PT = work[:, 4 * UW:6 * UW].rearrange("p (r c) -> p r c", r=2)
        OT = work[:, 6 * UW:7 * UW].rearrange("p (r c) -> p r c", r=2)
        O = work[:, 7 * UW:8 * UW].rearrange("p (r b c) -> p r b c", r=2, b=GB)
        OdT = work[:, 8 * UW:9 * UW].rearrange("p (r c) -> p r c", r=2)
        sg = work[:, 0:GT * 3].rearrange("p (r c) -> p r c", r=3)
        gu = work[:, GT * 3:GT * 6].rearrange("p (r c) -> p r c", r=3)
        hid = work[:, GT * 6:GT * 9].rearrange("p (r c) -> p r c", r=3)
        wide = work[:, GT * 9:GT * 13]
        wraw = sb("wraw", [128, 9, D])
        wT = sb("wT", [128, 9, D])
        wm = sb("wm", [128, 4, D])
        bo = sb("bo", [128, D])
        mneg = sb("mneg", [128, D])
        cm = sb("cm", [128, D])
        idf = sb("idf", [128, 128])
        idb = sb("idb", [128, 128], BF16)
        tr = sb("tr", [128, 16, 16])
        stats = sb("stats", [128, GB, 6])
        mv = sb("mv", [128, 2, GB, 2])
        veps = sb("veps", [128, GB])
        half = sb("half", [128, GB])
        rstd = sb("rstd", [128, 2, GB])
        negm = sb("negm", [128, 4, UH])
        den = sb("den", [128, H])
        rden = sb("rden", [128, H])
        sel = sb("sel1s", [128, C1, 128], BF16)
        gw = {MOE: sb("gw1", [128, E1]), ROUTE: sb("gw2", [128, E2])}
        earlier = sb("earlier", [128, 2, 128], BF16)
        start_r = sb("start_r", [128, E2])
        base = sb("base", [128, E2])
        step_r = sb("step_r", [128, 32 + TILES])
        dest = sb("dest", [128, B, KEEP2])
        chosen = sb("chosen", [128, 2, GB * E2], BF16)
        indexf = sb("indexf", [128, GB, KEEP2])
        index = sb("index", [128, 2, GB, KEEP2], I32)
        yindex = sb("yindex", [128, QT], I32)
        tl = sb("tl", [1, 8, TILES])
        table = sb("table", [1, 2 * TILES + E2], I32)
        bias_r = sb("bias_r", [128, E1])
        wg1 = sb("wg1", [128, E1 * M1 + 128])
        wu1 = sb("wu1", [128, E1 * M1 + 128])
        wd1 = sb("wd1", [128, C1 + 1, D])
        wg2 = heavy[:, 0:WE]
        wu2 = heavy[:, WE:2 * WE]
        wd2 = heavy[:, 2 * WE:3 * WE]
        t_sg = work[:, 0:2 * M2].rearrange("p (r c) -> p r c", r=2)
        t_hid = work[:, 2 * M2:4 * M2].rearrange("p (r c) -> p r c", r=2)
        t_hT = work[:, 4 * M2:6 * M2].rearrange("p (r c) -> p r c", r=2)
        free = GT * 12
        pay = work[:, free:free + 2 * GB * KEEP2 * ROW].rearrange("p (r b c w) -> p r b c w", r=2, b=GB, c=KEEP2)
        free = 6 * M2
        t_rows = work[:, free:free + QT * ROW].rearrange("p (q w) -> p q w", q=QT)
        free += QT * ROW
        t_y = work[:, free:free + QT * D].rearrange("p (q w) -> p q w", q=QT)
        y_both = heavy[:, 0:KEEP2 * B * D].rearrange("p (c b d) -> p c b d", c=KEEP2, b=B)
        staged = nc.dram_tensor("staged", (2, H * STACK, GT), BF16, kind="Internal").ap()
        routed = nc.dram_tensor("routed", (E2 * REGION + E2 * S, ROW), F32, kind="Internal").ap()
        outputs = nc.dram_tensor("outputs", (KEEP2 * TOKENS + 2 * E2 * S, D), F32, kind="Internal").ap()
        NR = 64
        lr = sb("lr", [128, 14, NR])
        combp = sb("combp", [128, GB, 128], BF16)
        combT = sb("combT", [128, 2, GT], BF16)
        WQ, WK, WV, WOUT, XWO, LQ, LK, LV, LO = range(9)
        MQ, MK, MV, MO = range(4)
        NE = {MOE: E1, ROUTE: E2}
        QRY, KEY = range(2)

        block = stack.enter_context(nc.Block())

        def groups(eng, body):
            body(0, 0, True, False)
            with eng.Fori(0, (NG - 2) // 2) as j:
                body(2 * j + 1, 1, False, False)
                body(2 * j + 2, 0, False, False)
            body(NG - 1, (NG - 1) % 2, False, True)

        def groups_ahead(eng, body):
            body(0, 0, True, 2)
            with eng.Fori(0, (NG - 4) // 2) as j:
                body(2 * j + 1, 1, False, 2)
                body(2 * j + 2, 0, False, 2)
            for g in range(NG - 3, NG):
                body(g, g % 2, False, min(2, NG - 1 - g))

        def follows_on(st):
            return st in ATTN and st - 1 in ATTN

        def target(st, g, p, left, off):
            if off <= left:
                return st, g + off, (p + off) % 2
            if follows_on(st + 1):
                return st + 1, off - left - 1, (p + off) % 2
            return None, 0, 0

        def upcoming(st, g, p, left, t):
            found = []
            for off in (1, 2):
                ts, tg, tp = target(st, g, p, left, off)
                if ts is not None:
                    o, ks = PARTS_AT[ts].get(t, (0, ()))
                    if o == off:
                        found += [(ts, tg, tp, k) for k in ks]
            return found

        def sent_before(g, p):
            return GROUP_SENT // 2 * (g - p)

        def landed(t, q):
            return 16 // QT * (t - q)

        def tiles(eng, body):
            for q in range(QT):
                body(q, q, q == 0, False)
            with eng.Fori(1, TILES // QT - 1) as j:
                for q in range(QT):
                    body(QT * j + q, q, False, False)
            for q in range(QT):
                body(TILES - QT + q, q, False, q == QT - 1)

        def before(st, g, c):
            if c >= 2:
                return g, c - 2
            n = CHUNKS[st]
            return g - 1, n - 1 if (n - 1) % 2 == c else n - 2

        @block.sync
        def _(sp):
            xv = x.rearrange("b s d -> s b d")
            sp.dma_start(X[:, 0:GB, :], xv[:, 0:GB, :]).then_inc(s_x0, 16)
            sp.dma_start(idf[:, :], ident).then_inc(s_w0, 16)
            sp.dma_start(wraw[:, 0:3, :], w_qkv.rearrange("(t o) i -> o t i", t=3)).then_inc(s_w0, 16)
            for n, w in ((WOUT, w_out), (XWO, x0_wo), (LQ, l_wq), (LK, l_wk), (LV, l_wv), (LO, l_wo)):
                sp.dma_start(wraw[:, n, :], w).then_inc(s_w0, 16)
            sp.dma_start(X[:, GB:B, :], xv[:, GB:B, :]).then_inc(s_x1, 16)
            for n, w in ((MQ, m_wq), (MK, m_wk), (MV, m_wv), (MO, m_wo)):
                sp.dma_start(wm[:, n, :], w).then_inc(s_w1, 16)
            sp.dma_start(bo[:, :], m_bo.rearrange("(a d) -> a d", a=1).broadcast_to([128, D])).then_inc(s_w1, 16)
            sp.dma_start(mneg[:, :], mask[0, 0]).then_inc(s_w1, 16)
            sp.dma_start(cm[:, :], causal).then_inc(s_w1, 16)
            sp.dma_start(tr[:, :, :], tri.rearrange("(a j) i -> a j i", a=1).broadcast_to([128, 16, 16])).then_inc(s_w1, 16)
            sp.dma_start(gw[MOE][:, :], gate1).then_inc(s_w1, 16)
            sp.dma_start(gw[ROUTE][:, :], gate2).then_inc(s_w1, 16)
            sp.dma_start(start_r[:, :], starts.rearrange("(a e) -> a e", a=1).broadcast_to([128, E2])).then_inc(s_w1, 16)
            sp.dma_start(base[:, :], starts.rearrange("(a e) -> a e", a=1).broadcast_to([128, E2])).then_inc(s_w1, 16)
            sp.dma_start(step_r[:, :], steps.rearrange("(a e) -> a e", a=1).broadcast_to([128, 32 + TILES])).then_inc(s_w1, 16)
            sp.dma_start(dest[:, :, :], dests).then_inc(s_w1, 16)
            sp.dma_start(routed[E2 * REGION:, :], padding[E2 * S:, :]).then_inc(s_pad, 16)
            sp.dma_start(bias_r[:, :], bias1.rearrange("(a d) -> a d", a=1).broadcast_to([128, E1])).then_inc(s_w1, 16)
            sp.dma_start(wg1[:, 0:E1 * M1].rearrange("p (e m) -> p e m", e=E1), w_gate1.rearrange("e h m -> h e m")).then_inc(s_w1, 16)
            sp.dma_start(wu1[:, 0:E1 * M1].rearrange("p (e m) -> p e m", e=E1), w_up1.rearrange("e h m -> h e m")).then_inc(s_w1, 16)
            sp.dma_start(wg1[:, E1 * M1:], s_gate1).then_inc(s_w1, 16)
            sp.dma_start(wu1[:, E1 * M1:], s_up1).then_inc(s_w1, 16)
            sp.dma_start(wd1[:, 0:C1, :], w_down1.rearrange("(c two) m h -> (two m) c h", two=2)).then_inc(s_w1, 16)
            sp.dma_start(wd1[:, C1, :], s_down1).then_inc(s_w1, 16)

            def context(st, g, p):
                sp.wait_ge(s_cT, at("cT", st, g - 1, 0))
                settle(sp, "sp")
                if st == CROSS:
                    sp.wait_ge(s_ve, at("ve", st, g - 1, 0))
                    settle(sp, "sp")
                sp.wait_ge(s_ctx, at("ctx", st, g, 0))
                settle(sp, "sp")
                b0 = g * GB
                sp.dma_start(crow[:, p, :, :], ctx.rearrange("b s d -> s b d")[:, bass.ds(b0, GB), :]).then_inc(s_ctx, 16)

            def slots(st, op, part, early):
                side = ONE_SIDE if op == (QRY if st == LINEAR else KEY) else OTHER_SIDE
                to = staged[op].rearrange("(h s d) t -> s h d t", s=SLOTS, d=HD)
                return [(to[i], parts[:, op, part, :]) for i in range(SLOTS) if side[i] == part and (i < EARLY) == early]

            def stack_up(st, op, p, early):
                rows = staged[op].rearrange("(a i r) t -> i r a t", i=2, r=STACK)
                lo, hi = (0, EARLY * HD) if early else (EARLY * HD, STACK)
                if op == (QRY if st == LINEAR else KEY):
                    return [(spread[64 * i + lo:64 * i + hi, p, :, i, :], rows[i, lo:hi]) for i in range(2)]
                return [(stacked[64 * i + lo:64 * i + hi, p, :, :], rows[i, lo:hi]) for i in range(2)]

            def queries(st, g, p):
                sp.wait_ge(s_qe, at("qe", st, g, 1))
                settle(sp, "sp")
                sp.wait_ge(s_spread, at("spread", st, g, 0))
                settle(sp, "sp")
                for to, rows in slots(st, QRY, 0, True):
                    sp.dma_start(to, rows).then_inc(s_qst, 16)
                for to, rows in slots(st, QRY, 0, False):
                    sp.dma_start(to, rows).then_inc(s_qsl, 16)
                sp.wait_ge(s_qp, at("qp", st, g, 1))
                settle(sp, "sp")
                for to, rows in slots(st, QRY, 1, True):
                    sp.dma_start(to, rows).then_inc(s_qst, 16)
                sp.wait_ge(s_qp, at("qp", st, g, 2))
                settle(sp, "sp")
                for to, rows in slots(st, QRY, 2, False):
                    sp.dma_start(to, rows).then_inc(s_qsl, 16)
                sp.wait_ge(s_qst, at("qst", st, g, 64))
                settle(sp, "sp")
                for to, rows in stack_up(st, QRY, p, True):
                    sp.dma_start(to, rows).then_inc(s_spread, 16)
                sp.wait_ge(s_qsl, at("qsl", st, g, 32))
                settle(sp, "sp")
                for to, rows in stack_up(st, QRY, p, False):
                    sp.dma_start(to, rows).then_inc(s_spread, 16)

            def keys(st, g, p):
                sp.wait_ge(s_ke, at("ke", st, g, 1))
                settle(sp, "sp")
                sp.wait_ge(s_spread, at("spread", st, g, 0))
                settle(sp, "sp")
                for to, rows in slots(st, KEY, 0, True):
                    sp.dma_start(to, rows).then_inc(s_kst, 16)
                for to, rows in slots(st, KEY, 0, False):
                    sp.dma_start(to, rows).then_inc(s_ksl, 16)
                sp.wait_ge(s_kp, at("kp", st, g, 1))
                settle(sp, "sp")
                for to, rows in slots(st, KEY, 1, True):
                    sp.dma_start(to, rows).then_inc(s_kst, 16)
                sp.wait_ge(s_kp, at("kp", st, g, 2))
                settle(sp, "sp")
                for to, rows in slots(st, KEY, 2, False):
                    sp.dma_start(to, rows).then_inc(s_ksl, 16)
                sp.wait_ge(s_kst, at("kst", st, g, 64))
                settle(sp, "sp")
                for to, rows in stack_up(st, KEY, p, True):
                    sp.dma_start(to, rows).then_inc(s_spread, 16)
                sp.wait_ge(s_ksl, at("ksl", st, g, 32))
                settle(sp, "sp")
                for to, rows in stack_up(st, KEY, p, False):
                    sp.dma_start(to, rows).then_inc(s_spread, 16)

            def spreading(st, g, p):
                if st == CROSS:
                    keys(st, g, p)
                    queries(st, g, p)
                else:
                    queries(st, g, p)
                    keys(st, g, p)

            sp.wait_ge(s_zero, 3)
            for st in ATTN:
                if not follows_on(st):
                    spreading(st, 0, 0)

                def body(g, p, first, left):
                    for off in (1, 2):
                        ts, tg, tp = target(st, g, p, left, off)
                        if (ts, off) in ((CROSS, 1), (MASKX, 2)):
                            context(ts, tg, tp)
                    ts, tg, tp = target(st, g, p, left, 1)
                    if ts is not None:
                        spreading(ts, tg, tp)
                groups_ahead(sp, body)
            sp.wait_ge(s_s, at("s", MASKX, NG, 0))
            settle(sp, "sp")
            sp.dma_start(wg2.rearrange("p (e m) -> p e m", e=E2), e_w1.rearrange("e h m -> h e m")).then_inc(s_w2, 16)
            sp.dma_start(wu2.rearrange("p (e m) -> p e m", e=E2), e_w3.rearrange("e h m -> h e m")).then_inc(s_w2, 16)
            sp.dma_start(wd2.rearrange("p (e n) -> p e n", n=D), e_w2.rearrange("e (c p) h -> p (e c) h", p=128)).then_inc(s_w2, 16)

            sp.wait_ge(s_ends, 1)
            for e in range(0, E2, 2):
                row = sp.value_load(table[0:1, 2 * TILES + e:2 * TILES + e + 1], min_val=0, max_val=E2 * REGION - S)
                sp.dma_start(routed[bass.ds(row, S), :], padding[e * S:(e + 1) * S, :]).then_inc(s_pad, 16)
            sp.wait_ge(s_pad, 16 * (1 + E2 // 2))
            sp.wait_ge(s_padodd, 16 * (E2 // 2))
            sp.wait_ge(s_table, TABLE_STEPS)
            for p in range(2):
                sp.wait_ge(s_sent[p], NG // 2 * GROUP_SENT)

            def fetch(t, q, first, last):
                row = sp.value_load(table[0:1, bass.ds(t, 1)], min_val=0, max_val=E2 * REGION + (E2 - 1) * S)
                if not isinstance(t, int) or t >= QT:
                    sp.wait_ge(s_rT, t - QT + 1)
                    settle(sp, "sp")
                    sp.wait_ge(s_yw, 2 * (t - QT + 1))
                    settle(sp, "sp")
                sp.dma_start(t_rows[:, q, :], routed[bass.ds(row, S), :]).then_inc(s_rows[q], 16)
            tiles(sp, fetch)

            for q in range(QT):
                sp.wait_ge(s_ysent[q], landed(TILES + q, q))
            both = outputs[0:KEEP2 * TOKENS, :].rearrange("(c b s) d -> c s b d", c=KEEP2, s=S)
            for n in range(SUMS):
                rows = slice(n * SB, (n + 1) * SB)
                for c in range(KEEP2):
                    sp.dma_start(y_both[:, c, rows, :], both[c][:, rows, :]).then_inc(s_back[n], 16)
            for n in range(SUMS):
                rows = slice(n * SB, (n + 1) * SB)
                sp.wait_ge(s_sum, n + 1)
                sp.dma_start(out.rearrange("b s d -> s b d")[:, rows, :], X[:, rows, :]).then_inc(s_out, 16)
            sp.wait_ge(s_out, 16 * SUMS)

        @block.gpsimd
        def _(pool):
            pool.dma_start(idb[:, :], ident).then_inc(s_tab, 16)
            pool.dma_start(sel[:, :, :], sel1).then_inc(s_tab, 16)
            pool.dma_start(earlier[:, :, :], before_t).then_inc(s_tab, 16)
            pool.memset(heavy[:, 2 * WE:], 0.0).then_inc(s_zero, 1)
            pool.memset(half[:, :], -0.5).then_inc(s_ones, 1)
            pool.memset(V[:, :, :, :, HD:HD + 1], 1.0).then_inc(s_ones, 1)
            pool.memset(combp[:, :, :], 0.0).then_inc(s_ones, 1)
            pool.wait_ge(s_ones, 3)

            def rsqrt(st, g, p):
                pool.wait_ge(s_veps, at("veps", st, g, 1))
                pool.tensor_tensor(rstd[:, p, :], veps[:, :], half[:, :], ALU.pow).then_inc(s_rstd, 1)

            def values(st, g, p):
                pool.wait_ge(s_ctx, at("ctx", st, g, 16))
                pool.wait_ge(s_pv, at("pv", st, g - 1, 0))
                settle(pool, "pool")
                pool.tensor_copy(V[:, p, :, :, 0:HD], crow[:, p, :, :].rearrange("p b (h d) -> p b h d", d=HD)).then_inc(s_ve, 1)

            def query_parts(st, g):
                if st != MASKX:
                    pool.wait_ge(s_qr, at("qr", st, g, 1))
                    pool.wait_ge(s_qst, at("qst", st, g, 0))
                    pool.wait_ge(s_qsl, at("qsl", st, g, 0))
                    settle(pool, "pool")
                    pool.tensor_copy(parts[:, QRY, 1, :], rest[:, QRY, :]).then_inc(s_qp, 1)
                pool.wait_ge(s_qp, at("qp", st, g, 1))
                pool.tensor_tensor(parts[:, QRY, 2, :], rest[:, QRY, :], parts[:, QRY, 1, :], ALU.subtract).then_inc(s_qp, 1)

            def key_parts(st, g):
                if st != MASKX:
                    pool.wait_ge(s_kr, at("kr", st, g, 1))
                    pool.wait_ge(s_kst, at("kst", st, g, 0))
                    pool.wait_ge(s_ksl, at("ksl", st, g, 0))
                    settle(pool, "pool")
                    pool.tensor_copy(parts[:, KEY, 1, :], rest[:, KEY, :]).then_inc(s_kp, 1)
                pool.wait_ge(s_kp, at("kp", st, g, 1))
                pool.tensor_tensor(parts[:, KEY, 2, :], rest[:, KEY, :], parts[:, KEY, 1, :], ALU.subtract).then_inc(s_kp, 1)

            def operand_parts(st, g):
                if st == CROSS:
                    key_parts(st, g)
                    query_parts(st, g)
                elif st == LINEAR:
                    query_parts(st, g)
                else:
                    query_parts(st, g)
                    key_parts(st, g)

            def shift(st, g, t):
                pool.wait_ge(s_negm, at("negm", st, g, t + 1))
                n = UE[st]
                tv = T[:, t % 4, 0:n * S].rearrange("p (h k) -> p h k", h=n)
                pool.tensor_tensor(tv, tv, negm[:, t % 4, 0:n].unsqueeze(2).broadcast_to([128, n, S]), ALU.add).then_inc(s_t, 1)

            def before_which(st, g):
                pool.wait_ge(s_route, at("route", st, g, 16))
                shape = [128, GB, E1, E1]
                same = wide[:, 0:1024].rearrange("p (b j i) -> p b j i", b=GB, j=E1)
                pool.tensor_tensor(same, same, tr[:, :, :].unsqueeze(1).broadcast_to(shape), ALU.mult).then_inc(s_before, 1)
                pool.wait_ge(s_before, at("before", st, g, 1))
                pool.tensor_tensor(wide[:, 0:1024], wide[:, 0:1024], wide[:, 1024:2048], ALU.add).then_inc(s_before, 1)

            def scatter(g, p, rows):
                for b in rows:
                    for c in range(KEEP2):
                        pool.indirect_dma_start(out=routed, out_offset=bass.IndirectOffsetOnAxis(ap=index[:, p, b, c:c + 1], axis=0),
                                                in_=pay[:, p, b, c, :], in_offset=None).then_inc(s_sent[p], 16)

            def attention(st):
                if not follows_on(st):
                    rsqrt(st, 0, 0)
                    operand_parts(st, 0)
                    rsqrt(st, 1, 1)

                def body(g, p, first, left):
                    s1, g1, p1 = target(st, g, p, left, 1)
                    s2, g2, p2 = target(st, g, p, left, 2)
                    if s1 == CROSS:
                        rsqrt(s1, g1, p1)
                    if s1 is not None and st != MASKX:
                        operand_parts(s1, g1)
                    if s1 == CROSS:
                        values(s1, g1, p1)
                    if st == MASKX:
                        for t in range(UN):
                            shift(st, g, t)
                            if t == 1 and left >= 1:
                                query_parts(st, g + 1)
                            if t == 2 and left >= 1:
                                key_parts(st, g + 1)
                            if t == 6 and left >= 2:
                                rsqrt(st, g + 2, p)
                    elif s2 in TWO_AHEAD:
                        rsqrt(s2, g2, p2)
                groups_ahead(pool, body)

            def experts(st):
                rsqrt(st, 0, 0)
                before_which(st, 0)

                def body(g, p, first, last):
                    if not last:
                        rsqrt(st, g + 1, 1 - p)
                        before_which(st, g + 1)
                groups(pool, body)

            def route():
                rsqrt(ROUTE, 0, 0)
                rsqrt(ROUTE, 1, 1)

                def body(g, p, first, left):
                    pool.wait_ge(s_pay, at("pay", ROUTE, g, 2))
                    settle(pool, "pool")
                    pool.wait_ge(s_payw, at("payw", ROUTE, g, 1))
                    settle(pool, "pool")
                    pool.wait_ge(s_index, at("index", ROUTE, g, 1))
                    settle(pool, "pool")
                    scatter(g, p, range(GB // 2))
                    if left >= 2:
                        rsqrt(ROUTE, g + 2, p)
                    scatter(g, p, range(GB // 2, GB))
                groups_ahead(pool, body)

            attention(SELF)
            attention(CROSS)
            experts(MOE)
            attention(LINEAR)
            attention(MASKX)
            route()

            def send(t, q, first, last):
                pool.wait_ge(s_yw, 2 * (t + 1))
                settle(pool, "pool")
                pool.indirect_dma_start(out=outputs, out_offset=bass.IndirectOffsetOnAxis(ap=yindex[:, q:q + 1], axis=0),
                                        in_=t_y[:, q, :], in_offset=None).then_inc(s_ysent[q], 16)
            tiles(pool, send)

        @block.scalar
        def _(act):
            for n in range(3):
                act.wait_ge(s_wT, n + 1)
                act.activation(wT[:, 3 * n:3 * n + 3, :], front[:, 0:3 * D].rearrange("p (a b) -> p a b", a=3), ACT.Copy).then_inc(s_wTe, 1)

            def features():
                act.activation(phi_e[:, :], front[:, :], ACT.Exp).then_inc(s_phi, 1)
                act.activation(phi_r[:, :], front[:, :], ACT.Relu).then_inc(s_phi, 1)

            def first_query_part(st, g, rows):
                act.wait_ge(s_qst, at("qst", st, g, 0))
                act.wait_ge(s_qsl, at("qsl", st, g, 0))
                act.activation(parts[:, QRY, 0, :], rows, ACT.Copy).then_inc(s_qe, 1)

            def first_key_part(st, g, rows):
                act.wait_ge(s_kst, at("kst", st, g, 0))
                act.wait_ge(s_ksl, at("ksl", st, g, 0))
                act.activation(parts[:, KEY, 0, :], rows, ACT.Copy).then_inc(s_ke, 1)

            def second_query_part(st, g):
                act.wait_ge(s_qr, at("qr", st, g, 1))
                act.activation(parts[:, QRY, 1, :], rest[:, QRY, :], ACT.Copy).then_inc(s_qp, 1)

            def second_key_part(st, g):
                act.wait_ge(s_kr, at("kr", st, g, 1))
                act.activation(parts[:, KEY, 1, :], rest[:, KEY, :], ACT.Copy).then_inc(s_kp, 1)

            def front_part(st, g, p, k):
                if k == 0 and st == MASKX:
                    act.wait_ge(s_cT, at("cT", st, g, 1))
                    act.activation(cT[:, p, :], front[:, :], ACT.Copy).then_inc(s_cTe, 1)
                if k == 0 and st == CROSS:
                    act.wait_ge(s_cT, at("cT", st, g, 1))
                    first_key_part(st, g, front[:, :])
                if k == 1:
                    act.wait_ge(s_xT, at("xT", st, g, 1))
                    if st == CROSS:
                        first_query_part(st, g, front[:, :])
                    else:
                        act.activation(xT[:, p, :], front[:, :], ACT.Copy).then_inc(s_xTe, 1)
                if k == 2 and st in (SELF, MASKX):
                    act.wait_ge(s_q, at("q", st, g, 1))
                    first_query_part(st, g, front[:, :])
                if k == 2 and st == LINEAR:
                    act.wait_ge(s_q, at("q", st, g, 1))
                    act.wait_ge(s_kf, at("kf", st, g, 0))
                    features()
                if k == 3 and st in (SELF, MASKX):
                    act.wait_ge(s_k, at("k", st, g, 1))
                    first_key_part(st, g, front[:, :])
                if k == 3 and st == LINEAR:
                    act.wait_ge(s_k, at("k", st, g, 1))
                    act.wait_ge(s_qf, at("qf", st, g, 1))
                    features()
                    first_query_part(st, g, src[:, p, :])
                if k == 4 and st == LINEAR:
                    act.wait_ge(s_kf, at("kf", st, g, 1))
                    first_key_part(st, g, dense[:, p, :])
                    second_key_part(st, g)
                if k == 5 and st != CROSS:
                    act.wait_ge(s_v, at("v", st, g, 1))
                    act.activation(V[:, p, :, :, 0:HD], front[:, :].rearrange("p (b h d) -> p b h d", b=GB, d=HD), ACT.Copy).then_inc(s_ve, 1)

            def shifted_exponential(st, g, t):
                act.wait_ge(s_negm, at("negm", st, g, t + 1))
                for i in range(UE[st], UH):
                    tv = T[:, t % 4, i * S:(i + 1) * S]
                    m = act.activation(tv, tv, ACT.Exp, bias=negm[:, t % 4, i:i + 1])
                m.then_inc(s_eb, 1)

            def exponential(st, g, t):
                act.wait_ge(s_t, at("t", st, g, t + 1))
                tv = T[:, t % 4, 0:UE[st] * S]
                act.activation(tv, tv, ACT.Exp, scale=1.0 if st == MASKX else SCALE).then_inc(s_e, 1)

            def copy_turned(st, g, t):
                act.wait_ge(s_pt, at("pt", st, g, t + 1))
                act.activation(PT[:, t % 2, :], turned[:, :], ACT.Copy).then_inc(s_pte, 1)

            def copy_out(st, g, b):
                act.wait_ge(s_pv, at("pv", st, g, 2 * b + 2))
                act.activation(OT[:, b % 2, :], back[:, :], ACT.Copy).then_inc(s_ot, 1)

            def slot(st, g, p, t, first, left, flush):
                if t % 2 == 0:
                    if t >= 4 and not flush:
                        copy_out(st, g, (t - 4) // 2)
                    elif t < 4 and not first:
                        copy_out(st, g - 1, (t + UN - 4) // 2)
                if st != LINEAR:
                    if t >= 2:
                        if not flush:
                            copy_turned(st, g, t - 2)
                    elif not first:
                        copy_turned(st, g - 1, t + UN - 2)
                if not flush:
                    s1, g1, p1 = target(st, g, p, left, 1)
                    if s1 == MASKX and t == 1:
                        second_query_part(s1, g1)
                    if s1 == MASKX and t == 2:
                        second_key_part(s1, g1)
                    for ts, tg, tp, k in upcoming(st, g, p, left, t):
                        front_part(ts, tg, tp, k)
                if t == 4 and not first:
                    act.wait_ge(s_oT, at("oT", st, g - 1, 1))
                    act.activation(OdT[:, 1 - p, :], front[:, :], ACT.Copy).then_inc(s_oTe, 1)
                if st == MASKX and not flush:
                    shifted_exponential(st, g, t)
                if st != LINEAR and not flush:
                    exponential(st, g, t)

            def attention(st):
                if not follows_on(st):
                    for k in range(6):
                        front_part(st, 0, 0, k)
                    for k in PARTS_AT[st][7][1]:
                        front_part(st, 1, 1, k)

                def body(g, p, first, left):
                    for t in range(UN):
                        slot(st, g, p, t, first, left, False)
                groups_ahead(act, body)
                for t in range(5):
                    slot(st, NG, NG % 2, t, False, 0, True)

            def experts(st):
                def routing(g, p, k):
                    if k == 0:
                        act.wait_ge(s_xT, at("xT", st, g, 1))
                        act.activation(xT[:, p, :], front[:, :], ACT.Copy).then_inc(s_xTe, 1)
                    if k == 1:
                        n = GB * NE[st]
                        act.wait_ge(s_lg, at("lg", st, g, 1))
                        act.activation(lr[:, 0, 0:n], front[:, 0:n], ACT.Exp, scale=-1.0).then_inc(s_rexp, 1)
                    if k == 2:
                        act.wait_ge(s_combT, at("combT", st, g, 1))
                        act.activation(combT[:, p, :], front[:, :].bitcast(BF16)[:, 0:GT], ACT.Copy).then_inc(s_combTe, 1)

                for k in range(3):
                    routing(0, 0, k)
                ROUTE_AT = {2: 0, 3: 1}

                def body(g, p, first, last):
                    for c in range(CHUNKS[st]):
                        act.wait_ge(s_gate, at("gate", st, g, c + 1))
                        act.wait_ge(s_gu, at("gu", st, g, c - 2))
                        act.activation(sg[:, c % 3, :], score[:, 0, (c % 2) * GT:(c % 2 + 1) * GT], ACT.Silu).then_inc(s_silu, 1)
                        if c in ROUTE_AT and not last:
                            routing(g + 1, 1 - p, ROUTE_AT[c])
                    if not last:
                        routing(g + 1, 1 - p, 2)
                groups(act, body)

            def route():
                st = ROUTE

                def fill(g, p):
                    act.wait_ge(s_xn, at("xn", st, g, GB))
                    if not isinstance(g, int) or g >= 2:
                        act.wait_ge(s_sent[p], sent_before(g, p))
                    act.activation(pay[:, p, :, :, 0:D], xn[:, p, :, :].unsqueeze(2).broadcast_to([128, GB, KEEP2, D]), ACT.Copy).then_inc(s_pay, 1)
                    act.activation(pay[:, p, :, :, DEST], dest[:, bass.ds(g * GB, GB), :], ACT.Copy).then_inc(s_pay, 1)

                def copy_x(g, p):
                    act.wait_ge(s_xT, at("xT", st, g, 1))
                    act.activation(xT[:, p, :], front[:, :], ACT.Copy).then_inc(s_xTe, 1)

                copy_x(0, 0)
                fill(0, 0)

                def body(g, p, first, last):
                    n = GB * E2
                    act.wait_ge(s_route, at("route", st, g, 2))
                    act.activation(lr[:, 3, 0:n], lr[:, 2, 0:n], ACT.Exp).then_inc(s_rexp, 1)
                    if not last:
                        copy_x(g + 1, 1 - p)
                        fill(g + 1, 1 - p)
                groups(act, body)

            def routed_experts():
                act.wait_ge(s_ends, 1)
                for e in range(1, E2, 2):
                    row = act.value_load(table[0:1, 2 * TILES + e:2 * TILES + e + 1], min_val=0, max_val=E2 * REGION - S)
                    act.dma_start(routed[bass.ds(row, S), :], padding[e * S:(e + 1) * S, :]).then_inc(s_padodd, 16)

                def copy_hidden(t, p):
                    act.wait_ge(s_hT, t + 1)
                    act.activation(t_hT[:, p, :], turned[:, p * M2:(p + 1) * M2], ACT.Copy).then_inc(s_hTe, 1)

                def body(t, q, first, last):
                    p = q % 2
                    act.wait_ge(s_tg, t + 1)
                    if not isinstance(t, int) or t >= 2:
                        act.wait_ge(s_thid, t - 1)
                    act.activation(t_sg[:, p, :], score[:, 0, p * M2:(p + 1) * M2], ACT.Silu).then_inc(s_tsilu, 1)
                    if not first:
                        copy_hidden(t - 1, 1 - p)
                tiles(act, body)
                copy_hidden(TILES - 1, (TILES - 1) % 2)

            attention(SELF)
            attention(CROSS)
            experts(MOE)
            attention(LINEAR)
            attention(MASKX)
            route()
            routed_experts()

        @block.tensor
        def _(pe):
            pe.wait_ge(s_w0, 16 * 8)
            for n in range(3):
                if n:
                    pe.wait_ge(s_wTe, n)
                for k in range(3):
                    m = pe.transpose(front[:, k * D:(k + 1) * D], wraw[:, 3 * n + k, :], idf[:, :])
                m.then_inc(s_wT, 1)
            pe.wait_ge(s_wTe, 3)
            pe.wait_ge(s_zero, 3)
            pe.wait_ge(s_ones, 3)

            def transposed_x(st, g, p):
                pe.wait_ge(s_xn, at("xn", st, g, GB))
                for b in range(GB):
                    m = pe.transpose(front[:, b * S:(b + 1) * S], xn[:, p, b, :], idf[:, :])
                m.then_inc(s_xT, 1)

            def front_free(st, g):
                if st != CROSS or isinstance(g, int) and g == 0:
                    pe.wait_ge(s_ve, at("ve", st, g, 0))
                if st == CROSS:
                    pe.wait_ge(s_qr, at("qr", st, g, 0))
                pe.wait_ge(s_xupd, at("xupd", st, g - 2, 0))

            def front_part(st, g, p, k, tail):
                own = st in (SELF, LINEAR)
                if follows_on(st) and isinstance(g, int) and g == 1 and k == (0 if st == CROSS else 2):
                    pe.wait_ge(s_xupd, at("xupd", st, 0, 0))
                if k == 0:
                    front_free(st, g)
                    if st in (CROSS, MASKX):
                        pe.wait_ge(s_ctx, at("ctx", st, g, 16))
                        for b in range(GB):
                            m = pe.transpose(front[:, b * S:(b + 1) * S], crow[:, p, b, :], idf[:, :])
                        m.then_inc(s_cT, 1)
                if k == 1:
                    if st == MASKX:
                        pe.wait_ge(s_cTe, at("cTe", st, g, 1))
                    if st == CROSS:
                        pe.wait_ge(s_kr, at("kr", st, g, 1))
                    transposed_x(st, g, p)
                if k == 2 and st != CROSS:
                    pe.wait_ge(s_xTe, at("xTe", st, g, 1))
                    w = {SELF: wT[:, WQ, :], LINEAR: wT[:, LQ, :], MASKX: wm[:, MQ, :]}[st]
                    pe.matmul(front[:, :], w, xT[:, p, :], start=True, stop=True).then_inc(s_q, 1)
                if k == 3 and st != CROSS:
                    if st == LINEAR:
                        pe.wait_ge(s_phi, at("phi", st, g, 2))
                    else:
                        pe.wait_ge(s_qr, at("qr", st, g, 1))
                    w = {SELF: wT[:, WK, :], LINEAR: wT[:, LK, :], MASKX: wm[:, MK, :]}[st]
                    pe.matmul(front[:, :], w, (xT if own else cT)[:, p, :], start=True, stop=True).then_inc(s_k, 1)
                if k == 5 and st != CROSS:
                    if st == LINEAR:
                        pe.wait_ge(s_phi, at("phi", st, g, 4))
                    else:
                        pe.wait_ge(s_kr, at("kr", st, g, 1))
                    if tail:
                        pe.wait_ge(s_oTe, at("oTe", st, g - 2, 1))
                    w = {SELF: wT[:, WV, :], LINEAR: wT[:, LV, :], MASKX: wm[:, MV, :]}[st]
                    for b in range(GB):
                        m = pe.matmul(front[:, b * D:(b + 1) * D], (xT if own else cT)[:, p, b * S:(b + 1) * S], w, start=True, stop=True)
                    m.then_inc(s_v, 1)

            def scores(st, g, p, t):
                if t == 0:
                    pe.wait_ge(s_spread, at("spread", st, g, 128))
                if st == MASKX:
                    pe.wait_ge(s_sm, at("sm", st, g, t - 1))
                else:
                    pe.wait_ge(s_t, at("t", st, g, t - 1))
                b, u = t // 2, t % 2
                cols = slice(b * S, (b + 1) * S)
                for q in range(UH // 2):
                    a = UH // 2 * u + q
                    m = pe.matmul(score[:, t % 2, q * 2 * S:(q + 1) * 2 * S], stacked[:, p, a, cols], spread[:, p, a, :, cols], start=True, stop=True)
                m.then_inc(s_s, 1)

            def turn(st, g, t):
                if st == MASKX:
                    pe.wait_ge(s_eb, at("eb", st, g, t + 1))
                pe.wait_ge(s_e, at("e", st, g, t + 1))
                pe.wait_ge(s_pte, at("pte", st, g, t))
                for h in range(UH):
                    m = pe.transpose(turned[:, h * S:(h + 1) * S], T[:, t % 4, h * S:(h + 1) * S], idf[:, :])
                m.then_inc(s_pt, 1)

            def weigh(st, g, p, t):
                b, u = t // 2, t % 2
                if st == LINEAR:
                    pe.wait_ge(s_t, at("t", st, g, t + 1))
                else:
                    pe.wait_ge(s_pte, at("pte", st, g, t + 1))
                if t == 0:
                    pe.wait_ge(s_ve, at("ve", st, g, 1))
                if u == 0:
                    pe.wait_ge(s_on, at("on", st, g, b))
                for i in range(UH):
                    h = UH * u + i
                    j, s = h % 4, h // 4
                    mov = T[:, t % 4, i * S:(i + 1) * S] if st == LINEAR else PT[:, t % 2, i * S:(i + 1) * S]
                    m = pe.matmul(back[32 * j:32 * j + HD + 1, s * S:(s + 1) * S], V[:, p, b, h, :], mov, start=True, stop=True)
                m.then_inc(s_pv, 1)

            def token_rows(st, g, b):
                pe.wait_ge(s_ot, at("ot", st, g, b + 1))
                for s in range(4):
                    m = pe.transpose(back[:, s * 128:(s + 1) * 128], OT[:, b % 2, s * S:(s + 1) * S], idf[:, :])
                m.then_inc(s_oq, 1)

            def out_rows(st, g, p, others, og):
                pe.wait_ge(s_on, at("on", st, g, GB))
                if others == CROSS:
                    pe.wait_ge(s_qr, at("qr", others, og, 1))
                elif others == LINEAR:
                    pe.wait_ge(s_phi, at("phi", others, og, 4))
                elif others is not None:
                    pe.wait_ge(s_kr, at("kr", others, og, 1))
                elif st == SELF:
                    pe.wait_ge(s_qr, at("qr", CROSS, 0, 1))
                elif st == LINEAR:
                    pe.wait_ge(s_xTe, at("xTe", MASKX, 1, 1))
                pe.wait_ge(s_xupd, at("xupd", st, g, 0))
                for b in range(GB):
                    m = pe.transpose(front[:, b * S:(b + 1) * S], O[:, p, b, :], idf[:, :])
                m.then_inc(s_oT, 1)

            def project(st, g, p, others, og):
                pe.wait_ge(s_oTe, at("oTe", st, g, 1))
                if others not in (None, CROSS):
                    pe.wait_ge(s_ve, at("ve", others, og, 1))
                w = {SELF: wT[:, WOUT, :], CROSS: wT[:, XWO, :], LINEAR: wT[:, LO, :], MASKX: wm[:, MO, :]}[st]
                for b in range(GB):
                    m = pe.matmul(front[:, b * D:(b + 1) * D], OdT[:, p, b * S:(b + 1) * S], w, start=True, stop=True)
                m.then_inc(s_y, 1)

            def turn_behind(st, g, t, first, flush):
                if st != LINEAR:
                    if t >= 2:
                        if not flush:
                            turn(st, g, t - 2)
                    elif not first:
                        turn(st, g - 1, t + UN - 2)

            def weigh_behind(st, g, p, t, first, flush):
                if t >= 3:
                    if not flush:
                        weigh(st, g, p, t - 3)
                elif not first:
                    weigh(st, g - 1, 1 - p, t + UN - 3)

            def slot(st, g, p, t, first, left, flush):
                now = upcoming(st, g, p, left, t) if not flush else []
                others, og, _ = target(st, g, p, left, 1) if not flush else (None, 0, 0)
                for ts, tg, tp, k in now:
                    if ts == LINEAR and t == 7:
                        front_part(ts, tg, tp, k, not first)
                if not flush and t + 1 < UN:
                    scores(st, g, p, t + 1)
                elif not flush and left >= 1:
                    scores(st, g + 1, 1 - p, 0)
                if t % 2 == 0:
                    weigh_behind(st, g, p, t, first, flush)
                    turn_behind(st, g, t, first, flush)
                else:
                    turn_behind(st, g, t, first, flush)
                    weigh_behind(st, g, p, t, first, flush)
                if t % 2 == 0:
                    if t >= 4 and not flush:
                        token_rows(st, g, (t - 4) // 2)
                    elif t < 4 and not first:
                        token_rows(st, g - 1, (t + UN - 4) // 2)
                for ts, tg, tp, k in now:
                    if not (ts == LINEAR and t == 7):
                        front_part(ts, tg, tp, k, not first)
                if t == 4 and not first:
                    out_rows(st, g - 1, 1 - p, others, og)
                if t == 6 and not first:
                    project(st, g - 1, 1 - p, others, og)

            def attention(st):
                if not follows_on(st):
                    if st > 0:
                        pe.wait_ge(s_xupd, at("xupd", st, 0, 0))
                    for k in range(6):
                        front_part(st, 0, 0, k, False)
                    for k in PARTS_AT[st][7][1]:
                        front_part(st, 1, 1, k, False)
                scores(st, 0, 0, 0)

                def body(g, p, first, left):
                    for t in range(UN):
                        slot(st, g, p, t, first, left, False)
                groups_ahead(pe, body)
                for t in range(7):
                    slot(st, NG, NG % 2, t, False, 0, True)

            def experts(st):
                n = CHUNKS[st]

                def routing(g, p, k):
                    if k == 0:
                        pe.wait_ge(s_combTe, at("combTe", st, g, 0))
                        transposed_x(st, g, p)
                    if k == 1:
                        pe.wait_ge(s_xTe, at("xTe", st, g, 1))
                        for b in range(GB):
                            m = pe.matmul(front[:, b * NE[st]:(b + 1) * NE[st]], xT[:, p, b * S:(b + 1) * S], gw[st][:, :], start=True, stop=True)
                        m.then_inc(s_lg, 1)
                    if k == 2:
                        pe.wait_ge(s_comb, at("comb", st, g, 1))
                        for b in range(GB):
                            m = pe.transpose(front[:, :].bitcast(BF16)[:, b * S:(b + 1) * S], combp[:, b, :], idb[:, :])
                        m.then_inc(s_combT, 1)

                def chunk(g, p, c):
                    pg, pc = before(st, g, c)
                    cols = slice(c * 128, (c + 1) * 128)
                    pe.wait_ge(s_silu, at("silu", st, pg, pc + 1))
                    pe.matmul(score[:, 0, (c % 2) * GT:(c % 2 + 1) * GT], wg1[:, cols], xT[:, p, :], start=True, stop=True).then_inc(s_gate, 1)
                    pe.wait_ge(s_gu, at("gu", st, pg, pc + 1))
                    pe.matmul(score[:, 1, (c % 2) * GT:(c % 2 + 1) * GT], wu1[:, cols], xT[:, p, :], start=True, stop=True).then_inc(s_up, 1)
                    if c < C1:
                        if c == 0:
                            pe.wait_ge(s_combTe, at("combTe", st, g, 1))
                        pe.wait_ge(s_h, at("h", st, g, c - 1))
                        pe.matmul(turned[:, (c % 2) * GT:(c % 2 + 1) * GT], sel[:, c, :], combT[:, p, :], start=True, stop=True).then_inc(s_cw, 1)

                def down(g, c):
                    if c == C1:
                        pe.wait_ge(s_gu, at("gu", st, g, c + 1))
                        rows = gu
                    else:
                        pe.wait_ge(s_h, at("h", st, g, c + 1))
                        rows = hid
                    if c == 0:
                        pe.wait_ge(s_xupd, at("xupd", st, g, 0))
                    for b in range(GB):
                        m = pe.matmul(back[:, b * D:(b + 1) * D], rows[:, c % 3, b * S:(b + 1) * S], wd1[:, c, :],
                                      start=(c == 0 and b == 0), stop=(c == n - 1), skip_group_check=True)
                    m.then_inc(s_down, 1)

                pe.wait_ge(s_w1, 16 * W1_LOADS)
                pe.wait_ge(s_tab, 16 * 3)
                pe.wait_ge(s_xupd, at("xupd", st, 0, 0))
                for k in range(3):
                    routing(0, 0, k)
                ROUTE_AT = {2: 0, 3: 1}

                def body(g, p, first, last):
                    for c in range(n):
                        chunk(g, p, c)
                        if c in ROUTE_AT and not last:
                            routing(g + 1, 1 - p, ROUTE_AT[c])
                        if c >= 2:
                            down(g, c - 2)
                        elif not first:
                            down(g - 1, n - 2 + c)
                    if not last:
                        routing(g + 1, 1 - p, 2)
                groups(pe, body)
                down(NG - 1, n - 2)
                down(NG - 1, n - 1)

            def route():
                st = ROUTE

                def logits(g, p):
                    pe.wait_ge(s_xTe, at("xTe", st, g, 1))
                    for b in range(GB):
                        m = pe.matmul(back[:, b * E2:(b + 1) * E2], xT[:, p, b * S:(b + 1) * S], gw[st][:, :], start=True, stop=True)
                    m.then_inc(s_lg, 1)

                def places(g, p):
                    pe.wait_ge(s_chosen, at("chosen", st, g, 1))
                    ch = chosen[:, p, :].rearrange("p (b e) -> p b e", b=GB)
                    for b in range(GB + 1):
                        if b < GB:
                            m = pe.matmul(score[:, 0, b * E2:(b + 1) * E2], earlier[:, 0, :], ch[:, b, :], start=True, stop=(b == 0))
                        for a in range(b):
                            m = pe.matmul(score[:, 0, b * E2:(b + 1) * E2], earlier[:, 1, :], ch[:, a, :], start=(b == GB and a == 0), stop=(a == b - 1))
                    m.then_inc(s_place, 1)

                pe.wait_ge(s_xupd, at("xupd", st, 0, 0))
                transposed_x(st, 0, 0)

                def body(g, p, first, last):
                    logits(g, p)
                    places(g, p)
                    if not last:
                        transposed_x(st, g + 1, 1 - p)
                groups(pe, body)

            def routed_experts():
                def turn_rows(t, q):
                    pe.wait_ge(s_rows[q], landed(t, q) + 16)
                    if not isinstance(t, int) or t >= 1:
                        pe.wait_ge(s_rTe, t)
                    pe.transpose(front[:, 0:S], t_rows[:, q, 0:D], idf[:, :]).then_inc(s_rT, 1)

                def turn_hidden(t, p):
                    pe.wait_ge(s_thid, t + 1)
                    if not isinstance(t, int) or t >= 2:
                        pe.wait_ge(s_hTe, t - 1)
                    for c in range(M2 // 128):
                        m = pe.transpose(turned[:, p * M2 + c * 128:p * M2 + (c + 1) * 128], t_hid[:, p, c * 128:(c + 1) * 128], idf[:, :])
                    m.then_inc(s_hT, 1)

                def down(t, p, col):
                    pe.wait_ge(s_hTe, t + 1)
                    if not isinstance(t, int) or t >= 1:
                        pe.wait_ge(s_yw, 2 * t)
                    for c in range(M2 // 128):
                        m = pe.matmul(back[:, 0:D], t_hT[:, p, c * 128:(c + 1) * 128], wd2[:, bass.ds(col + c * D, D)],
                                      start=(c == 0), stop=(c == M2 // 128 - 1))
                    m.then_inc(s_ty, 1)

                def column(t):
                    return pe.value_load(table[0:1, bass.ds(TILES + t, 1)], min_val=0, max_val=(E2 - 1) * M2)

                pe.wait_ge(s_table, TABLE_STEPS)
                pe.wait_ge(s_w2, 16 * 3)
                turn_rows(0, 0)

                def body(t, q, first, last):
                    p = q % 2
                    col = column(t)
                    pe.wait_ge(s_rTe, t + 1)
                    if not isinstance(t, int) or t >= 2:
                        pe.wait_ge(s_tsilu, t - 1)
                    pe.matmul(score[:, 0, p * M2:(p + 1) * M2], xT[:, p, 0:S], wg2[:, bass.ds(col, M2)], start=True, stop=True).then_inc(s_tg, 1)
                    if not first:
                        turn_hidden(t - 1, 1 - p)
                    if not last:
                        turn_rows(t + 1, (q + 1) % QT)
                    if not isinstance(t, int) or t >= 2:
                        pe.wait_ge(s_thid, t - 1)
                    pe.matmul(score[:, 1, p * M2:(p + 1) * M2], xT[:, p, 0:S], wu2[:, bass.ds(col, M2)], start=True, stop=True).then_inc(s_tu, 1)
                    if not first:
                        down(t - 1, 1 - p, column(t - 1))
                tiles(pe, body)
                turn_hidden(TILES - 1, (TILES - 1) % 2)
                down(TILES - 1, (TILES - 1) % 2, column(TILES - 1))

            attention(SELF)
            attention(CROSS)
            experts(MOE)
            attention(LINEAR)
            attention(MASKX)
            route()
            routed_experts()

        @block.vector
        def _(dve):
            dve.memset(heavy[:, 0:2 * WE], 0.0).then_inc(s_zero, 1)
            dve.memset(back[:, :], 0.0).then_inc(s_zero, 1)
            dve.wait_ge(s_x0, 16)
            dve.sem_inc(s_xupd, 1)

            def rows(g):
                return X[:, bass.ds(g * GB, GB), :]

            def statistics(st, g, p):
                if st > SELF:
                    dve.wait_ge(s_xupd, at("xupd", st - 1, g, 1))
                xg = rows(g)
                dve.wait_ge(s_aggr, at("aggr", st, g, 0))
                for b in range(GB):
                    dve.bn_stats(stats[:, b, :], xg[:, b, :]).then_inc(s_stat, 1)
                dve.wait_ge(s_stat, at("stat", st, g, GB))
                settle(dve, "dve")
                for b in range(GB):
                    dve.bn_aggr(mv[:, p, b, :], stats[:, b, :]).then_inc(s_aggr, 1)
                dve.wait_ge(s_aggr, at("aggr", st, g, GB))
                dve.wait_ge(s_rstd, at("rstd", st, g, 0))
                dve.tensor_scalar(veps[:, :], mv[:, p, :, 1], LN_EPS, None, ALU.add).then_inc(s_veps, 1)

            def normalise(st, g, p):
                dve.wait_ge(s_rstd, at("rstd", st, g, 1))
                xg = rows(g)
                for b in range(GB):
                    dve.tensor_scalar(xn[:, p, b, :], xg[:, b, :], mv[:, p, b, 0:1], rstd[:, p, b:b + 1], ALU.subtract, ALU.mult).then_inc(s_xn, 1)

            def query_rest(st, g, rows):
                dve.wait_ge(s_qp, at("qp", st, g, 0))
                dve.wait_ge(s_qe, at("qe", st, g, 1))
                dve.tensor_tensor(rest[:, QRY, :], rows, parts[:, QRY, 0, :], ALU.subtract).then_inc(s_qr, 1)

            def key_rest(st, g, rows):
                dve.wait_ge(s_kp, at("kp", st, g, 0))
                dve.wait_ge(s_ke, at("ke", st, g, 1))
                dve.tensor_tensor(rest[:, KEY, :], rows, parts[:, KEY, 0, :], ALU.subtract).then_inc(s_kr, 1)

            def front_part(st, g, p, k):
                if k == 0 and st == CROSS:
                    key_rest(st, g, front[:, :])
                if k == 1 and st == CROSS:
                    query_rest(st, g, front[:, :])
                if k == 2 and st in (SELF, MASKX):
                    query_rest(st, g, front[:, :])
                if k == 3 and st in (SELF, MASKX):
                    key_rest(st, g, front[:, :])
                if k == 2 and st == LINEAR:
                    dve.wait_ge(s_phi, at("phi", st, g, 2))
                    dve.scalar_tensor_tensor(src[:, p, :], phi_e[:, :], 1.0, phi_r[:, :], ALU.min, ALU.add).then_inc(s_qf, 1)
                if k == 3 and st == LINEAR:
                    dve.wait_ge(s_phi, at("phi", st, g, 4))
                    dve.scalar_tensor_tensor(dense[:, p, :], phi_e[:, :], 1.0, phi_r[:, :], ALU.min, ALU.add).then_inc(s_kf, 1)
                    query_rest(st, g, src[:, p, :])
                if k == 4 and st == LINEAR:
                    key_rest(st, g, dense[:, p, :])
                    dve.wait_ge(s_kp, at("kp", st, g, 1))
                    dve.tensor_tensor(parts[:, KEY, 2, :], rest[:, KEY, :], parts[:, KEY, 1, :], ALU.subtract).then_inc(s_kp, 1)

            def scores(st, g, t, between):
                dve.wait_ge(s_s, at("s", st, g, t + 1))
                sv = score[:, t % 2, :].rearrange("p (h k) -> p h k", h=UH)
                tv = T[:, t % 4, :].rearrange("p (h k) -> p h k", h=UH)
                nm = negm[:, t % 4, :]
                if st == LINEAR:
                    dve.wait_ge(s_pv, at("pv", st, g, t - 3))
                    dve.tensor_tensor(tv, sv, cm[:, :].unsqueeze(1).broadcast_to([128, UH, S]), ALU.mult).then_inc(s_t, 1)
                    between()
                elif st == MASKX:
                    dve.scalar_tensor_tensor(tv, sv, SCALE, mneg[:, :].unsqueeze(1).broadcast_to([128, UH, S]), ALU.mult, ALU.add).then_inc(s_sm, 1)
                    between()
                    dve.wait_ge(s_sm, at("sm", st, g, t + 1))
                    dve.wait_ge(s_t, at("t", st, g, t - 3))
                    dve.wait_ge(s_eb, at("eb", st, g, t - 3))
                    dve.tensor_reduce(nm, tv, AX.X, ALU.max, negate=True).then_inc(s_negm, 1)
                else:
                    dve.tensor_reduce(nm, sv, AX.X, ALU.max, negate=True).then_inc(s_negm, 1)
                    between()
                    dve.wait_ge(s_negm, at("negm", st, g, t + 1))
                    dve.tensor_tensor(tv, sv, nm.unsqueeze(2).broadcast_to([128, UH, S]), ALU.add).then_inc(s_t, 1)

            def divide(st, g, p, b):
                dve.wait_ge(s_oq, at("oq", st, g, b + 1))
                ov = back[:, :].rearrange("p (h r) -> p h r", h=H)
                d = ov[:, :, HD]
                if st == LINEAR:
                    dve.tensor_scalar(den[:, :], d, DEN_EPS, None, ALU.add).then_inc(s_den, 1)
                    dve.wait_ge(s_den, at("den", st, g, b + 1))
                    d = den[:, :]
                dve.reciprocal(rden[:, :], d).then_inc(s_rden, 1)
                dve.wait_ge(s_rden, at("rden", st, g, b + 1))
                dve.tensor_tensor(O[:, p, b, :].rearrange("p (h d) -> p h d", d=HD), ov[:, :, 0:HD],
                                  rden[:, :].unsqueeze(2).broadcast_to([128, H, HD]), ALU.mult).then_inc(s_on, 1)

            def residual(st, g):
                xg = rows(g)
                if st == MASKX:
                    dve.tensor_tensor(xg, xg, bo[:, :].unsqueeze(1).broadcast_to([128, GB, D]), ALU.add).then_inc(s_bias, 1)
                    dve.wait_ge(s_bias, at("bias", st, g, 1))
                dve.wait_ge(s_y, at("y", st, g, 1))
                dve.tensor_tensor(xg, front[:, :].rearrange("p (b d) -> p b d", b=GB), xg, ALU.add).then_inc(s_xupd, 1)

            def slot(st, g, p, t, first, left, flush):
                def between():
                    if t % 2 == 1:
                        if t >= 5 and not flush:
                            divide(st, g, p, (t - 5) // 2)
                        elif t < 5 and not first:
                            divide(st, g - 1, 1 - p, (t + UN - 5) // 2)
                    if t == 7 and not first:
                        residual(st, g - 1)
                    if s1 == CROSS and t == 0:
                        normalise(s1, g1, p1)
                    if s2 in TWO_AHEAD and t == 6:
                        statistics(s2, g2, p2)
                    if s2 in TWO_AHEAD and t == 7:
                        normalise(s2, g2, p2)
                        if s2 == LINEAR:
                            front_part(s2, g2, p2, 2)
                    if s1 is not None and t > 0:
                        for k in PARTS_AT[s1].get(t - 1, (1, ()))[1]:
                            front_part(s1, g1, p1, k)
                s1, g1, p1 = target(st, g, p, left, 1) if not flush else (None, 0, 0)
                s2, g2, p2 = target(st, g, p, left, 2) if not flush else (None, 0, 0)
                if s1 == CROSS and t == 0:
                    statistics(s1, g1, p1)
                if flush:
                    between()
                else:
                    scores(st, g, t, between)

            def attention(st):
                if st == MASKX:
                    dve.tensor_scalar(mneg[:, :], mneg[:, :], -1.0, 1.0, ALU.mult, ALU.add).then_inc(s_mneg, 1)
                    dve.wait_ge(s_mneg, 1)
                    dve.tensor_scalar(mneg[:, :], mneg[:, :], MASKED, None, ALU.mult).then_inc(s_mneg, 1)
                    dve.wait_ge(s_mneg, 2)
                if not follows_on(st):
                    statistics(st, 0, 0)
                    normalise(st, 0, 0)
                    for k in range(5):
                        front_part(st, 0, 0, k)
                    if st == SELF:
                        dve.wait_ge(s_x1, 16)
                    statistics(st, 1, 1)
                    normalise(st, 1, 1)
                    if st == LINEAR:
                        front_part(st, 1, 1, 2)

                def body(g, p, first, left):
                    for t in range(UN):
                        slot(st, g, p, t, first, left, False)
                groups_ahead(dve, body)
                for t in range(8):
                    slot(st, NG, NG % 2, t, False, 0, True)

            def ranks(st, g, k, val, m, out_i, pieces=(0, 1)):
                keep = {4: 2, 16: 4, 8: 2}[m]
                v3 = val.rearrange("p (b e) -> p b e", b=GB)

                def step(g, k, ins):
                    ins.then_inc(s_route, 1)
                    dve.wait_ge(s_route, at("route", st, g, k))

                shape = [128, GB, m, m]
                a = wide[:, 0:GB * m * m]
                bq = wide[:, 1024:1024 + GB * m * m]
                comp = v3.unsqueeze(2).broadcast_to(shape)
                cand = v3.unsqueeze(3).broadcast_to(shape)
                av = a.rearrange("p (b j i) -> p b j i", b=GB, j=m)
                bv = bq.rearrange("p (b j i) -> p b j i", b=GB, j=m)
                left = tr[:, 0:m, 0:m].unsqueeze(1).broadcast_to(shape)
                if 0 in pieces:
                    dve.tensor_tensor(av, comp, cand, ALU.is_equal).then_inc(s_route, 1)
                    dve.tensor_tensor(bv, comp, cand, ALU.is_gt).then_inc(s_route, 1)
                if 1 in pieces:
                    if m == 16:
                        dve.wait_ge(s_before, at("before", st, g, 2))
                    else:
                        dve.wait_ge(s_route, at("route", st, g, k + 2))
                        step(g, k + 3, dve.tensor_tensor(av, av, left, ALU.mult))
                        step(g, k + 4, dve.tensor_tensor(a, a, bq, ALU.add))
                    k -= 2 if m == 16 else 0
                    step(g, k + 5, dve.tensor_reduce(lr[:, out_i, 0:GB * m], a.rearrange("p (c i) -> p c i", i=m), AX.X, ALU.add))
                    step(g, k + 6, dve.tensor_scalar(lr[:, out_i, 0:GB * m], lr[:, out_i, 0:GB * m], float(keep), None, ALU.is_lt))

            def experts(st):
                n, ne = CHUNKS[st], NE[st]
                w = GB * ne

                def step(g, k, ins):
                    ins.then_inc(s_route, 1)
                    dve.wait_ge(s_route, at("route", st, g, k))

                def small(i, width=w):
                    return lr[:, i, 0:width]

                def by_row(a, m=ne):
                    return a.rearrange("p (b e) -> p b e", b=GB)

                def parts(g, k, c):
                    c3 = by_row(c)
                    r = by_row(small(12))
                    step(g, k + 1, dve.tensor_copy(combp[:, :, 0:ne], c3))
                    step(g, k + 2, dve.tensor_tensor(r, c3, combp[:, :, 0:ne], ALU.subtract))
                    step(g, k + 3, dve.tensor_copy(combp[:, :, 16:16 + ne], r))
                    step(g, k + 4, dve.tensor_tensor(r, r, combp[:, :, 16:16 + ne], ALU.subtract))
                    dve.tensor_copy(combp[:, :, 32:32 + ne], r).then_inc(s_comb, 1)

                def route_moe(g, k):
                    if k == 0:
                        dve.wait_ge(s_rexp, at("rexp", st, g, 1))
                        step(g, 1, dve.tensor_scalar(small(1), small(0), 1.0, None, ALU.add))
                        step(g, 2, dve.reciprocal(small(2), small(1)))
                        step(g, 3, dve.tensor_tensor(by_row(small(3)), by_row(small(2)), bias_r[:, :].unsqueeze(1).broadcast_to([128, GB, E1]), ALU.add))
                        a = small(3).rearrange("p (c i) -> p c i", i=4)
                        pr = wide[:, 0:6 * 16].rearrange("p (c i) -> p c i", i=6)
                        dve.tensor_tensor(pr[:, :, 0:3], a[:, :, 0:3], a[:, :, 1:4], ALU.add).then_inc(s_route, 1)
                        dve.tensor_tensor(pr[:, :, 3:5], a[:, :, 0:2], a[:, :, 2:4], ALU.add).then_inc(s_route, 1)
                        step(g, 6, dve.tensor_tensor(pr[:, :, 5:6], a[:, :, 0:1], a[:, :, 3:4], ALU.add))
                        step(g, 7, dve.tensor_reduce(lr[:, 4, 0:16], pr, AX.X, ALU.max))
                    if k == 1:
                        ranks(st, g, 7, lr[:, 4, 0:16], 4, 5)
                        step(g, 14, dve.tensor_tensor(small(6).rearrange("p (c i) -> p c i", i=4), small(3).rearrange("p (c i) -> p c i", i=4),
                                                      lr[:, 5, 0:16].unsqueeze(2).broadcast_to([128, 16, 4]), ALU.mult))
                    if k == 2:
                        ranks(st, g, 14, small(6), 16, 7, (0,))
                    if k == 3:
                        ranks(st, g, 14, small(6), 16, 7, (1,))
                    if k == 4:
                        step(g, 19, dve.tensor_tensor(small(8), small(6), small(7), ALU.mult))
                        weights(g, 19, 2.5, 1e-20)

                def weights(g, k, scale, eps):
                    dve.tensor_reduce(lr[:, 9, 0:GB], by_row(small(8)), AX.X, ALU.add).then_inc(s_wsum, 1)
                    dve.wait_ge(s_wsum, at("wsum", st, g, 1))
                    dve.tensor_scalar(lr[:, 10, 0:GB], lr[:, 9, 0:GB], eps, None, ALU.add).then_inc(s_wsum, 1)
                    dve.wait_ge(s_wsum, at("wsum", st, g, 2))
                    dve.reciprocal(lr[:, 11, 0:GB], lr[:, 10, 0:GB]).then_inc(s_wsum, 1)
                    dve.wait_ge(s_wsum, at("wsum", st, g, 3))
                    dve.tensor_tensor(by_row(small(13)), by_row(small(8)), lr[:, 11, 0:GB].unsqueeze(2).broadcast_to([128, GB, ne]), ALU.mult).then_inc(s_wsum, 1)
                    dve.wait_ge(s_wsum, at("wsum", st, g, 4))
                    dve.tensor_scalar(small(8), small(13), scale, None, ALU.mult).then_inc(s_wsum, 1)
                    dve.wait_ge(s_wsum, at("wsum", st, g, 5))
                    parts(g, k, small(8))

                def routing(g, p, k):
                    if k == 0:
                        statistics(st, g, p)
                    elif k == 1:
                        normalise(st, g, p)
                    else:
                        route_moe(g, k - 2)

                dve.wait_ge(s_w1, 16 * W1_LOADS)
                dve.wait_ge(s_ones, 3)
                for k in range(7):
                    routing(0, 0, k)
                ROUTE_AT = {0: (0,), 1: (1,), 3: (2, 3), 4: (4,), 6: (5,), 7: (6,)}

                def chunk(g, c):
                    b, r = c % 2, c % 3
                    dve.wait_ge(s_up, at("up", st, g, c + 1))
                    dve.wait_ge(s_silu, at("silu", st, g, c + 1))
                    dve.tensor_tensor(gu[:, r, :], score[:, 1, b * GT:(b + 1) * GT], sg[:, r, :], ALU.mult).then_inc(s_gu, 1)
                    if c < C1:
                        dve.wait_ge(s_cw, at("cw", st, g, c + 1))
                        dve.wait_ge(s_gu, at("gu", st, g, c + 1))
                        dve.tensor_tensor(hid[:, r, :], turned[:, b * GT:(b + 1) * GT], gu[:, r, :], ALU.mult).then_inc(s_h, 1)

                def body(g, p, first, last):
                    for c in range(n):
                        chunk(g, c)
                        if not last:
                            for k in ROUTE_AT.get(c, ()):
                                routing(g + 1, 1 - p, k)
                        if c == 1 and not first:
                            added(g - 1)

                def added(g):
                    xg = rows(g)
                    dve.wait_ge(s_down, at("down", st, g, n))
                    dve.tensor_tensor(xg, back[:, :].rearrange("p (b d) -> p b d", b=GB), xg, ALU.add).then_inc(s_xupd, 1)
                groups(dve, body)
                added(NG - 1)

            def route():
                st = ROUTE
                w = GB * E2
                dve.wait_ge(s_w1, 16 * W1_LOADS)
                statistics(st, 0, 0)
                normalise(st, 0, 0)

                def step(g, k, ins):
                    ins.then_inc(s_route, 1)
                    dve.wait_ge(s_route, at("route", st, g, k))

                def small(i):
                    return lr[:, i, 0:w]

                def by_row(a):
                    return a.rearrange("p (b e) -> p b e", b=GB)

                def body(g, p, first, last):
                    if not last:
                        statistics(st, g + 1, 1 - p)
                    dve.wait_ge(s_lg, at("lg", st, g, 1))
                    dve.tensor_copy(small(0), back[:, 0:w]).then_inc(s_lge, 1)
                    dve.wait_ge(s_lge, at("lge", st, g, 1))
                    step(g, 1, dve.tensor_reduce(lr[:, 1, 0:GB], by_row(small(0)), AX.X, ALU.max))
                    step(g, 2, dve.tensor_tensor(by_row(small(2)), by_row(small(0)), lr[:, 1, 0:GB].unsqueeze(2).broadcast_to([128, GB, E2]), ALU.subtract))
                    ranks(st, g, 2, small(0), E2, 7)
                    dve.tensor_copy(chosen[:, p, :], small(7)).then_inc(s_chosen, 1)
                    if not last:
                        normalise(st, g + 1, 1 - p)
                    dve.wait_ge(s_rexp, at("rexp", st, g, 1))
                    step(g, 9, dve.tensor_tensor(small(8), small(3), small(7), ALU.mult))
                    dve.tensor_reduce(lr[:, 9, 0:GB], by_row(small(8)), AX.X, ALU.add).then_inc(s_wsum, 1)
                    dve.wait_ge(s_wsum, at("wsum", st, g, 1))
                    dve.reciprocal(lr[:, 10, 0:GB], lr[:, 9, 0:GB]).then_inc(s_wsum, 1)
                    dve.wait_ge(s_wsum, at("wsum", st, g, 2))
                    dve.tensor_tensor(by_row(small(13)), by_row(small(8)), lr[:, 10, 0:GB].unsqueeze(2).broadcast_to([128, GB, E2]), ALU.mult).then_inc(s_wsum, 1)
                    dve.wait_ge(s_wsum, at("wsum", st, g, 3))
                    dve.wait_ge(s_place, at("place", st, g, 1))
                    step(g, 10, dve.tensor_tensor(by_row(small(4)), by_row(score[:, 0, 0:w]), base[:, :].unsqueeze(1).broadcast_to([128, GB, E2]), ALU.add))
                    step(g, 11, dve.tensor_tensor(base[:, :], score[:, 0, w:w + E2], base[:, :], ALU.add))
                    step(g, 12, dve.tensor_tensor(small(5), small(4), small(7), ALU.mult))
                    step(g, 13, dve.tensor_reduce(indexf[:, :, 1], by_row(small(5)), AX.X, ALU.max))
                    step(g, 14, dve.scalar_tensor_tensor(small(6), small(7), -FAR, small(4), ALU.mult, ALU.add))
                    step(g, 15, dve.tensor_reduce(lr[:, 11, 0:GB], by_row(small(6)), AX.X, ALU.min))
                    step(g, 16, dve.tensor_scalar(indexf[:, :, 0], lr[:, 11, 0:GB], FAR, None, ALU.add))
                    both = wide[:, 0:KEEP2 * w].rearrange("p (b c e) -> p b c e", b=GB, c=KEEP2)
                    shape = [128, GB, KEEP2, E2]
                    step(g, 17, dve.tensor_tensor(both, by_row(small(5)).unsqueeze(2).broadcast_to(shape), indexf[:, :, :].unsqueeze(3).broadcast_to(shape), ALU.is_equal))
                    step(g, 18, dve.tensor_tensor(both, both, by_row(small(13)).unsqueeze(2).broadcast_to(shape), ALU.mult))
                    if not isinstance(g, int) or g >= 2:
                        dve.wait_ge(s_sent[p], sent_before(g, p))
                    dve.tensor_reduce(pay[:, p, :, :, WEIGHT], both, AX.X, ALU.add).then_inc(s_payw, 1)
                    dve.tensor_copy(index[:, p, :, :], indexf[:, :, :]).then_inc(s_index, 1)
                groups(dve, body)

            def tabulate():
                def step(k, ins):
                    ins.then_inc(s_table, 1)
                    dve.wait_ge(s_table, k)

                ends = base[0:1, :]
                dve.tensor_copy(table[:, 2 * TILES:], ends).then_inc(s_ends, 1)
                big = wide[0:1, 0:TILES * E2]
                tokens, full, cover, end = (tl[:, i, 0:E2] for i in range(4))
                expert, skipped, row, col = (tl[:, i, :] for i in range(4, 8))
                step(1, dve.tensor_tensor(tokens, ends, start_r[0:1, :], ALU.subtract))
                over = wide[0:1, 0:E2 * 32].rearrange("p (e k) -> p e k", e=E2)
                step(2, dve.tensor_tensor(over, tokens.unsqueeze(2).broadcast_to([1, E2, 32]), step_r[0:1, 0:32].unsqueeze(1).broadcast_to([1, E2, 32]), ALU.is_gt))
                step(3, dve.tensor_reduce(full, over, AX.X, ALU.add))
                square = wide[0:1, 0:E2 * E2].rearrange("p (e k) -> p e k", e=E2)
                step(4, dve.tensor_tensor(square, tr[0:1, 0:E2, 0:E2], full.unsqueeze(1).broadcast_to([1, E2, E2]), ALU.mult))
                step(5, dve.tensor_reduce(cover, square, AX.X, ALU.add))
                step(6, dve.tensor_tensor(end, cover, full, ALU.add))
                step(7, dve.tensor_scalar(end, end, float(S), None, ALU.mult))
                past = big.rearrange("p (t e) -> p t e", e=E2)
                shape = [1, TILES, E2]
                nth = step_r[0:1, 32:32 + TILES]
                step(8, dve.tensor_tensor(past, nth.unsqueeze(2).broadcast_to(shape), end.unsqueeze(1).broadcast_to(shape), ALU.is_ge))
                step(9, dve.tensor_reduce(expert, past, AX.X, ALU.add))
                step(10, dve.tensor_tensor(past, past, full.unsqueeze(1).broadcast_to(shape), ALU.mult))
                step(11, dve.tensor_reduce(skipped, past, AX.X, ALU.add))
                step(12, dve.scalar_tensor_tensor(row, skipped, -float(S), nth, ALU.mult, ALU.add))
                step(13, dve.scalar_tensor_tensor(row, expert, float(REGION), row, ALU.mult, ALU.add))
                step(14, dve.tensor_scalar(col, expert, float(E2 - 1), float(M2), ALU.min, ALU.mult))
                dve.tensor_copy(table[:, 0:TILES], row).then_inc(s_table, 1)
                dve.tensor_copy(table[:, TILES:2 * TILES], col).then_inc(s_table, 1)

            def routed_experts():
                def copy_rows(t, p):
                    dve.wait_ge(s_rT, t + 1)
                    dve.tensor_copy(xT[:, p, 0:S], front[:, 0:S]).then_inc(s_rTe, 1)

                def weighted(t, q):
                    dve.wait_ge(s_ty, t + 1)
                    if not isinstance(t, int) or t >= QT:
                        dve.wait_ge(s_ysent[q], landed(t, q))
                    dve.tensor_scalar(t_y[:, q, :], back[:, 0:D], t_rows[:, q, WEIGHT:WEIGHT + 1], None, ALU.mult).then_inc(s_yw, 1)
                    dve.tensor_copy(yindex[:, q:q + 1], t_rows[:, q, DEST:DEST + 1]).then_inc(s_yw, 1)

                copy_rows(0, 0)

                def body(t, q, first, last):
                    p = q % 2
                    if not last:
                        if not isinstance(t, int) or t >= 1:
                            dve.wait_ge(s_tu, t)
                        copy_rows(t + 1, 1 - p)
                    dve.wait_ge(s_tsilu, t + 1)
                    dve.wait_ge(s_tu, t + 1)
                    if not isinstance(t, int) or t >= 2:
                        dve.wait_ge(s_hT, t - 1)
                    dve.tensor_tensor(t_hid[:, p, :], score[:, 1, p * M2:(p + 1) * M2], t_sg[:, p, :], ALU.mult).then_inc(s_thid, 1)
                    if not first:
                        weighted(t - 1, (q - 1) % QT)
                tiles(dve, body)
                weighted(TILES - 1, (TILES - 1) % QT)

            def add():
                for n in range(SUMS):
                    xs = X[:, n * SB:(n + 1) * SB, :]
                    dve.wait_ge(s_back[n], 16 * KEEP2)
                    dve.tensor_tensor(xs, y_both[:, 0, n * SB:(n + 1) * SB, :], xs, ALU.add).then_inc(s_half, 1)
                    dve.wait_ge(s_half, n + 1)
                    dve.tensor_tensor(xs, y_both[:, 1, n * SB:(n + 1) * SB, :], xs, ALU.add).then_inc(s_sum, 1)

            attention(SELF)
            attention(CROSS)
            experts(MOE)
            attention(LINEAR)
            attention(MASKX)
            route()
            tabulate()
            routed_experts()
            add()


_INS = ["x", "ctx_1024", "mask_1x1xSxS2_fk0", "L0_attn_w_qkv", "L0_attn_w_out", "L0_xattn_Wo",
        "L0_ffn_gate_kernel", "L0_ffn_gate_bias", "L0_ffn_w_gate", "L0_ffn_w_up", "L0_ffn_w_down",
        "L0_ffn_sw_gate", "L0_ffn_sw_up", "L0_ffn_sw_down", "L1_attn_Wq", "L1_attn_Wk",
        "L1_attn_Wv", "L1_attn_Wo", "L1_xattn_Wq", "L1_xattn_Wk", "L1_xattn_Wv", "L1_xattn_Wo",
        "L1_xattn_bo", "L1_ffn_gate", "L1_ffn_experts_w1", "L1_ffn_experts_w2", "L1_ffn_experts_w3"]


def constants():
    k = np.arange(128)
    col = np.arange(128)
    sel1 = np.stack([(k[:, None] < 48) & (k[:, None] % 16 == 2 * c + (col[None, :] >= M1)) for c in range(C1)], 1)
    padding = np.zeros((2 * E2 * S, ROW), np.float32)
    padding[:, DEST] = KEEP2 * TOKENS + np.arange(2 * E2 * S)
    dests = k[:, None, None] + S * np.arange(B)[None, :, None] + TOKENS * np.arange(KEEP2)[None, None, :]
    return {
        "ident": np.eye(128, dtype=np.float32),
        "causal": (k[:, None] <= k[None, :]).astype(np.float32),
        "tri": (np.arange(16)[None, :] < np.arange(16)[:, None]).astype(np.float32),
        "sel1": sel1.astype(np.float32),
        "before": np.stack([k[:, None] < col[None, :], np.ones((128, 128), bool)], 1).astype(np.float32),
        "starts": (REGION * np.arange(E2)).astype(np.float32),
        "steps": (S * np.concatenate([np.arange(32), np.arange(TILES)])).astype(np.float32),
        "dests": dests.astype(np.float32),
        "padding": padding,
    }


def kernel(**inputs):
    import concourse.bacc as _bacc
    from concourse.bass_utils import run_bass_kernel_spmd as _run

    nc = _bacc.Bacc("TRN2", target_bir_lowering=False, num_devices=1)
    arrays, args = {}, []
    for name, a in [(n, inputs[n]) for n in _INS] + list(constants().items()):
        a = np.ascontiguousarray(a)
        arrays[f"in_{name}"] = a
        args.append(nc.dram_tensor(f"in_{name}", a.shape, mybir.dt.from_np(a.dtype), kind="ExternalInput").ap())
    args.append(nc.dram_tensor("out_0", (B, S, D), F32, kind="ExternalOutput").ap())
    decoder(nc, *args)
    r = _run(nc, [arrays], core_ids=[0])
    return r.results[0]["out_0"]
```
